# Optimizing a Trainium2 kernel written in Bass

```python
import numpy as np
import jax
import jax.numpy as jnp

def _softmax(x, axis=-1):
    return jax.nn.softmax(x, axis=axis)

def _gelu(x):
    return jax.nn.gelu(x, approximate=True)

def _silu(x):
    return jax.nn.silu(x)

def _sigmoid(x):
    return jax.nn.sigmoid(x)

def _layernorm(x, axis=-1, eps=1e-05):
    m = jnp.mean(x, axis=axis, keepdims=True)
    v = jnp.var(x, axis=axis, keepdims=True)
    return (x - m) / jnp.sqrt(v + eps)

def _scatter_add(tgt, idx, src, axis=0):
    return tgt.at[idx].add(src)

def _segment_sum(src, seg, n):
    return jax.ops.segment_sum(src, seg, n)
kernel_name = 'mk_decoder_postln_d2_seqx_r4_57658c'

def setup_inputs(seed: int=0):
    np.random.seed(seed)
    _w = jnp.asarray

    def _rec_inputs():
        import jax
        import jax.numpy as jnp
        _rk = jax.random.key(seed)
        x = 7.22e-05 + 1 * jax.random.normal(jax.random.fold_in(_rk, 1), (8, 256, 256), jnp.float32)
        _lenS = 256 - jax.random.randint(jax.random.fold_in(_rk, 7), (8,), 0, max(1, 256 // 4) + 1, jnp.int32)
        _lenS2 = 77 - jax.random.randint(jax.random.fold_in(_rk, 8), (8,), 0, max(1, 77 // 4) + 1, jnp.int32)
        _ctx_768P = jax.random.normal(jax.random.fold_in(_rk, 11), (8, 16, 192), jnp.float32)
        _ctx_768c = jax.random.dirichlet(jax.random.fold_in(_rk, 511), 0.3 * jnp.ones((16,), jnp.float32), (8, 77))
        _ctx_768t = jnp.einsum('bsk,bkd->bsd', _ctx_768c, _ctx_768P)
        _ctx_768t = _ctx_768t * jax.lax.rsqrt(jnp.mean(jnp.square(_ctx_768t)) + 1e-12) * 0.953939
        ctx_768 = -0.000191848 + 0.999787 * (_ctx_768t + 0.3 * jax.random.normal(jax.random.fold_in(_rk, 611), (8, 77, 192), jnp.float32))
        return (x, ctx_768)
    x, ctx_768 = _rec_inputs()

    def _L0_attn_setup():
        import jax, jax.numpy as jnp
        import numpy as np
        H = 16
        BUCKETS = 64
        MAX_REL = 128

        def _log_bucket(rel, bucket_size, max_position):
            mid = bucket_size // 2
            sign = jnp.sign(rel).astype(jnp.float32)
            abs_pos = jnp.where((rel < mid) & (rel > -mid), mid - 1, jnp.abs(rel)).astype(jnp.float32)
            log_pos = jnp.ceil(jnp.log(abs_pos / mid) / np.log((max_position - 1) / mid) * (mid - 1)) + mid
            bucket = jnp.where(abs_pos <= mid, rel.astype(jnp.float32), log_pos * sign)
            return bucket.astype(jnp.int32)

        def _rel_pos(seq_len):
            ids = jnp.arange(seq_len)
            rel = ids[:, None] - ids[None, :]
            return _log_bucket(rel, BUCKETS, MAX_REL)
        key = jax.random.key(seed)
        ks = jax.random.split(key, 16)
        B, S, D = (4, 256, 256)
        K2 = 2 * BUCKETS
        s = 0.02

        def lin(k, din, dout):
            return jax.random.normal(k, (din, dout), jnp.float32) * s
        return {'hidden_states': jax.random.normal(ks[0], (B, S, D), jnp.float32), 'Wq': lin(ks[1], D, D), 'bq': jnp.zeros((D,), jnp.float32), 'Wk': lin(ks[2], D, D), 'bk': jnp.zeros((D,), jnp.float32), 'Wv': lin(ks[3], D, D), 'bv': jnp.zeros((D,), jnp.float32), 'Wo': lin(ks[4], D, D), 'bo': jnp.zeros((D,), jnp.float32), 'rel_emb': jax.random.normal(ks[5], (K2, D), jnp.float32) * s, 'ln_g': jnp.ones((D,), jnp.float32), 'ln_b': jnp.zeros((D,), jnp.float32), 'Wpk': lin(ks[6], D, D), 'bpk': jnp.zeros((D,), jnp.float32), 'Wpq': lin(ks[7], D, D), 'bpq': jnp.zeros((D,), jnp.float32)}
    _L0_attn_all = _L0_attn_setup()
    _L0_attn_in = {k: v for k, v in _L0_attn_all.items() if k in ('Wq', 'bq', 'Wk', 'bk', 'Wv', 'bv', 'Wo', 'bo', 'rel_emb', 'ln_g', 'ln_b', 'Wpk', 'bpk', 'Wpq', 'bpq')}
    del _L0_attn_all

    def _L0_xattn_setup():
        import jax, jax.numpy as jnp
        import numpy as np
        NUM_HEADS = 16
        CLAMP = 10000.0
        key = jax.random.key(seed)
        ks = jax.random.split(key, 8)
        B, Nq, Nkv, Cq, Ckv = (4, 512, 512, 256, 192)
        s_q = 1.0 / np.sqrt(Cq)
        s_kv = 1.0 / np.sqrt(Ckv)
        return {'query': jax.random.normal(ks[0], (B, Nq, Cq), jnp.float32), 'key_value': jax.random.normal(ks[1], (B, Nkv, Ckv), jnp.float32), 'Wq': jax.random.normal(ks[2], (Cq, Cq), jnp.float32) * s_q, 'bq': jnp.zeros((Cq,), jnp.float32), 'Wk': jax.random.normal(ks[3], (Ckv, Cq), jnp.float32) * s_kv, 'bk': jnp.zeros((Cq,), jnp.float32), 'Wv': jax.random.normal(ks[4], (Ckv, Cq), jnp.float32) * s_kv, 'bv': jnp.zeros((Cq,), jnp.float32), 'Wo': jax.random.normal(ks[5], (Cq, Cq), jnp.float32) * s_q, 'bo': jnp.zeros((Cq,), jnp.float32)}
    _L0_xattn_all = _L0_xattn_setup()
    _L0_xattn_in = {k: v for k, v in _L0_xattn_all.items() if k in ('Wq', 'bq', 'Wk', 'bk', 'Wv', 'bv', 'Wo', 'bo')}
    del _L0_xattn_all

    def _L0_ffn_setup():
        import jax, jax.numpy as jnp
        import numpy as np
        B, S, D, H, E = (4, 512, 256, 512, 8)
        key = jax.random.key(seed)
        ks = jax.random.split(key, 8)
        scale = 0.02
        return {'x': jax.random.normal(ks[0], (B, S, D), dtype=jnp.float32), 'Wr': jax.random.normal(ks[1], (D, E), dtype=jnp.float32) * scale, 'br': jnp.zeros((E,), dtype=jnp.float32), 'W1': jax.random.normal(ks[2], (E, D, H), dtype=jnp.float32) * scale, 'b1': jnp.zeros((E, H), dtype=jnp.float32), 'W2': jax.random.normal(ks[3], (E, H, D), dtype=jnp.float32) * scale, 'b2': jnp.zeros((E, D), dtype=jnp.float32)}
    _L0_ffn_all = _L0_ffn_setup()
    _L0_ffn_in = {k: v for k, v in _L0_ffn_all.items() if k in ('Wr', 'br', 'W1', 'b1', 'W2', 'b2')}
    del _L0_ffn_all

    def _L1_attn_setup():
        import jax, jax.numpy as jnp
        import numpy as np
        DIM = 256
        HEADS = 16
        DIM_HEAD = 64
        SEG = 128
        PM = 16
        THETA = 10000.0
        EPS = 1e-06

        def rmsnorm(x, w):
            var = jnp.mean(x * x, axis=-1, keepdims=True)
            return x * jax.lax.rsqrt(var + EPS) * w

        def rope(x):
            n, d = (x.shape[-2], x.shape[-1])
            inv_freq = 1.0 / THETA ** (jnp.arange(0, d, 2, dtype=jnp.float32) / d)
            freqs = jnp.arange(n, dtype=jnp.float32)[:, None] * inv_freq
            cos = jnp.repeat(jnp.cos(freqs), 2, axis=-1)
            sin = jnp.repeat(jnp.sin(freqs), 2, axis=-1)
            xp = x.reshape(*x.shape[:-1], d // 2, 2)
            x_rot = jnp.stack((-xp[..., 1], xp[..., 0]), axis=-1).reshape(x.shape)
            return x * cos + x_rot * sin
        key = jax.random.key(seed)
        ks = jax.random.split(key, 7)
        s = lambda fan_in: 1.0 / np.sqrt(fan_in)
        return {'seq': jax.random.normal(ks[0], (2, 2048, DIM), dtype=jnp.float32), 'norm_w': jnp.ones((DIM,), dtype=jnp.float32), 'w_qkv': jax.random.normal(ks[1], (DIM, 3 * HEADS * DIM_HEAD), dtype=jnp.float32) * s(DIM), 'pm_k': jax.random.normal(ks[2], (HEADS, PM, DIM_HEAD), dtype=jnp.float32) * 0.02, 'pm_v': jax.random.normal(ks[3], (HEADS, PM, DIM_HEAD), dtype=jnp.float32) * 0.02, 'w_out': jax.random.normal(ks[4], (HEADS * DIM_HEAD, DIM), dtype=jnp.float32) * s(HEADS * DIM_HEAD), 'b_out': jax.random.normal(ks[5], (DIM,), dtype=jnp.float32) * 0.01}
    _L1_attn_all = _L1_attn_setup()
    _L1_attn_in = {k: v for k, v in _L1_attn_all.items() if k in ('norm_w', 'w_qkv', 'pm_k', 'pm_v', 'w_out', 'b_out')}
    del _L1_attn_all

    def _L1_xattn_setup():
        import jax, jax.numpy as jnp
        import numpy as np
        QUERY_DIM = 256
        KEY_DIM = 192
        NUM_HEADS = 16
        HEAD_DIM = QUERY_DIM // NUM_HEADS
        SCALE = HEAD_DIM ** (-0.5)
        key = jax.random.key(seed)
        ks = jax.random.split(key, 11)
        B, Nq, Nk = (4, 1024, 256)
        s_q = QUERY_DIM ** (-0.5)
        s_k = KEY_DIM ** (-0.5)
        return {'query': jax.random.normal(ks[0], (B, Nq, QUERY_DIM), jnp.float32), 'key': jax.random.normal(ks[1], (B, Nk, KEY_DIM), jnp.float32), 'value': jax.random.normal(ks[2], (B, Nk, KEY_DIM), jnp.float32), 'Wq': jax.random.normal(ks[3], (QUERY_DIM, QUERY_DIM), jnp.float32) * s_q, 'bq': jnp.zeros((QUERY_DIM,), jnp.float32), 'Wk': jax.random.normal(ks[4], (KEY_DIM, QUERY_DIM), jnp.float32) * s_k, 'bk': jnp.zeros((QUERY_DIM,), jnp.float32), 'Wv': jax.random.normal(ks[5], (KEY_DIM, QUERY_DIM), jnp.float32) * s_k, 'bv': jnp.zeros((QUERY_DIM,), jnp.float32), 'Wo': jax.random.normal(ks[6], (QUERY_DIM, QUERY_DIM), jnp.float32) * s_q, 'bo': jnp.zeros((QUERY_DIM,), jnp.float32)}
    _L1_xattn_all = _L1_xattn_setup()
    _L1_xattn_in = {k: v for k, v in _L1_xattn_all.items() if k in ('Wq', 'bq', 'Wk', 'bk', 'Wv', 'bv', 'Wo', 'bo')}
    del _L1_xattn_all

    def _L1_ffn_setup():
        import jax, jax.numpy as jnp
        import numpy as np
        D = 256
        E = 8
        K = 2
        DF = 1024
        B, S = (2, 512)
        EPS_LN = 1e-05
        EPS_TOPK = 1e-08

        def _xavier(key, shape, fan_in, fan_out, dtype=jnp.float32):
            bound = float(np.sqrt(6.0 / (fan_in + fan_out)))
            return jax.random.uniform(key, shape, dtype, -bound, bound)
        key = jax.random.key(seed)
        kx, kg, k1, k2 = jax.random.split(key, 4)
        return {'x': jax.random.normal(kx, (B, S, D), jnp.float32), 'gamma': jnp.ones((D,), jnp.float32), 'beta': jnp.zeros((D,), jnp.float32), 'Wg': _xavier(kg, (E, D), D, E), 'bg': jnp.zeros((E,), jnp.float32), 'W1': _xavier(k1, (E, DF, D), D, DF), 'b1': jnp.zeros((E, DF), jnp.float32), 'W2': _xavier(k2, (E, D, DF), DF, D), 'b2': jnp.zeros((E, D), jnp.float32)}
    _L1_ffn_all = _L1_ffn_setup()
    _L1_ffn_in = {k: v for k, v in _L1_ffn_all.items() if k in ('gamma', 'beta', 'Wg', 'bg', 'W1', 'b1', 'W2', 'b2')}
    del _L1_ffn_all
    return {'x': x, 'ctx_768': ctx_768, 'L0_attn_Wq': _L0_attn_in['Wq'], 'L0_attn_bq': _L0_attn_in['bq'], 'L0_attn_Wk': _L0_attn_in['Wk'], 'L0_attn_bk': _L0_attn_in['bk'], 'L0_attn_Wv': _L0_attn_in['Wv'], 'L0_attn_bv': _L0_attn_in['bv'], 'L0_attn_Wo': _L0_attn_in['Wo'], 'L0_attn_bo': _L0_attn_in['bo'], 'L0_attn_rel_emb': _L0_attn_in['rel_emb'], 'L0_attn_ln_g': _L0_attn_in['ln_g'], 'L0_attn_ln_b': _L0_attn_in['ln_b'], 'L0_attn_Wpk': _L0_attn_in['Wpk'], 'L0_attn_bpk': _L0_attn_in['bpk'], 'L0_attn_Wpq': _L0_attn_in['Wpq'], 'L0_attn_bpq': _L0_attn_in['bpq'], 'L0_xattn_Wq': _L0_xattn_in['Wq'], 'L0_xattn_bq': _L0_xattn_in['bq'], 'L0_xattn_Wk': _L0_xattn_in['Wk'], 'L0_xattn_bk': _L0_xattn_in['bk'], 'L0_xattn_Wv': _L0_xattn_in['Wv'], 'L0_xattn_bv': _L0_xattn_in['bv'], 'L0_xattn_Wo': _L0_xattn_in['Wo'], 'L0_xattn_bo': _L0_xattn_in['bo'], 'L0_ffn_Wr': _L0_ffn_in['Wr'], 'L0_ffn_br': _L0_ffn_in['br'], 'L0_ffn_W1': _L0_ffn_in['W1'], 'L0_ffn_b1': _L0_ffn_in['b1'], 'L0_ffn_W2': _L0_ffn_in['W2'], 'L0_ffn_b2': _L0_ffn_in['b2'], 'L1_attn_norm_w': _L1_attn_in['norm_w'], 'L1_attn_w_qkv': _L1_attn_in['w_qkv'], 'L1_attn_pm_k': _L1_attn_in['pm_k'], 'L1_attn_pm_v': _L1_attn_in['pm_v'], 'L1_attn_w_out': _L1_attn_in['w_out'], 'L1_attn_b_out': _L1_attn_in['b_out'], 'L1_xattn_Wq': _L1_xattn_in['Wq'], 'L1_xattn_bq': _L1_xattn_in['bq'], 'L1_xattn_Wk': _L1_xattn_in['Wk'], 'L1_xattn_bk': _L1_xattn_in['bk'], 'L1_xattn_Wv': _L1_xattn_in['Wv'], 'L1_xattn_bv': _L1_xattn_in['bv'], 'L1_xattn_Wo': _L1_xattn_in['Wo'], 'L1_xattn_bo': _L1_xattn_in['bo'], 'L1_ffn_gamma': _L1_ffn_in['gamma'], 'L1_ffn_beta': _L1_ffn_in['beta'], 'L1_ffn_Wg': _L1_ffn_in['Wg'], 'L1_ffn_bg': _L1_ffn_in['bg'], 'L1_ffn_W1': _L1_ffn_in['W1'], 'L1_ffn_b1': _L1_ffn_in['b1'], 'L1_ffn_W2': _L1_ffn_in['W2'], 'L1_ffn_b2': _L1_ffn_in['b2']}

def reference(x, ctx_768, L0_attn_Wq, L0_attn_bq, L0_attn_Wk, L0_attn_bk, L0_attn_Wv, L0_attn_bv, L0_attn_Wo, L0_attn_bo, L0_attn_rel_emb, L0_attn_ln_g, L0_attn_ln_b, L0_attn_Wpk, L0_attn_bpk, L0_attn_Wpq, L0_attn_bpq, L0_xattn_Wq, L0_xattn_bq, L0_xattn_Wk, L0_xattn_bk, L0_xattn_Wv, L0_xattn_bv, L0_xattn_Wo, L0_xattn_bo, L0_ffn_Wr, L0_ffn_br, L0_ffn_W1, L0_ffn_b1, L0_ffn_W2, L0_ffn_b2, L1_attn_norm_w, L1_attn_w_qkv, L1_attn_pm_k, L1_attn_pm_v, L1_attn_w_out, L1_attn_b_out, L1_xattn_Wq, L1_xattn_bq, L1_xattn_Wk, L1_xattn_bk, L1_xattn_Wv, L1_xattn_bv, L1_xattn_Wo, L1_xattn_bo, L1_ffn_gamma, L1_ffn_beta, L1_ffn_Wg, L1_ffn_bg, L1_ffn_W1, L1_ffn_b1, L1_ffn_W2, L1_ffn_b2):
    import jax
    import jax.numpy as jnp

    def _L0_attn_ref(hidden_states, Wq, bq, Wk, bk, Wv, bv, Wo, bo, rel_emb, ln_g, ln_b, Wpk, bpk, Wpq, bpq):
        import jax, jax.numpy as jnp
        import numpy as np
        H = 16
        BUCKETS = 64
        MAX_REL = 128

        def _log_bucket(rel, bucket_size, max_position):
            mid = bucket_size // 2
            sign = jnp.sign(rel).astype(jnp.float32)
            abs_pos = jnp.where((rel < mid) & (rel > -mid), mid - 1, jnp.abs(rel)).astype(jnp.float32)
            log_pos = jnp.ceil(jnp.log(abs_pos / mid) / np.log((max_position - 1) / mid) * (mid - 1)) + mid
            bucket = jnp.where(abs_pos <= mid, rel.astype(jnp.float32), log_pos * sign)
            return bucket.astype(jnp.int32)

        def _rel_pos(seq_len):
            ids = jnp.arange(seq_len)
            rel = ids[:, None] - ids[None, :]
            return _log_bucket(rel, BUCKETS, MAX_REL)
        B, S, D = hidden_states.shape
        hd = D // H
        span = BUCKETS

        def shape_heads(x):
            return x.reshape(*x.shape[:-1], H, hd).swapaxes(-2, -3)
        q = shape_heads(hidden_states @ Wq + bq)
        k = shape_heads(hidden_states @ Wk + bk)
        v = shape_heads(hidden_states @ Wv + bv)
        scale_factor = 3
        scores = jnp.einsum('bhsd,bhkd->bhsk', q, k) / jnp.sqrt(jnp.float32(hd * scale_factor))
        mu = rel_emb.mean(-1, keepdims=True)
        var = rel_emb.var(-1, keepdims=True)
        re = (rel_emb - mu) / jnp.sqrt(var + 1e-05) * ln_g + ln_b
        pos_k = shape_heads(re @ Wpk + bpk)
        pos_q = shape_heads(re @ Wpq + bpq)
        rel = _rel_pos(S)
        bias_scale = jnp.sqrt(jnp.float32(hd * 2))
        c2p = jnp.einsum('bhsd,hkd->bhsk', q, pos_k)
        c2p_idx = jnp.clip(rel + span, 0, 2 * span - 1)
        c2p = jnp.take_along_axis(c2p, jnp.broadcast_to(c2p_idx[None, None], (B, H, S, S)), axis=-1)
        scores = scores + c2p / bias_scale
        p2c = jnp.einsum('bhsd,hkd->bhsk', k, pos_q)
        p2c_idx = jnp.clip(-rel + span, 0, 2 * span - 1)
        p2c = jnp.take_along_axis(p2c, jnp.broadcast_to(p2c_idx[None, None], (B, H, S, S)), axis=-1)
        scores = scores + p2c.swapaxes(-1, -2) / bias_scale
        probs = jax.nn.softmax(scores.astype(jnp.float32), axis=-1).astype(q.dtype)
        ctx = jnp.einsum('bhsk,bhkd->bhsd', probs, v)
        ctx = ctx.swapaxes(1, 2).reshape(B, S, D)
        return ctx @ Wo + bo

    def _L0_xattn_ref(query, key_value, Wq, bq, Wk, bk, Wv, bv, Wo, bo):
        import jax, jax.numpy as jnp
        import numpy as np
        NUM_HEADS = 16
        CLAMP = 10000.0
        B, Nq, Cq = query.shape
        Nkv = key_value.shape[1]
        H = NUM_HEADS
        D = Cq // H
        scale = D ** (-0.5)
        q = (query @ Wq + bq).reshape(B, Nq, H, D).transpose(0, 2, 1, 3)
        k = (key_value @ Wk + bk).reshape(B, Nkv, H, D).transpose(0, 2, 1, 3)
        v = (key_value @ Wv + bv).reshape(B, Nkv, H, D).transpose(0, 2, 1, 3)
        attn = jnp.einsum('bhqd,bhkd->bhqk', q, k) * scale
        attn = jnp.clip(attn, -CLAMP, CLAMP)
        attn = jax.nn.softmax(attn, axis=-1)
        attn = jnp.where(jnp.any(jnp.isnan(attn)), jnp.asarray(1.0 / Nkv, attn.dtype), attn)
        x = jnp.einsum('bhqk,bhkd->bqhd', attn, v).reshape(B, Nq, Cq)
        return x @ Wo + bo

    def _L0_ffn_ref(x, Wr, br, W1, b1, W2, b2):
        import jax, jax.numpy as jnp
        import numpy as np
        B, S, D, H, E = (4, 512, 256, 512, 8)
        d = x.shape[-1]
        tokens = x.reshape(-1, d)
        logits = tokens @ Wr + br
        probs = jax.nn.softmax(logits, axis=-1)
        expert = jnp.argmax(probs, axis=-1)
        max_prob = jnp.take_along_axis(probs, expert[:, None], axis=-1)
        h = jax.nn.relu(jnp.einsum('td,edh->teh', tokens, W1) + b1[None])
        y = jnp.einsum('teh,ehd->ted', h, W2) + b2[None]
        out = jnp.take_along_axis(y, expert[:, None, None], axis=1)[:, 0, :]
        return (out * max_prob).reshape(x.shape)

    def _L1_attn_ref(seq, norm_w, w_qkv, pm_k, pm_v, w_out, b_out):
        import jax, jax.numpy as jnp
        import numpy as np
        DIM = 256
        HEADS = 16
        DIM_HEAD = 64
        SEG = 128
        PM = 16
        THETA = 10000.0
        EPS = 1e-06

        def rmsnorm(x, w):
            var = jnp.mean(x * x, axis=-1, keepdims=True)
            return x * jax.lax.rsqrt(var + EPS) * w

        def rope(x):
            n, d = (x.shape[-2], x.shape[-1])
            inv_freq = 1.0 / THETA ** (jnp.arange(0, d, 2, dtype=jnp.float32) / d)
            freqs = jnp.arange(n, dtype=jnp.float32)[:, None] * inv_freq
            cos = jnp.repeat(jnp.cos(freqs), 2, axis=-1)
            sin = jnp.repeat(jnp.sin(freqs), 2, axis=-1)
            xp = x.reshape(*x.shape[:-1], d // 2, 2)
            x_rot = jnp.stack((-xp[..., 1], xp[..., 0]), axis=-1).reshape(x.shape)
            return x * cos + x_rot * sin
        b, n_orig, _ = seq.shape
        n_pad = -n_orig % SEG
        x = jnp.pad(seq, ((0, 0), (0, n_pad), (0, 0))) if n_pad else seq
        n = x.shape[1]
        xn = rmsnorm(x, norm_w)
        qkv = xn @ w_qkv
        q, k, v = jnp.split(qkv, 3, axis=-1)
        split = lambda t: t.reshape(b, n, HEADS, DIM_HEAD).transpose(0, 2, 1, 3)
        q, k, v = (split(q), split(k), split(v))
        q, k = (rope(q), rope(k))
        w = n // SEG
        seg = lambda t: t.reshape(b, HEADS, w, SEG, DIM_HEAD).transpose(0, 2, 1, 3, 4).reshape(b * w, HEADS, SEG, DIM_HEAD)
        q_s, k_s, v_s = (seg(q), seg(k), seg(v))
        pmk = jnp.broadcast_to(pm_k[None], (b * w, HEADS, PM, DIM_HEAD))
        pmv = jnp.broadcast_to(pm_v[None], (b * w, HEADS, PM, DIM_HEAD))
        k_s = jnp.concatenate((pmk, k_s), axis=-2)
        v_s = jnp.concatenate((pmv, v_s), axis=-2)
        scale = DIM_HEAD ** (-0.5)
        scores = jnp.einsum('bhid,bhjd->bhij', q_s, k_s) * scale
        rows = jnp.arange(SEG)[:, None]
        cols = jnp.arange(PM + SEG)[None, :]
        allowed = (cols < PM) | (cols - PM <= rows)
        scores = jnp.where(allowed, scores, jnp.finfo(scores.dtype).min)
        attn = jax.nn.softmax(scores, axis=-1)
        out = jnp.einsum('bhij,bhjd->bhid', attn, v_s)
        out = out.transpose(0, 2, 1, 3).reshape(b * w, SEG, HEADS * DIM_HEAD)
        out = out @ w_out + b_out
        out = out.reshape(b, n, DIM)[:, :n_orig]
        return out

    def _L1_xattn_ref(query, key, value, Wq, bq, Wk, bk, Wv, bv, Wo, bo):
        import jax, jax.numpy as jnp
        import numpy as np
        QUERY_DIM = 256
        KEY_DIM = 192
        NUM_HEADS = 16
        HEAD_DIM = QUERY_DIM // NUM_HEADS
        SCALE = HEAD_DIM ** (-0.5)
        B, Nq, _ = query.shape
        Nk = key.shape[1]
        q = (query @ Wq + bq).reshape(B, Nq, NUM_HEADS, HEAD_DIM).transpose(0, 2, 1, 3)
        k = (key @ Wk + bk).reshape(B, Nk, NUM_HEADS, HEAD_DIM).transpose(0, 2, 1, 3)
        v = (value @ Wv + bv).reshape(B, Nk, NUM_HEADS, HEAD_DIM).transpose(0, 2, 1, 3)
        attn = jnp.einsum('bhqd,bhkd->bhqk', q, k) * SCALE
        attn = jax.nn.softmax(attn, axis=-1)
        out = jnp.einsum('bhqk,bhkd->bhqd', attn, v)
        out = out.transpose(0, 2, 1, 3).reshape(B, Nq, QUERY_DIM)
        return out @ Wo + bo

    def _L1_ffn_ref(x, gamma, beta, Wg, bg, W1, b1, W2, b2):
        import jax, jax.numpy as jnp
        import numpy as np
        D = 256
        E = 8
        K = 2
        DF = 1024
        B, S = (2, 512)
        EPS_LN = 1e-05
        EPS_TOPK = 1e-08

        def _xavier(key, shape, fan_in, fan_out, dtype=jnp.float32):
            bound = float(np.sqrt(6.0 / (fan_in + fan_out)))
            return jax.random.uniform(key, shape, dtype, -bound, bound)
        b, s, d = x.shape
        mu = jnp.mean(x, axis=-1, keepdims=True)
        var = jnp.mean((x - mu) ** 2, axis=-1, keepdims=True)
        xn = (x - mu) / jnp.sqrt(var + EPS_LN) * gamma + beta
        xf = xn.reshape(-1, d)
        logits = xf @ Wg.T + bg
        probs = jax.nn.softmax(logits, axis=-1)
        tp, ti = jax.lax.top_k(probs, K)
        tp = tp / (jnp.sum(tp, axis=-1, keepdims=True) + EPS_TOPK)
        w = jnp.sum(jax.nn.one_hot(ti, E, dtype=xf.dtype) * tp[..., None], axis=1)
        h = jax.nn.gelu(jnp.einsum('td,efd->tef', xf, W1) + b1, approximate=False)
        y = jnp.einsum('tef,edf->ted', h, W2) + b2
        out = jnp.einsum('ted,te->td', y, w)
        return x + out.reshape(b, s, d)
    x = _layernorm(x + _L0_attn_ref(x, L0_attn_Wq, L0_attn_bq, L0_attn_Wk, L0_attn_bk, L0_attn_Wv, L0_attn_bv, L0_attn_Wo, L0_attn_bo, L0_attn_rel_emb, L0_attn_ln_g, L0_attn_ln_b, L0_attn_Wpk, L0_attn_bpk, L0_attn_Wpq, L0_attn_bpq), axis=-1)
    x = _layernorm(x + _L0_xattn_ref(x, ctx_768, L0_xattn_Wq, L0_xattn_bq, L0_xattn_Wk, L0_xattn_bk, L0_xattn_Wv, L0_xattn_bv, L0_xattn_Wo, L0_xattn_bo), axis=-1)
    x = _layernorm(x + _L0_ffn_ref(x, L0_ffn_Wr, L0_ffn_br, L0_ffn_W1, L0_ffn_b1, L0_ffn_W2, L0_ffn_b2), axis=-1)
    x = _layernorm(x + _L1_attn_ref(x, L1_attn_norm_w, L1_attn_w_qkv, L1_attn_pm_k, L1_attn_pm_v, L1_attn_w_out, L1_attn_b_out), axis=-1)
    x = _layernorm(x + _L1_xattn_ref(x, ctx_768, ctx_768, L1_xattn_Wq, L1_xattn_bq, L1_xattn_Wk, L1_xattn_bk, L1_xattn_Wv, L1_xattn_bv, L1_xattn_Wo, L1_xattn_bo), axis=-1)
    x = _layernorm(x + _L1_ffn_ref(x, L1_ffn_gamma, L1_ffn_beta, L1_ffn_Wg, L1_ffn_bg, L1_ffn_W1, L1_ffn_b1, L1_ffn_W2, L1_ffn_b2), axis=-1)
    return x

_drawn_inputs = setup_inputs


def setup_inputs(seed=0):
    import zlib

    import numpy as np

    out = dict(_drawn_inputs(seed))
    spreads = {'L0_attn_bq': (0.0, 0.8),
     'L0_attn_bk': (0.0, 0.8),
     'L0_attn_bv': (0.0, 0.1),
     'L0_attn_bo': (0.0, 0.1),
     'L0_attn_ln_g': (1.0, 0.6),
     'L0_attn_ln_b': (0.0, 0.8),
     'L0_attn_bpk': (0.0, 2.0),
     'L0_attn_bpq': (0.0, 0.8),
     'L0_xattn_bq': (0.0, 0.274),
     'L0_xattn_bk': (0.0, 2.0),
     'L0_xattn_bv': (0.0, 0.1),
     'L0_xattn_bo': (0.0, 0.1),
     'L0_ffn_br': (0.0, 0.286),
     'L0_ffn_b1': (0.0, 0.788),
     'L0_ffn_b2': (0.0, 0.302),
     'L1_attn_norm_w': (1.0, 0.2),
     'L1_xattn_bq': (0.0, 0.282),
     'L1_xattn_bk': (0.0, 2.0),
     'L1_xattn_bv': (0.0, 0.1),
     'L1_xattn_bo': (0.0, 0.1),
     'L1_ffn_gamma': (1.0, 0.2),
     'L1_ffn_beta': (0.0, 0.1),
     'L1_ffn_bg': (0.0, 0.1),
     'L1_ffn_b1': (0.0, 0.1),
     'L1_ffn_b2': (0.0, 0.1)}
    factors = {'L0_attn_Wq': 8.0,
     'L0_attn_Wk': 8.0,
     'L0_attn_Wv': 5.573,
     'L0_attn_rel_emb': 8.0,
     'L0_attn_Wpk': 8.0,
     'L0_attn_Wpq': 8.0,
     'L1_attn_pm_k': 64.0,
     'L1_attn_pm_v': 27.667,
     'L1_attn_b_out': 3.976}
    for name, (base, spread) in spreads.items():
        noise = np.random.default_rng([zlib.crc32(name.encode()), seed]).standard_normal(out[name].shape)
        drawn = base * np.exp(spread * noise) if base else spread * noise
        out[name] = jnp.asarray(drawn.astype(out[name].dtype))
    for name, factor in factors.items():
        out[name] = (out[name] * factor).astype(out[name].dtype)
    return out
```

```python
from contextlib import ExitStack

import numpy as np

import concourse.bass as bass
from concourse import mybir

F32 = mybir.dt.float32
I32 = mybir.dt.int32
U32 = mybir.dt.uint32
ALU = mybir.AluOpType
ACT = mybir.ActivationFunctionType
AXX = mybir.AxisListType.X

P = 128
B, S, D = 8, 256, 256
T = B * S
KC = D // P
NT = S // P
H, HD = 16, 16
HG = 4
NG = H // HG
HC = P // HD
CK, CD = 77, 192
CC = CD // 2
REL = 2 * S - 1
WIN = S + P - 1
CLAMP = 10000.0
LN_EPS = 1e-5


def at_least(eng, sem, value):
    if not (isinstance(value, int) and value <= 0):
        eng.wait_ge(sem, value)


def own_wait(eng, sem):
    eng.sem_inc(sem, 1)


class Chain:

    def __init__(self, eng, sem, waited=None):
        self.eng, self.sem, self.waited, self.n, self.base = eng, sem, waited, 0, 0

    def start(self, base):
        self.base, self.n = base, 0

    def link(self, ins):
        ins.then_inc(self.sem, 1)
        self.n += 1
        self.eng.wait_ge(self.sem, self.base + self.n)


def broadcast_mid(ap, n):
    return bass.AP(ap.tensor, ap.offset, [ap.ap[0], [0, n], ap.ap[1]])


def broadcast_last(ap, n):
    return bass.AP(ap.tensor, ap.offset, [ap.ap[0], ap.ap[1], [0, n]])


class Alloc:

    def __init__(self, nc, phase, prefix):
        self.nc, self.phase, self.prefix = nc, phase, prefix
        self.sems = []

    def sb(self, name, shape, dt=F32):
        return self.phase.enter_context(self.nc.sbuf_tensor(self.prefix + name, shape, dt))

    def bank(self, name):
        return self.phase.enter_context(self.nc.psum_tensor(self.prefix + name, [P, 512], F32))

    def sem(self, name):
        self.sems.append(self.nc.alloc_semaphore(name=self.prefix + name))
        return self.sems[-1]

    def end(self):
        self.nc.all_engine_barrier()
        self.nc.clear_and_free_semaphores(self.sems)
        self.nc.all_engine_barrier()


class Cross:

    VECTOR_LINKS = 2 * (2 + 1) + 1 + 1
    POOL_LINKS = 1

    def __init__(self, al, a, w, clip, banks, shared):
        self.nc, self.a, self.clip = al.nc, a, clip
        self.w = w
        (self.FR0, self.FR1, self.SQ, self.TR, self.PO) = banks
        self.wq = al.sb("xwq", [P, KC, D])
        self.wk = al.sb("xwk", [CC, 2, D])
        self.wv = al.sb("xwv", [CC, 2, D])
        self.wo = al.sb("xwo", [P, NG, D])
        self.ctxT = al.sb("ctxT", [CC, 2, CK])
        self.x1T, self.OT, self.R, self.PT = shared
        self.qT = al.sb("xqT", [P, KC, S])
        self.kM = al.sb("xkM", [P, KC, HC * CK])
        self.v = al.sb("xv", [CK, H, 32])
        self.SX = al.sb("SX", [P, NT, H * CK])
        self.PX = self.SX
        self.mx = al.sb("xmx", [P, NT, H])
        self.sm = al.sb("xsm", [P, NT, H])
        self.rs = al.sb("xrs", [P, NT, H])
        self.X1B = al.sb("X1B", [P, NT, D])
        self.st = al.sb("xst", [P, NT, 6])
        self.mv = al.sb("xmv", [P, NT, 2])
        self.ve = al.sb("xve", [P, NT])
        self.rstd = al.sb("xrstd", [P, NT])
        self.X2 = al.sb("X2", [P, NT, D])
        s = al.sem
        self.sp_waited = s("x_sp_waited")
        self.weights = s("x_weights")
        self.zeroed = s("x_zeroed")
        self.ctx_in = s("x_ctx_in")
        self.x1T_ps = s("x_x1T_ps")
        self.x1T_sb = s("x_x1T_sb")
        self.q_ps = s("x_q_ps")
        self.q_sb = s("x_q_sb")
        self.kv_ps = s("x_kv_ps")
        self.kv_sb = s("x_kv_sb")
        self.sc_ps = s("x_sc_ps")
        self.sc_sb = s("x_sc_sb")
        self.shifted = s("x_shifted")
        self.exped = s("x_exped")
        self.recip = s("x_recip")
        self.normed = s("x_normed")
        self.pT_ps = s("x_pT_ps")
        self.pT_sbA = s("x_pT_sbA")
        self.pT_sbV = s("x_pT_sbV")
        self.o_ps = s("x_o_ps")
        self.o_sb = s("x_o_sb")
        self.y_ps = s("x_y_ps")
        self.x1b = s("x_x1b")
        self.r_sb = s("x_r_sb")
        self.var = s("x_var")
        self.rstd_ok = s("x_rstd")
        self.x2 = s("x_x2")
        self.stored = s("x_stored")

    def load_weights(self, sp):
        w = self.w
        sp.dma_start(self.wq[:], w["Wq"].rearrange("(k p) n -> p k n", p=P)).then_inc(self.weights, 16)
        sp.dma_start(self.wk[:], w["Wk"].rearrange("(k p) n -> p k n", p=CC)).then_inc(self.weights, 16)
        sp.dma_start(self.wv[:], w["Wv"].rearrange("(k p) n -> p k n", p=CC)).then_inc(self.weights, 16)
        sp.wait_ge(self.zeroed, 2)
        wo = w["Wo"].rearrange("(g j i) n -> j i g n", j=HG, i=HD)
        for j in range(HG):
            sp.dma_start(self.wo[32 * j:32 * j + HD, :, :], wo[j]).then_inc(self.weights, 16)

    WEIGHTS = (3 + HG) * 16

    def load_ctx(self, sp, b):
        at_least(sp, self.kv_ps, b)
        own_wait(sp, self.sp_waited)
        sp.dma_start(self.ctxT[:], self.a["ctxT"][b].rearrange("(k p) n -> p k n", p=CC)).then_inc(self.ctx_in, 16)

    def store(self, sp, b):
        sp.wait_ge(self.x2, b + 1)
        own_wait(sp, self.sp_waited)
        sp.dma_start(self.a["x2_out"][b].rearrange("(t p) n -> p t n", p=P), self.X2[:]).then_inc(self.stored, 16)

    def tensor(self, pe, b, x1_ready, banks_free):
        nc = self.nc
        pe.wait_ge(*x1_ready)
        banks_free(pe)
        for t in range(NT):
            for k in range(KC):
                last = nc.tensor.transpose(self.FR0[:, k * S + t * P:k * S + (t + 1) * P],
                                           self.a["X1"][:, t, k * P:(k + 1) * P], self.a["ident"][:])
        last.then_inc(self.x1T_ps, 1)
        pe.wait_ge(self.ctx_in, b * 16 + 16)
        pe.wait_ge(self.x1T_sb, b + 1)
        for c in range(KC):
            for k in range(KC):
                last = nc.tensor.matmul(self.FR1[:, c * S:(c + 1) * S], self.wq[:, k, c * P:(c + 1) * P],
                                        self.x1T[:, k, :], start=k == 0, stop=k == KC - 1)
        last.then_inc(self.q_ps, 1)
        for c in range(KC):
            for k in range(2):
                nc.tensor.matmul(self.FR0[:, c * CK:(c + 1) * CK], self.wk[:, k, c * P:(c + 1) * P],
                                 self.ctxT[:, k, :], start=k == 0, stop=k == 1)
        for k in range(2):
            last = nc.tensor.matmul(self.FR0[0:CK, S:S + D], self.ctxT[:, k, :], self.wv[:, k, :],
                                    start=k == 0, stop=k == 1)
        last.then_inc(self.kv_ps, 1)
        pe.wait_ge(self.q_sb, b + 1)
        pe.wait_ge(self.kv_sb, b + 1)
        for t in range(NT):
            for q in range(4):
                if t:
                    pe.wait_ge(self.sc_sb, 8 * b + q + 1)
                nc.tensor.matmul(self.SQ[q][:, 0:4 * CK], self.qT[:, q // 2, t * P:(t + 1) * P],
                                 self.kM[:, q // 2, (q % 2) * 4 * CK:(q % 2 + 1) * 4 * CK],
                                 start=True, stop=True).then_inc(self.sc_ps, 1)
        for hp in range(H // 2):
            if hp == 0:
                pe.wait_ge(self.normed, 2 * b + 2)
            if hp >= 2:
                pe.wait_ge(self.pT_sbA if hp % 2 == 0 else self.pT_sbV, 4 * b + hp // 2)
            for u in range(2):
                for t in range(NT):
                    h = 2 * hp + u
                    last = nc.tensor.transpose(self.TR[hp % 2][0:CK, u * S + t * P:u * S + (t + 1) * P],
                                               self.PX[:, t, h * CK:(h + 1) * CK], self.a["ident"][:])
            last.then_inc(self.pT_ps, 1)
        for g in range(NG):
            pe.wait_ge(self.pT_sbA, 4 * b + g + 1)
            pe.wait_ge(self.pT_sbV, 4 * b + g + 1)
            if g:
                pe.wait_ge(self.o_sb, 4 * b + g)
            for j in range(HG):
                h = HG * g + j
                last = nc.tensor.matmul(self.PO[32 * j:32 * j + 32, 0:S], self.v[:, h, :], self.PT[:, h, :],
                                        start=True, stop=True)
            last.then_inc(self.o_ps, 1)
        pe.wait_ge(self.o_sb, 4 * b + 4)
        for t in range(NT):
            for g in range(NG):
                last = nc.tensor.matmul(self.FR1[:, t * D:(t + 1) * D], self.OT[:, g, t * P:(t + 1) * P],
                                        self.wo[:, g, :], start=g == 0, stop=g == NG - 1)
        last.then_inc(self.y_ps, 1)

    def scalar(self, act, b):
        nc = self.nc
        act.wait_ge(self.x1T_ps, b + 1)
        nc.scalar.activation(self.x1T[:].rearrange("p k n -> p (k n)"), self.FR0[:], ACT.Copy).then_inc(self.x1T_sb, 1)
        act.wait_ge(self.q_ps, b + 1)
        for c in range(KC):
            last = nc.scalar.activation(self.qT[:, c, :], self.FR1[:, c * S:(c + 1) * S], ACT.Identity,
                                        bias=self.a["xbq"][:, c:c + 1])
        last.then_inc(self.q_sb, 1)
        for t in range(NT):
            if not self.clip:
                for q in range(4):
                    act.wait_ge(self.sc_ps, 8 * b + 4 * t + q + 1)
                    nc.scalar.activation(self.SX[:, t, q * 4 * CK:(q + 1) * 4 * CK], self.SQ[q][:, 0:4 * CK],
                                         ACT.Copy).then_inc(self.sc_sb, 1)
        for t in range(NT):
            act.wait_ge(self.shifted, 2 * b + t + 1)
            nc.scalar.activation(self.PX[:, t, :], self.SX[:, t, :], ACT.Exp,
                                 scale=float(HD) ** -0.5).then_inc(self.exped, 1)
        for hp in range(0, H // 2, 2):
            act.wait_ge(self.pT_ps, 8 * b + hp + 1)
            nc.scalar.activation(self.PT[:, 2 * hp:2 * hp + 2, :].rearrange("p h n -> p (h n)"),
                                 self.TR[0][0:CK, :], ACT.Copy).then_inc(self.pT_sbA, 1)
        for g in range(NG):
            act.wait_ge(self.o_ps, 4 * b + g + 1)
            nc.scalar.activation(self.OT[:, g, :], self.PO[:, 0:S], ACT.Copy).then_inc(self.o_sb, 1)

    def vector(self, dve, b, chain):
        nc, a = self.nc, self.a
        dve.wait_ge(self.kv_ps, b + 1)
        for c in range(KC):
            nc.vector.scalar_tensor_tensor(
                out=self.kM[:, c, :].rearrange("p (h n) -> p h n", h=HC),
                in0=broadcast_mid(self.FR0[:, c * CK:(c + 1) * CK], HC), scalar=a["xbk"][:, c:c + 1],
                in1=broadcast_last(a["headmask"][:, 0:HC], CK), op0=ALU.add, op1=ALU.mult)
        nc.vector.tensor_tensor(self.v[:, :, 0:HD], self.FR0[0:CK, S:S + D].rearrange("p (h n) -> p h n", h=H),
                                a["xbv"][0:CK, :].rearrange("p (h n) -> p h n", h=H), ALU.add).then_inc(self.kv_sb, 1)
        lim = CLAMP / float(HD) ** -0.5
        for t in range(NT):
            if self.clip:
                for q in range(4):
                    dve.wait_ge(self.sc_ps, 8 * b + 4 * t + q + 1)
                    last = nc.vector.tensor_scalar(self.SX[:, t, q * 4 * CK:(q + 1) * 4 * CK], self.SQ[q][:, 0:4 * CK],
                                                   lim, -lim, ALU.min, ALU.max)
                    last.then_inc(self.sc_sb, 1)
            dve.wait_ge(self.sc_sb, 8 * b + 4 * t + 4)
            chain.link(nc.vector.tensor_reduce(self.mx[:, t, :], self.SX[:, t, :].rearrange("p (h n) -> p h n", h=H),
                                               AXX, ALU.max))
            nc.vector.tensor_tensor(self.SX[:, t, :].rearrange("p (h n) -> p h n", h=H),
                                    self.SX[:, t, :].rearrange("p (h n) -> p h n", h=H),
                                    broadcast_last(self.mx[:, t, :], CK), ALU.subtract).then_inc(self.shifted, 1)
        for t in range(NT):
            dve.wait_ge(self.exped, 2 * b + t + 1)
            chain.link(nc.vector.tensor_reduce(self.sm[:, t, :], self.PX[:, t, :].rearrange("p (h n) -> p h n", h=H),
                                               AXX, ALU.add))
            nc.vector.reciprocal(self.rs[:, t, :], self.sm[:, t, :]).then_inc(self.recip, 1)
        for hp in range(1, H // 2, 2):
            dve.wait_ge(self.pT_ps, 8 * b + hp + 1)
            nc.vector.tensor_copy(self.PT[:, 2 * hp:2 * hp + 2, :].rearrange("p h n -> p (h n)"),
                                  self.TR[1][0:CK, :]).then_inc(self.pT_sbV, 1)
        dve.wait_ge(self.y_ps, b + 1)
        dve.wait_ge(self.x1b, b + 1)
        nc.vector.tensor_tensor(self.R[:].rearrange("p t n -> p (t n)"), self.FR1[:],
                                self.X1B[:].rearrange("p t n -> p (t n)"), ALU.add).then_inc(self.r_sb, 1)
        dve.wait_ge(self.r_sb, b + 1)
        layernorm_stats(nc, chain, self.R, self.st, self.mv, self.ve, self.var, LN_EPS)
        dve.wait_ge(self.rstd_ok, b + 1)
        at_least(dve, self.stored, 16 * b)
        layernorm_apply(nc, self.R, self.mv, self.rstd, self.X2).then_inc(self.x2, 1)

    def pool(self, pool, b, x1_ready):
        nc, a = self.nc, self.a
        pool.wait_ge(*x1_ready)
        at_least(pool, self.r_sb, b)
        nc.gpsimd.tensor_tensor(self.X1B[:], a["X1"][:], broadcast_mid(a["xbo"], NT), ALU.add).then_inc(self.x1b, 1)
        for t in range(NT):
            pool.wait_ge(self.recip, 2 * b + t + 1)
            v = self.PX[:, t, :].rearrange("p (h n) -> p h n", h=H)
            nc.gpsimd.tensor_tensor(v, v, broadcast_last(self.rs[:, t, :], CK), ALU.mult).then_inc(self.normed, 1)
        pool.wait_ge(self.var, b + 1)
        nc.gpsimd.tensor_tensor(self.rstd[:], self.ve[:], a["neghalf"][:, 0:NT], ALU.pow).then_inc(self.rstd_ok, 1)

    VECTOR_LINKS = 2 * NT + 2


def layernorm_stats(nc, chain, R, st, mv, ve, var, eps):
    for t in range(NT):
        last = nc.vector.bn_stats(st[:, t, :], R[:, t, :])
    chain.link(last)
    own_wait(chain.eng, chain.waited)
    for t in range(NT):
        last = nc.vector.bn_aggr(mv[:, t, :], st[:, t, :])
    chain.link(last)
    nc.vector.tensor_scalar(ve[:], mv[:, :, 1], eps, None, ALU.add).then_inc(var, 1)


def layernorm_apply(nc, R, mv, rstd, out):
    for t in range(NT):
        last = nc.vector.tensor_scalar(out[:, t, :], R[:, t, :], mv[:, t, 0:1], rstd[:, t:t + 1],
                                       ALU.subtract, ALU.mult)
    return last


def relative_attention_phase(nc, d):
    with ExitStack() as phase:
        al = Alloc(nc, phase, "a_")
        sb, sem = al.sb, al.sem
        scale = float(3 * HD) ** -0.5
        table_scale = float(3 * HD / (2 * HD)) ** 0.5

        FR0, FR1, BD0, BD1, SC0, SC1, PTB, PO = [al.bank(n) for n in
                                                 ("FR0", "FR1", "BD0", "BD1", "SC0", "SC1", "PTB", "PO")]
        BD, SC = [BD0, BD1], [SC0, SC1]

        ident = sb("ident", [P, P])
        headmask = sb("headmask", [P, HC])
        col = sb("col", [P, 8])
        row = sb("row", [P, 5, D])
        neghalf = sb("neghalf", [P, NT])
        wq = sb("wq", [P, KC, D])
        wk = sb("wk", [P, KC, D])
        wv = sb("wv", [P, KC, D])
        wo = sb("wo", [P, NG, D])
        E = [sb("E1", [P, KC, REL]), sb("E2", [P, KC, REL])]
        XIN = sb("XIN", [P, NT, D])
        XB = sb("XB", [P, NT, D])
        xT = sb("xT", [P, KC, S])
        qM = sb("qM", [P, H, S])
        kT = sb("kT", [P, KC, S])
        kM = sb("kM", [P, H, S])
        v = sb("v", [P, NT, H, 32])
        ST = [[sb(f"stage{k}{i}", [P, HG, NT, WIN]) for i in range(2)] for k in range(2)]
        SK1 = sb("skewed1", [P, 2, HG, NT, S])
        SK = [[sb(f"skewed{k}0", [P, HG, NT, S]), SK1[:, k]] for k in range(2)]
        SS = sb("SS", [P, 2, NT, S])
        PR = sb("PR", [P, 2, NT, S])
        mx = sb("mx", [P, 2, NT])
        nb = sb("nb", [P, 2, NT])
        sm = sb("sm", [P, 2, NT])
        rs = sb("rs", [P, 2, NT])
        OT = sb("OT", [P, NG, S])
        R = sb("R", [P, NT, D])
        st = sb("st", [P, NT, 6])
        mv = sb("mv", [P, NT, 2])
        ve = sb("ve", [P, NT])
        rstd = sb("rstd", [P, NT])
        X1 = sb("X1", [P, NT, D])
        remb = SS[:, 0, 0, :]
        rows = [PR[:, 0, 0, :], PR[:, 0, 1, :]]
        prow = ST[0][0][:].rearrange("p h i w -> p (h i w)")[:, 0:4 * D].rearrange("p (r n) -> p r n", r=4)

        scratch = [nc.dram_tensor(f"a_band{k}", (2, HG * NT, P, WIN), F32, kind="Internal").ap() for k in range(2)]

        a = {"ident": ident, "headmask": headmask, "neghalf": neghalf, "X1": X1,
             "ctxT": d["ctxT"], "x2_out": d["x2"],
             "xbq": col[:, 4:6], "xbk": col[:, 6:8], "xbv": row[:, 3, :], "xbo": row[:, 4, :]}
        x = Cross(al, a, d["L0_xattn"], True, (FR0, FR1, [BD0, BD1, SC0, SC1], [PTB, SC1], PO),
                  (xT, OT, R, SK1[0:CK].rearrange("p k h i s -> p (k h i) s")))
        PTr = sb("PTr", [P, 4, NT, S])

        consts = sem("consts")
        weights = sem("weights")
        zeroed = sem("zeroed")
        tv = sem("table_vector")
        tp = sem("table_pool")
        tt = sem("table_tensor")
        x_in, sp_waited = sem("x_in"), sem("sp_waited")
        xT_ps, xT_sb = sem("xT_ps"), sem("xT_sb")
        q_ps, k_ps, v_ps = sem("q_ps"), sem("k_ps"), sem("v_ps")
        q_sb, k_sb, v_sb, kM_sb, xb = sem("q_sb"), sem("k_sb"), sem("v_sb"), sem("kM_sb"), sem("xb")
        band_ps = [sem("band_ps0"), sem("band_ps1")]
        band_sb = [sem("band_sb0"), sem("band_sb1")]
        band_out = sem("band_out")
        band_in = [sem("band_in0"), sem("band_in1")]
        sc_ps = sem("sc_ps")
        maxed = sem("maxed")
        negmax = sem("negmax")
        exped = sem("exped")
        normed = sem("normed")
        pT_ps, pT_sb = sem("pT_ps"), sem("pT_sb")
        o_ps, o_sb = sem("o_ps"), sem("o_sb")
        y_ps, r_sb, var, rstd_ok, x1_ok = sem("y_ps"), sem("r_sb"), sem("var"), sem("rstd"), sem("x1")
        dv, waited = sem("dve_chain"), sem("dve_waited")

        ATTN_LINKS = H + 2
        LINKS = ATTN_LINKS + x.VECTOR_LINKS
        X1_READY = lambda b: (x1_ok, b + 1)

        with nc.Block() as block:

            @block.sync
            def _(sp):
                for dst, src in ((ident[:], d["ident"]), (headmask[:], d["headmask"]), (col[:], d["L0_col"]),
                                 (remb, d["L0_rel_emb"]),
                                 (row[:], d["L0_row"].partition_broadcast(P)),
                                 (prow, d["L0_prow"].partition_broadcast(P)),
                                 (qM[:, 0:4, :].rearrange("p h n -> p (h n)")[:, 0:2 * REL], d["onehot"])):
                    sp.dma_start(dst, src).then_inc(consts, 16)
                for dst, src in ((kM[:, 0:2, :], d["L0_Wpk"]), (kM[:, 2:4, :], d["L0_Wpq"]), (wq[:], d["L0_Wq"]),
                                 (wk[:], d["L0_Wk"]), (wv[:], d["L0_Wv"])):
                    sp.dma_start(dst, src.rearrange("(k p) n -> p k n", p=P)).then_inc(weights, 16)
                sp.wait_ge(zeroed, 2)
                w4 = d["L0_Wo"].rearrange("(g j i) n -> j i g n", j=HG, i=HD)
                for j in range(HG):
                    sp.dma_start(wo[32 * j:32 * j + HD, :, :], w4[j]).then_inc(weights, 16)
                x.load_weights(sp)

                def load_x(b):
                    at_least(sp, xb, b)
                    at_least(sp, xT_ps, b)
                    own_wait(sp, sp_waited)
                    sp.dma_start(XIN[:], d["x"][b].rearrange("(t p) n -> p t n", p=P)).then_inc(x_in, 16)

                def bands(b, g):
                    n = 4 * b + g
                    for i in range(2):
                        sp.wait_ge(band_sb[i], 32 * b + 8 * (g + 1))
                    own_wait(sp, sp_waited)
                    for k in range(2):
                        at_least(sp, band_in[k], 16 * (n - 1))
                        sp.dma_start(scratch[k][g % 2].rearrange("n p w -> p n w"),
                                     ST[k][g % 2][:].rearrange("p h i w -> p (h i) w")).then_inc(band_out, 16)
                    sp.wait_ge(band_out, 32 * (n + 1))
                    own_wait(sp, sp_waited)
                    at_least(sp, maxed, 4 * (n - 1))
                    at_least(sp, sc_ps, 4 * (n - 1))
                    if g == 1:
                        at_least(sp, x.o_ps, 4 * b)
                    for k in range(2):
                        base = scratch[k][g % 2]
                        src = bass.AP(base.tensor, base.offset + P - 1,
                                      [[WIN - 1, P], [P * WIN, HG * NT], [1, S]])
                        sp.dma_start((SK[k][0][:] if g % 2 == 0 else SK[k][1]).rearrange("p h i s -> p (h i) s"), src).then_inc(band_in[k], 16)

                load_x(0)
                bands(0, 0)
                def step(b):
                    load_x(b + 1)
                    for g in range(1, NG):
                        bands(b, g)
                    bands(b + 1, 0)
                    x.load_ctx(sp, b)
                    x.store(sp, b)

                step(0)
                with sp.Fori(1, B - 1) as b:
                    step(b)
                for g in range(1, NG):
                    bands(B - 1, g)
                x.load_ctx(sp, B - 1)
                x.store(sp, B - 1)
                sp.wait_ge(x.stored, 16 * B)

            @block.tensor
            def _(pe):
                pe.wait_ge(consts, 112)
                pe.wait_ge(weights, (5 + HG) * 16)
                pe.wait_ge(x.weights, x.WEIGHTS)
                pe.wait_ge(tv, 5)
                for k in range(KC):
                    last = nc.tensor.transpose(FR0[:, k * P:(k + 1) * P], remb[:, k * P:(k + 1) * P], ident[:])
                last.then_inc(tt, 1)
                pe.wait_ge(tv, 6)
                for n in range(2):
                    for k in range(KC):
                        last = nc.tensor.matmul(FR1[:, n * D:(n + 1) * D], xT[:, k, 0:P], kM[:, 2 * n + k, :],
                                                start=k == 0, stop=k == KC - 1)
                last.then_inc(tt, 1)
                pe.wait_ge(tv, 8)
                onehot = qM[:, 0:4, :].rearrange("p h n -> p (h n)")
                for n in range(2):
                    for c in range(KC):
                        last = nc.tensor.matmul([BD0, BD1, SC0, SC1][2 * n + c][:, 0:REL],
                                                rows[n][:, c * P:(c + 1) * P], onehot[:, n * REL:(n + 1) * REL],
                                                start=True, stop=True)
                last.then_inc(tt, 1)
                pe.wait_ge(tv, 9)

                def front(b):
                    pe.wait_ge(x_in, 16 * b + 16)
                    at_least(pe, x.kv_sb, b - 1)
                    for t in range(NT):
                        for k in range(KC):
                            last = nc.tensor.transpose(FR0[:, k * S + t * P:k * S + (t + 1) * P],
                                                       XIN[:, t, k * P:(k + 1) * P], ident[:])
                    last.then_inc(xT_ps, 1)
                    pe.wait_ge(xT_sb, b + 1)
                    at_least(pe, r_sb, b)
                    for c in range(KC):
                        for k in range(KC):
                            last = nc.tensor.matmul(FR1[:, c * S:(c + 1) * S], wq[:, k, c * P:(c + 1) * P],
                                                    xT[:, k, :], start=k == 0, stop=k == KC - 1)
                    last.then_inc(q_ps, 1)
                    for c in range(KC):
                        for k in range(KC):
                            last = nc.tensor.matmul(FR0[:, c * S:(c + 1) * S], wk[:, k, c * P:(c + 1) * P],
                                                    xT[:, k, :], start=k == 0, stop=k == KC - 1)
                    last.then_inc(k_ps, 1)
                    pe.wait_ge(q_sb, b + 1)
                    for t in range(NT):
                        for k in range(KC):
                            last = nc.tensor.matmul(FR1[:, t * D:(t + 1) * D], xT[:, k, t * P:(t + 1) * P],
                                                    wv[:, k, :], start=k == 0, stop=k == KC - 1)
                    last.then_inc(v_ps, 1)

                def band(b, h):
                    if h == 0:
                        pe.wait_ge(q_sb, b + 1)
                        pe.wait_ge(kM_sb, b + 1)
                    c = h // HC
                    for k, src in enumerate((qM, kM)):
                        for i in range(NT):
                            at_least(pe, band_sb[i], 32 * b + 2 * h + k)
                            nc.tensor.matmul(BD[i][:, 0:WIN], src[:, h, i * P:(i + 1) * P],
                                             E[k][:, c, P - P * i:P - P * i + WIN],
                                             start=True, stop=True).then_inc(band_ps[i], 1)

                def scores(b, h):
                    g, c = h // HG, h // HC
                    if h % HG == 0:
                        pe.wait_ge(band_in[1], 16 * (4 * b + g + 1))
                    if h >= 2:
                        pe.wait_ge(maxed, 16 * b + h - 1)
                    for i in range(NT):
                        for j in range(NT):
                            nc.tensor.matmul(SC[h % 2][:, i * S + j * P:i * S + (j + 1) * P],
                                             SK[1][g % 2][:, h % HG, j, i * P:(i + 1) * P], ident[:],
                                             start=j == 0, stop=False, skip_group_check=True)
                        last = nc.tensor.matmul(SC[h % 2][:, i * S:(i + 1) * S], qM[:, h, i * P:(i + 1) * P],
                                                kT[:, c, :], start=False, stop=True, skip_group_check=True)
                    last.then_inc(sc_ps, 1)

                def transposes(b, h):
                    pe.wait_ge(normed, 16 * b + h + 1)
                    at_least(pe, pT_sb, 16 * b + h)
                    for j in range(NT):
                        for i in range(NT):
                            last = nc.tensor.transpose(PTB[:, j * S + i * P:j * S + (i + 1) * P],
                                                       PR[:, h % 2, i, j * P:(j + 1) * P], ident[:])
                    last.then_inc(pT_ps, 1)

                def outputs(b, h):
                    pe.wait_ge(pT_sb, 16 * b + h + 1)
                    g, j = h // HG, h % HG
                    if j == 0:
                        at_least(pe, o_sb, 4 * b + g)
                    for t in range(NT):
                        last = nc.tensor.matmul(PO[32 * j:32 * j + 32, 0:S], v[:, t, h, :], PTr[:, h % 4, t, :],
                                                start=t == 0, stop=t == NT - 1)
                    last.then_inc(o_ps, 1)

                def attention(b):
                    for h in range(H):
                        if h + HG < H:
                            band(b, h + HG)
                        scores(b, h)
                        if h >= 1:
                            transposes(b, h - 1)
                        if h >= 2:
                            outputs(b, h - 2)
                    transposes(b, H - 1)
                    outputs(b, H - 2)
                    outputs(b, H - 1)
                    pe.wait_ge(o_sb, 4 * b + NG)
                    at_least(pe, x.r_sb, b)
                    for t in range(NT):
                        for g in range(NG):
                            last = nc.tensor.matmul(FR1[:, t * D:(t + 1) * D], OT[:, g, t * P:(t + 1) * P],
                                                    wo[:, g, :], start=g == 0, stop=g == NG - 1)
                    last.then_inc(y_ps, 1)

                def banks_free(b, staged):
                    def wait(pe):
                        pe.wait_ge(k_sb, staged // 32 if isinstance(staged, int) else b + 2)
                        for i in range(2):
                            pe.wait_ge(band_sb[i], staged)
                        if not isinstance(staged, int):
                            pe.wait_ge(v_sb, b + 2)
                    return wait

                front(0)
                for h in range(HG):
                    band(0, h)
                def step(b):
                    attention(b)
                    front(b + 1)
                    for h in range(HG):
                        band(b + 1, h)
                    x.tensor(pe, b, X1_READY(b), banks_free(b, 32 * (b + 1) + 8))

                step(0)
                with pe.Fori(1, B - 1) as b:
                    step(b)
                attention(B - 1)
                x.tensor(pe, B - 1, X1_READY(B - 1), banks_free(B - 1, 32 * B))

            @block.scalar
            def _(act):
                act.wait_ge(consts, 112)

                def front(b):
                    act.wait_ge(xT_ps, b + 1)
                    at_least(act, v_ps, b)
                    nc.scalar.activation(xT[:].rearrange("p k n -> p (k n)"), FR0[:], ACT.Copy).then_inc(xT_sb, 1)
                    act.wait_ge(k_ps, b + 1)
                    for c in range(KC):
                        last = nc.scalar.activation(kT[:, c, :], FR0[:, c * S:(c + 1) * S], ACT.Identity,
                                                    bias=col[:, 2 + c:3 + c])
                    last.then_inc(k_sb, 1)

                def stage(b, h):
                    g = h // HG
                    for k in range(2):
                        if h % HG == 0 and k == 0:
                            at_least(act, band_out, 32 * (4 * b + g - 1))
                        act.wait_ge(band_ps[0], 32 * b + 2 * h + k + 1)
                        nc.scalar.activation(ST[k][g % 2][:, h % HG, 0, :], BD0[:, 0:WIN],
                                             ACT.Copy).then_inc(band_sb[0], 1)

                def exps(b, h):
                    act.wait_ge(negmax, 16 * b + h + 1)
                    if h >= 2:
                        act.wait_ge(pT_ps, 16 * b + h - 1)
                    for i in range(NT):
                        last = nc.scalar.activation(PR[:, h % 2, i, :], SS[:, h % 2, i, :], ACT.Exp,
                                                    bias=nb[:, h % 2, i:i + 1], scale=scale,
                                                    accum_out=sm[:, h % 2, i:i + 1])
                    last.then_inc(exped, 1)

                def copy_pT(b, h):
                    act.wait_ge(pT_ps, 16 * b + h + 1)
                    if h >= 4:
                        act.wait_ge(o_ps, 16 * b + h - 3)
                    nc.scalar.activation(PTr[:, h % 4, :, :].rearrange("p t s -> p (t s)"), PTB[:],
                                         ACT.Copy).then_inc(pT_sb, 1)

                def copy_o(b, g):
                    act.wait_ge(o_ps, 16 * b + HG * (g + 1))
                    at_least(act, y_ps, b)
                    nc.scalar.activation(OT[:, g, :], PO[:, 0:S], ACT.Copy).then_inc(o_sb, 1)

                def attention(b):
                    for h in range(H):
                        if h + HG < H:
                            stage(b, h + HG)
                        exps(b, h)
                        if h >= 1:
                            copy_pT(b, h - 1)
                        if h >= HG + 1 and h % HG == 1:
                            copy_o(b, h // HG - 1)
                    copy_pT(b, H - 1)
                    copy_o(b, NG - 1)

                front(0)
                for h in range(HG):
                    stage(0, h)
                def step(b):
                    attention(b)
                    front(b + 1)
                    for h in range(HG):
                        stage(b + 1, h)
                    x.scalar(act, b)

                step(0)
                with act.Fori(1, B - 1) as b:
                    step(b)
                attention(B - 1)
                x.scalar(act, B - 1)

            @block.vector
            def _(dve):
                chain = Chain(dve, dv, waited)
                nc.vector.memset(wo[:], 0.0).then_inc(zeroed, 1)
                nc.vector.memset(v[:], 0.0).then_inc(zeroed, 1)
                nc.vector.memset(x.wo[:], 0.0).then_inc(x.zeroed, 1)
                nc.vector.memset(x.v[:], 0.0).then_inc(x.zeroed, 1)
                dve.wait_ge(consts, 112)
                nc.vector.bn_stats(st[:, 0, :], remb).then_inc(tv, 1)
                dve.wait_ge(tv, 1)
                nc.vector.bn_aggr(mv[:, 0, :], st[:, 0, :]).then_inc(tv, 1)
                dve.wait_ge(tv, 2)
                nc.vector.tensor_scalar(ve[:, 0:1], mv[:, 0, 1:2], LN_EPS, None, ALU.add).then_inc(tv, 1)
                dve.wait_ge(tp, 2)
                nc.vector.tensor_scalar(remb, remb, mv[:, 0, 0:1], rstd[:, 0:1], ALU.subtract,
                                        ALU.mult).then_inc(tv, 1)
                dve.wait_ge(tv, 4)
                nc.vector.tensor_tensor(remb, remb, prow[:, 0, :], ALU.mult).then_inc(zeroed, 1)
                dve.wait_ge(zeroed, 3)
                nc.vector.tensor_tensor(remb, remb, prow[:, 1, :], ALU.add).then_inc(tv, 1)
                dve.wait_ge(tt, 1)
                nc.vector.tensor_copy(xT[:, :, 0:P], FR0[:, 0:D].rearrange("p (k n) -> p k n", k=KC)).then_inc(tv, 1)
                dve.wait_ge(tt, 2)
                for n in range(2):
                    nc.vector.tensor_tensor(rows[n], FR1[:, n * D:(n + 1) * D], prow[:, 2 + n, :],
                                            ALU.add).then_inc(tv, 1)
                dve.wait_ge(tt, 3)
                for n in range(2):
                    for c in range(KC):
                        last = nc.vector.tensor_scalar(E[n][:, c, :], [BD0, BD1, SC0, SC1][2 * n + c][:, 0:REL],
                                                       table_scale, None, ALU.mult)
                last.then_inc(tv, 1)

                def front(b):
                    dve.wait_ge(q_ps, b + 1)
                    for c in range(KC):
                        last = nc.vector.scalar_tensor_tensor(
                            out=qM[:, c * HC:(c + 1) * HC, :], in0=broadcast_mid(FR1[:, c * S:(c + 1) * S], HC),
                            scalar=col[:, c:c + 1], in1=broadcast_last(headmask[:], S), op0=ALU.add, op1=ALU.mult)
                    last.then_inc(q_sb, 1)
                    dve.wait_ge(v_ps, b + 1)
                    nc.vector.tensor_tensor(v[:, :, :, 0:HD].rearrange("p t h n -> p (t h) n"),
                                            FR1[:].rearrange("p (g n) -> p g n", n=HD),
                                            row[:, 0:2, :].rearrange("p t (h n) -> p (t h) n", n=HD),
                                            ALU.add).then_inc(v_sb, 1)

                def stage(b, h):
                    g = h // HG
                    for k in range(2):
                        if h % HG == 0 and k == 0:
                            at_least(dve, band_out, 32 * (4 * b + g - 1))
                        dve.wait_ge(band_ps[1], 32 * b + 2 * h + k + 1)
                        nc.vector.tensor_copy(ST[k][g % 2][:, h % HG, 1, :], BD1[:, 0:WIN]).then_inc(band_sb[1], 1)

                def maxima(b, h):
                    g = h // HG
                    if h % HG == 0:
                        dve.wait_ge(band_in[0], 16 * (4 * b + g + 1))
                    dve.wait_ge(sc_ps, 16 * b + h + 1)
                    own_wait(dve, waited)
                    for i in range(NT):
                        last = nc.vector.tensor_tensor_reduce(
                            out=SS[:, h % 2, i, :], in0=SC[h % 2][:, i * S:(i + 1) * S],
                            in1=SK[0][g % 2][:, h % HG, i, :], scale=1.0, scalar=-3.0e38, op0=ALU.add, op1=ALU.max,
                            accum_out=mx[:, h % 2, i:i + 1])
                    last.then_inc(maxed, 1)
                    dve.wait_ge(maxed, 16 * b + h + 1)
                    nc.vector.tensor_scalar(nb[:, h % 2, :], mx[:, h % 2, :], -scale, None, ALU.mult).then_inc(negmax, 1)

                def norm(b, h):
                    dve.wait_ge(exped, 16 * b + h + 1)
                    chain.link(nc.vector.reciprocal(rs[:, h % 2, :], sm[:, h % 2, :]))
                    for i in range(NT):
                        last = nc.vector.tensor_scalar(PR[:, h % 2, i, :], PR[:, h % 2, i, :], rs[:, h % 2, i:i + 1],
                                                       None, ALU.mult)
                    last.then_inc(normed, 1)

                def attention(b):
                    for h in range(H):
                        if h + HG < H:
                            stage(b, h + HG)
                        maxima(b, h)
                        if h >= 1:
                            norm(b, h - 1)
                    norm(b, H - 1)
                    dve.wait_ge(y_ps, b + 1)
                    dve.wait_ge(xb, b + 1)
                    nc.vector.tensor_tensor(R[:].rearrange("p t n -> p (t n)"), FR1[:],
                                            XB[:].rearrange("p t n -> p (t n)"), ALU.add).then_inc(r_sb, 1)
                    dve.wait_ge(r_sb, b + 1)
                    layernorm_stats(nc, chain, R, st, mv, ve, var, LN_EPS)
                    dve.wait_ge(rstd_ok, b + 1)
                    layernorm_apply(nc, R, mv, rstd, X1).then_inc(x1_ok, 1)

                front(0)
                for h in range(HG):
                    stage(0, h)
                def step(b):
                    chain.start(LINKS * b)
                    attention(b)
                    front(b + 1)
                    for h in range(HG):
                        stage(b + 1, h)
                    x.vector(dve, b, chain)
                    assert chain.n == LINKS, (chain.n, LINKS)

                step(0)
                with dve.Fori(1, B - 1) as b:
                    step(b)
                chain.start(LINKS * (B - 1))
                attention(B - 1)
                x.vector(dve, B - 1, chain)

            @block.gpsimd
            def _(pool):
                nc.gpsimd.memset(neghalf[:], -0.5).then_inc(tp, 1)
                pool.wait_ge(tp, 1)
                pool.wait_ge(tv, 3)
                nc.gpsimd.tensor_tensor(rstd[:, 0:1], ve[:, 0:1], neghalf[:, 0:1], ALU.pow).then_inc(tp, 1)
                pool.wait_ge(tt, 3)

                def front(b):
                    pool.wait_ge(x_in, 16 * b + 16)
                    at_least(pool, r_sb, b)
                    nc.gpsimd.tensor_tensor(XB[:], XIN[:], broadcast_mid(row[:, 2, :], NT), ALU.add).then_inc(xb, 1)
                    pool.wait_ge(k_sb, b + 1)
                    at_least(pool, sc_ps, 16 * b)
                    for c in range(KC):
                        last = nc.gpsimd.tensor_tensor(kM[:, c * HC:(c + 1) * HC, :], broadcast_mid(kT[:, c, :], HC),
                                                       broadcast_last(headmask[:], S), ALU.mult)
                    last.then_inc(kM_sb, 1)

                front(0)
                def step(b):
                    pool.wait_ge(var, b + 1)
                    nc.gpsimd.tensor_tensor(rstd[:], ve[:], neghalf[:], ALU.pow).then_inc(rstd_ok, 1)
                    front(b + 1)
                    x.pool(pool, b, X1_READY(b))

                step(0)
                with pool.Fori(1, B - 1) as b:
                    step(b)
                pool.wait_ge(var, B)
                nc.gpsimd.tensor_tensor(rstd[:], ve[:], neghalf[:], ALU.pow).then_inc(rstd_ok, 1)
                x.pool(pool, B - 1, X1_READY(B - 1))
        al.end()

E8 = 8


def most_tiles(top):
    return (T * top + E8 * (P - 1)) // P


def experts_phase(nc, d, name, top, DF, func, normed):
    TT = T // P
    FC = DF // P
    MT = most_tiles(top)
    with ExitStack() as phase:
        al = Alloc(nc, phase, name)
        sb, sem = al.sb, al.sem
        ident = sb("ident", [P, P])
        before = sb("before", [P, P])
        ones = sb("ones", [P, P])
        iota = sb("iota", [P, E8 + MT])
        neghalf = sb("neghalf", [P, TT])
        X = sb("X", [P, TT, D])
        XN = sb("XN", [P, TT, D]) if normed else X
        xT = sb("xT", [P, 2, KC, P])
        wr = sb("wr", [P, KC, E8])
        br = sb("br", [P, E8])
        gb = sb("gb", [P, 2, D]) if normed else None
        LG = sb("LG", [P, TT, E8])
        V8 = sb("V8", [P, TT, E8])
        I8 = sb("I8", [P, TT, E8], U32)
        IF = sb("IF", [P, TT, E8])
        EX = sb("EX", [P, TT, E8])
        V2 = sb("V2", [P, TT])
        SE = sb("SE", [P, TT])
        G = sb("G", [P, top, TT])
        OH = [sb(f"OH{k}", [P, TT, E8]) for k in range(top)]
        OHS = sb("OHS", [P, TT, E8]) if top > 1 else OH[0]
        TP = sb("TP", [P, TT + 1, E8])
        NI = sb("NI", [P, E8], I32)
        NF = sb("NF", [P, E8])
        OFF = sb("OFF", [P, E8 + 1])
        PB = sb("PB", [P, TT, E8])
        SEL = sb("SEL", [P, TT, E8])
        PF = sb("PF", [P, top, TT])
        POS = sb("POS", [P, top, TT], U32)
        CMP = sb("CMP", [P, MT, E8 - 1])
        EF = sb("EF", [P, MT])
        EI = sb("EI", [P, MT], I32)
        NEW = sb("NEW", [P, MT], I32)
        NEF = sb("NEF", [P, MT])
        Z = sb("Z", [P, D])
        W1 = [sb(f"W1_{i}", [P, KC, DF]) for i in range(2)]
        W2 = [sb(f"W2_{i}", [P, FC, D]) for i in range(2)]
        B1 = [sb(f"B1_{i}", [P, FC]) for i in range(2)]
        B2 = [sb(f"B2_{i}", [P, D]) for i in range(2)]
        XS = [sb(f"XS{i}", [P, D]) for i in range(2)]
        XST = [sb(f"XST{i}", [P, KC, P]) for i in range(2)]
        HT = [sb(f"HT{i}", [P, FC, P]) for i in range(2)]
        YS = [sb(f"YS{i}", [P, D]) for i in range(2)]
        YG = sb("YG", [P, top, TT, D])
        st = sb("st", [P, TT, 6])
        mv = sb("mv", [P, TT, 2])
        ve = sb("ve", [P, TT])
        rstd = sb("rstd", [P, TT])
        OUT = XN if normed else sb("OUT", [P, TT, D])

        banks = [al.bank(f"ps{i}") for i in range(8)]
        psT = banks[0:2]
        psH = banks[2:6]
        psY = banks[6:8]
        psL = banks[2]
        psR, psC = banks[3], banks[4]

        xs = nc.dram_tensor(name + "sorted", (MT * P, D), F32, kind="Internal").ap()
        ys = nc.dram_tensor(name + "results", (MT * P, D), F32, kind="Internal").ap()

        consts, x_in, zeros_out = sem("consts"), sem("x_in"), sem("zeros_out")
        ez, eh = sem("zero_row"), sem("neghalf")
        rt_ps, rt_sb = sem("rt_ps"), sem("rt_sb")
        lg_ps, lg, ex, ranks = sem("lg_ps"), sem("lg"), sem("ex"), sem("ranks")
        oh, routed, gated, scattered = sem("oh"), sem("routed"), sem("gated"), sem("scattered")
        xn, var, rstd_ok = sem("xn"), sem("var"), sem("rstd")
        w1_in = [sem(f"w1_in{i}") for i in range(2)]
        w2_in = [sem(f"w2_in{i}") for i in range(2)]
        xsT_ps, xsT_sb = sem("xsT_ps"), sem("xsT_sb")
        h_ps, h_sb, y_ps, y_sb = sem("h_ps"), sem("h_sb"), sem("y_ps"), sem("y_sb")
        y_out = [sem(f"y_out{i}") for i in range(2)]
        gathered = [sem(f"gathered{q}") for q in range(4)]
        out_ok, stored = sem("out"), sem("stored")
        dv, sp_waited, pool_waited = sem("dve_chain"), sem("sp_waited"), sem("pool_waited")
        NB = FC // 4
        W1_PARTS, W2_PARTS = 3, 2

        with nc.Block() as block:

            @block.sync
            def _(sp):
                for dst, src in ((X[:], d["x"].rearrange("(t p) n -> p t n", p=P)),):
                    sp.dma_start(dst, src).then_inc(x_in, 16)
                loads = [(ident[:], d["ident"]), (before[:], d["before"]), (iota[:], d["iota"][:, 0:E8 + MT]),
                         (wr[:], d["Wr"].rearrange("(k p) n -> p k n", p=P)),
                         (br[:], d["br"].partition_broadcast(P))]
                loads += [(gb[:], d["gb"].partition_broadcast(P))] if normed else [(V8[:, 0, :], d["iota"][:, 0:E8])]
                for dst, src in loads:
                    sp.dma_start(dst, src).then_inc(consts, 16)
                sp.wait_ge(ez, 1)
                sp.dma_start(xs.rearrange("(m p) n -> p m n", p=P), broadcast_mid(Z[:], MT)).then_inc(zeros_out, 16)
                sp.wait_ge(routed, 1)
                sp.wait_ge(scattered, 16 * TT * top)

                def tile(n, i):
                    e = sp.value_load(EI[0:1, bass.ds(n, 1)], min_val=0, max_val=E8 - 1)
                    fresh = sp.value_load(NEW[0:1, bass.ds(n, 1)], min_val=0, max_val=1)
                    at_least(sp, h_ps, NB * (n - 1))
                    at_least(sp, h_sb, NB * (n - 1))
                    own_wait(sp, sp_waited)
                    sp.dma_start(XS[i][:], xs.rearrange("(m p) n -> m p n", p=P)[n]).then_inc(w1_in[i], 16)
                    sp.dma_start(W1[i][:], d["W1"][e].rearrange("(k p) n -> p k n", p=P), cond=fresh,
                                 cond_hint=True).then_inc(w1_in[i], 16)
                    sp.dma_start(B1[i][:], d["b1"][e]).then_inc(w1_in[i], 16)

                tile(0, 0)
                tile(1, 1)
                with sp.Fori(1, MT // 2) as m:
                    for i in range(2):
                        tile(2 * m + i, i)
                if MT % 2:
                    tile(MT - 1, 0)
                for q in range(4):
                    sp.wait_ge(out_ok, TT // 4 * (q + 1))
                    ts = slice(TT // 4 * q, TT // 4 * (q + 1))
                    sp.dma_start(d["out"].rearrange("(t p) n -> p t n", p=P)[:, ts, :], OUT[:, ts, :]).then_inc(stored, 16)
                sp.wait_ge(stored, 64)

            @block.tensor
            def _(pe):
                pe.wait_ge(consts, 96)
                pe.wait_ge(x_in, 16)
                for t in range(TT):
                    if normed:
                        pe.wait_ge(xn, t + 1)
                    if t >= 2:
                        pe.wait_ge(rt_sb, t - 1)
                    for k in range(KC):
                        last = nc.tensor.transpose(psT[t % 2][:, k * P:(k + 1) * P], XN[:, t, k * P:(k + 1) * P], ident[:])
                    last.then_inc(rt_ps, 1)
                    pe.wait_ge(rt_sb, t + 1)
                    for k in range(KC):
                        last = nc.tensor.matmul(psL[:, t * E8:(t + 1) * E8], xT[:, t % 2, k, :], wr[:, k, :],
                                                start=k == 0, stop=k == KC - 1)
                last.then_inc(lg_ps, 1)
                pe.wait_ge(oh, 1)
                flat = OHS[:].rearrange("p t e -> p (t e)")
                nc.tensor.matmul(psR[:, 0:TT * E8], before[:], flat, start=True, stop=True)
                nc.tensor.matmul(psC[:, 0:TT * E8], ones[:], flat, start=True, stop=True).then_inc(ranks, 1)

                def up(n, i, j):
                    pe.wait_ge(w1_in[i], 16 * W1_PARTS * (j + 1))
                    at_least(pe, xsT_sb, n - 1)
                    for k in range(KC):
                        last = nc.tensor.transpose(psT[i][:, k * P:(k + 1) * P], XS[i][:, k * P:(k + 1) * P], ident[:])
                    last.then_inc(xsT_ps, 1)
                    pe.wait_ge(xsT_sb, n + 1)
                    for f in range(FC):
                        bank = psH[(i * NB + f // 4) % 4]
                        if f % 4 == 0:
                            at_least(pe, h_sb, (n - 4 // NB + 1) * NB if NB * 2 > 4 else NB * (n - 1))
                        for k in range(KC):
                            last = nc.tensor.matmul(bank[:, (f % 4) * P:(f % 4 + 1) * P], W1[i][:, k, f * P:(f + 1) * P],
                                                    XST[i][:, k, :], start=k == 0, stop=k == KC - 1)
                        if f % 4 == 3:
                            last.then_inc(h_ps, 1)

                def down(n, i, j):
                    pe.wait_ge(h_sb, NB * (n + 1))
                    pe.wait_ge(w2_in[i], 16 * W2_PARTS * (j + 1))
                    at_least(pe, y_sb, n - 1)
                    for f in range(FC):
                        last = nc.tensor.matmul(psY[i][:, 0:D], HT[i][:, f, :], W2[i][:, f, :],
                                                start=f == 0, stop=f == FC - 1)
                    last.then_inc(y_ps, 1)

                up(0, 0, 0)
                up(1, 1, 0)
                down(0, 0, 0)
                with pe.Fori(1, MT // 2) as m:
                    up(2 * m, 0, m)
                    down(2 * m - 1, 1, m - 1)
                    up(2 * m + 1, 1, m)
                    down(2 * m, 0, m)
                if MT % 2:
                    up(MT - 1, 0, MT // 2)
                    down(MT - 2, 1, MT // 2 - 1)
                    down(MT - 1, 0, MT // 2)
                else:
                    down(MT - 1, 1, MT // 2 - 1)

            @block.scalar
            def _(act):
                for t in range(TT):
                    act.wait_ge(rt_ps, t + 1)
                    nc.scalar.activation(xT[:, t % 2, :, :].rearrange("p k n -> p (k n)"), psT[t % 2][:, 0:D],
                                         ACT.Copy).then_inc(rt_sb, 1)
                act.wait_ge(lg, 2)
                nc.scalar.activation(EX[:].rearrange("p t e -> p (t e)"), EX[:].rearrange("p t e -> p (t e)"),
                                     ACT.Exp).then_inc(ex, 1)
                nc.scalar.activation(V2[:], V2[:], ACT.Exp).then_inc(ex, 1)

                def up(n, i, j):
                    act.wait_ge(xsT_ps, n + 1)
                    nc.scalar.activation(XST[i][:].rearrange("p k n -> p (k n)"), psT[i][:, 0:D],
                                         ACT.Copy).then_inc(xsT_sb, 1)
                    act.wait_ge(w1_in[i], 16 * W1_PARTS * (j + 1))
                    at_least(act, y_ps, n - 1)
                    for f in range(FC):
                        bank = psH[(i * NB + f // 4) % 4]
                        if f % 4 == 0:
                            act.wait_ge(h_ps, NB * n + f // 4 + 1)
                        last = nc.scalar.activation(HT[i][:, f, :], bank[:, (f % 4) * P:(f % 4 + 1) * P], func,
                                                    bias=B1[i][:, f:f + 1])
                        if f % 4 == 3:
                            last.then_inc(h_sb, 1)

                up(0, 0, 0)
                up(1, 1, 0)
                with act.Fori(1, MT // 2) as m:
                    up(2 * m, 0, m)
                    up(2 * m + 1, 1, m)
                if MT % 2:
                    up(MT - 1, 0, MT // 2)

            @block.vector
            def _(dve):
                chain = Chain(dve, dv)
                nc.vector.memset(Z[:], 0.0).then_inc(ez, 1)
                nc.vector.memset(ones[:], 1.0)
                chain.link(nc.vector.memset(TP[:, 0, :], 0.0))
                nc.vector.memset(OFF[:, 0:1], 0.0)
                dve.wait_ge(consts, 96)
                dve.wait_ge(x_in, 16)
                if normed:
                    for t in range(TT):
                        last = nc.vector.bn_stats(st[:, t, :], X[:, t, :])
                    chain.link(last)
                    for t in range(TT):
                        last = nc.vector.bn_aggr(mv[:, t, :], st[:, t, :])
                    chain.link(last)
                    nc.vector.tensor_scalar(ve[:], mv[:, :, 1], LN_EPS, None, ALU.add).then_inc(var, 1)
                    dve.wait_ge(rstd_ok, 1)
                    for t in range(TT):
                        chain.link(nc.vector.tensor_scalar(XN[:, t, :], X[:, t, :], mv[:, t, 0:1], rstd[:, t:t + 1],
                                                           ALU.subtract, ALU.mult))
                        chain.link(nc.vector.tensor_tensor(XN[:, t, :], XN[:, t, :], gb[:, 0, :], ALU.mult))
                        nc.vector.tensor_tensor(XN[:, t, :], XN[:, t, :], gb[:, 1, :], ALU.add).then_inc(xn, 1)
                dve.wait_ge(lg_ps, 1)
                chain.link(nc.vector.tensor_tensor(LG[:], psL[:, 0:TT * E8].rearrange("p (t e) -> p t e", e=E8),
                                                   broadcast_mid(br[:], TT), ALU.add))
                for t in range(TT):
                    last = nc.vector.max(V8[:, t, :], LG[:, t, :])
                chain.link(last)
                for t in range(TT):
                    last = nc.vector.max_index(I8[:, t, :], V8[:, t, :], LG[:, t, :])
                chain.link(last)
                nc.vector.tensor_tensor(EX[:], LG[:], broadcast_last(V8[:, :, 0], E8), ALU.subtract).then_inc(lg, 1)
                nc.vector.tensor_tensor(V2[:], V8[:, :, 1], V8[:, :, 0], ALU.subtract).then_inc(lg, 1)
                chain.link(nc.vector.tensor_copy(IF[:], I8[:]))
                for k in range(top):
                    last = nc.vector.tensor_tensor(OH[k][:], broadcast_mid(iota[:, 0:E8], TT),
                                                   broadcast_last(IF[:, :, k], E8), ALU.is_equal)
                if top > 1:
                    chain.link(last)
                    last = nc.vector.tensor_tensor(OHS[:], OH[0][:], OH[1][:], ALU.add)
                last.then_inc(oh, 1)
                dve.wait_ge(ex, 2)
                chain.link(nc.vector.tensor_reduce(SE[:], EX[:], AXX, ALU.add))
                chain.link(nc.vector.reciprocal(G[:, 0, :], SE[:]))
                if top > 1:
                    chain.link(nc.vector.tensor_tensor(G[:, 1, :], G[:, 0, :], V2[:], ALU.mult))
                    chain.link(nc.vector.scalar_tensor_tensor(out=SE[:], in0=G[:, 0, :], scalar=1e-8, in1=G[:, 1, :],
                                                              op0=ALU.add, op1=ALU.add))
                    chain.link(nc.vector.reciprocal(V2[:], SE[:]))
                    chain.link(nc.vector.tensor_tensor(G[:], G[:], broadcast_mid(V2[:], top), ALU.mult))
                dve.wait_ge(ranks, 1)
                for t in range(TT):
                    chain.link(nc.vector.tensor_tensor(TP[:, t + 1, :], TP[:, t, :], psC[:, t * E8:(t + 1) * E8], ALU.add))
                chain.link(nc.vector.tensor_scalar(NF[:], TP[:, TT, :], float(P - 1), None, ALU.add))
                chain.link(nc.vector.tensor_copy(NI[:], NF[:]))
                shift = P.bit_length() - 1
                chain.link(nc.vector.tensor_scalar(NI[:], NI[:], shift, shift, ALU.arith_shift_right,
                                                   ALU.logical_shift_left))
                chain.link(nc.vector.tensor_copy(NF[:], NI[:]))
                for e in range(E8):
                    chain.link(nc.vector.tensor_tensor(OFF[:, e + 1:e + 2], OFF[:, e:e + 1], NF[:, e:e + 1], ALU.add))
                chain.link(nc.vector.tensor_tensor(PB[:], TP[:, 0:TT, :],
                                                   psR[:, 0:TT * E8].rearrange("p (t e) -> p t e", e=E8), ALU.add))
                chain.link(nc.vector.tensor_tensor(PB[:], PB[:], broadcast_mid(OFF[:, 0:E8], TT), ALU.add))
                for k in range(top):
                    chain.link(nc.vector.tensor_tensor(SEL[:], PB[:], OH[k][:], ALU.mult))
                    chain.link(nc.vector.tensor_reduce(PF[:, k, :], SEL[:], AXX, ALU.add))
                nc.vector.tensor_copy(POS[:], PF[:])
                chain.link(nc.vector.tensor_tensor(CMP[:], broadcast_mid(OFF[:, 1:E8], MT),
                                                   broadcast_last(iota[:, E8:E8 + MT], E8 - 1), ALU.is_le))
                chain.link(nc.vector.tensor_reduce(EF[:], CMP[:], AXX, ALU.add))
                nc.vector.tensor_copy(EI[:], EF[:])
                nc.vector.memset(NEF[:, 0:2], 1.0)
                chain.link(nc.vector.tensor_tensor(NEF[:, 2:MT], EF[:, 2:MT], EF[:, 0:MT - 2], ALU.not_equal))
                nc.vector.tensor_copy(NEW[:], NEF[:]).then_inc(routed, 1)

                def down(n, i, j):
                    dve.wait_ge(y_ps, n + 1)
                    dve.wait_ge(w2_in[i], 16 * W2_PARTS * (j + 1))
                    at_least(dve, y_out[i], 16 * j)
                    nc.vector.tensor_tensor(YS[i][:], psY[i][:, 0:D], B2[i][:], ALU.add).then_inc(y_sb, 1)

                if normed:
                    chain.link(nc.vector.tensor_scalar(X[:], X[:], 2.0, None, ALU.mult))

                down(0, 0, 0)
                down(1, 1, 0)
                with dve.Fori(1, MT // 2) as m:
                    down(2 * m, 0, m)
                    down(2 * m + 1, 1, m)
                if MT % 2:
                    down(MT - 1, 0, MT // 2)
                for t in range(TT):
                    dve.wait_ge(gathered[t // 4], 16 * top * 4)
                    for k in range(top):
                        chain.link(nc.vector.scalar_tensor_tensor(out=X[:, t, :], in0=YG[:, k, t, :],
                                                                  scalar=G[:, k, t:t + 1], in1=X[:, t, :],
                                                                  op0=ALU.mult, op1=ALU.add))
                    last = nc.vector.bn_stats(st[:, t, :], X[:, t, :])
                chain.link(last)
                for t in range(TT):
                    last = nc.vector.bn_aggr(mv[:, t, :], st[:, t, :])
                chain.link(last)
                nc.vector.tensor_scalar(ve[:], mv[:, :, 1], LN_EPS, None, ALU.add).then_inc(var, 1)
                dve.wait_ge(rstd_ok, 1 + normed)
                for t in range(TT):
                    nc.vector.tensor_scalar(OUT[:, t, :], X[:, t, :], mv[:, t, 0:1], rstd[:, t:t + 1],
                                            ALU.subtract, ALU.mult).then_inc(out_ok, 1)

            @block.gpsimd
            def _(pool):
                nc.gpsimd.memset(neghalf[:], -0.5).then_inc(eh, 1)
                pool.wait_ge(eh, 1)
                if normed:
                    pool.wait_ge(var, 1)
                    nc.gpsimd.tensor_tensor(rstd[:], ve[:], neghalf[:], ALU.pow).then_inc(rstd_ok, 1)
                    pool.wait_ge(xn, TT)
                pool.wait_ge(routed, 1)
                pool.wait_ge(zeros_out, 16)
                pool.wait_ge(x_in, 16)
                for t in range(TT):
                    for k in range(top):
                        nc.gpsimd.indirect_dma_start(xs, bass.IndirectOffsetOnAxis(POS[:, k, t:t + 1], 0),
                                                     XN[:, t, :], None).then_inc(scattered, 16)

                def second(n, i):
                    e = pool.value_load(EI[0:1, bass.ds(n, 1)], min_val=0, max_val=E8 - 1)
                    fresh = pool.value_load(NEW[0:1, bass.ds(n, 1)], min_val=0, max_val=1)
                    at_least(pool, y_ps, n - 1)
                    at_least(pool, y_sb, n - 1)
                    own_wait(pool, pool_waited)
                    pool.dma_start(W2[i][:], d["W2"][e].rearrange("(k p) n -> p k n", p=P), cond=fresh,
                                   cond_hint=True).then_inc(w2_in[i], 16)
                    pool.dma_start(B2[i][:], d["b2"][e].partition_broadcast(P)).then_inc(w2_in[i], 16)

                def store(n, i):
                    pool.wait_ge(y_sb, n + 1)
                    own_wait(pool, pool_waited)
                    pool.dma_start(ys.rearrange("(m p) n -> m p n", p=P)[n], YS[i][:]).then_inc(y_out[i], 16)

                second(0, 0)
                second(1, 1)
                store(0, 0)
                with pool.Fori(1, MT // 2) as m:
                    second(2 * m, 0)
                    store(2 * m - 1, 1)
                    second(2 * m + 1, 1)
                    store(2 * m, 0)
                if MT % 2:
                    second(MT - 1, 0)
                    store(MT - 2, 1)
                    store(MT - 1, 0)
                else:
                    store(MT - 1, 1)
                pool.wait_ge(y_out[0], 16 * ((MT + 1) // 2))
                pool.wait_ge(y_out[1], 16 * (MT // 2))
                for t in range(TT):
                    for k in range(top):
                        nc.gpsimd.indirect_dma_start(YG[:, k, t, :], None, ys,
                                                     bass.IndirectOffsetOnAxis(POS[:, k, t:t + 1], 0)).then_inc(gathered[t // 4], 16)
                pool.wait_ge(var, 1 + normed)
                nc.gpsimd.tensor_tensor(rstd[:], ve[:], neghalf[:], ALU.pow).then_inc(rstd_ok, 1)
        al.end()

DH = 64
PM = 16
CH = H * DH // P
INNER = H * DH
RMS_EPS = 1e-6


def segment_attention_phase(nc, d):
    with ExitStack() as phase:
        al = Alloc(nc, phase, "c_")
        sb, sem = al.sb, al.sem
        scale = float(DH) ** -0.5
        NK = PM + P

        FR0, FR1, QK, RT, SC0, SC1, PTB, PO = [al.bank(n) for n in
                                               ("FR0", "FR1", "QK", "RT", "SC0", "SC1", "PTB", "PO")]
        SC, QKB, RTB = [SC0, SC1], [QK, SC0], [RT, SC1]
        ident = sb("ident", [P, P])
        headmask = sb("headmask", [P, HC])
        col = sb("col", [P, 6])
        row = sb("row", [P, 3, D])
        cs = sb("cs", [P, 2, 2, S])
        rot = sb("rot", [P, P])
        mask = sb("mask", [P, NK])
        neghalf = sb("neghalf", [P, NT])
        wqkv = sb("wqkv", [P, KC, 3 * INNER])
        wout = sb("wout", [P, CH, D])
        XIN = sb("XIN", [P, NT, D])
        XB = sb("XB", [P, NT, D])
        XR = sb("XR", [P, NT, D])
        xT = sb("xT", [P, KC, S])
        raw, t1, t2 = [[sb(f"{n}{i}", [P, 2, S]) for i in range(2)] for n in ("raw", "t1", "t2")]
        qT = sb("qT", [P, CH, S])
        kP = sb("kP", [P, CH, 2, NT, NK])
        v = sb("v", [P, NT, INNER])
        vpm = sb("vpm", [P, 2, 8 * DH])
        SM = sb("SM", [P, 2, NK])
        PR = sb("PR", [P, 2, P])
        PP = sb("PP", [P, 2, 8 * PM])
        mx = sb("mx", [P, 2])
        nb = sb("nb", [P, 2])
        sm = sb("sm", [P, 2])
        rs = sb("rs", [P, 2])
        PTr = sb("PTr", [P, 8, P])
        PPT = sb("PPT", [P, 2, P])
        OT = sb("OT", [P, CH, S])
        R = sb("R", [P, NT, D])
        sq = sb("sq", [P, NT, D])
        ss = sb("ss", [P, NT])
        ms = sb("ms", [P, NT])
        rr = sb("rr", [P, NT])
        st = sb("st", [P, NT, 6])
        mv = sb("mv", [P, NT, 2])
        ve = sb("ve", [P, NT])
        rstd = sb("rstd", [P, NT])
        X1 = sb("X1", [P, NT, D])
        xPT = sb("xPT", [CK, H, S])
        a = {"ident": ident, "headmask": headmask, "neghalf": neghalf, "X1": X1,
             "ctxT": d["ctxT"], "x2_out": d["x5"],
             "xbq": col[:, 2:4], "xbk": col[:, 4:6], "xbv": row[:, 1, :], "xbo": row[:, 2, :]}
        x = Cross(al, a, d["L1_xattn"], False, (FR0, FR1, [QK, RT, SC0, SC1], [PTB, SC1], PO),
                  (xT, OT[:, 0:NG, :], R, xPT))

        consts, zeroed, hv = sem("consts"), sem("zeroed"), sem("neghalf")
        x_in = sem("x_in")
        ms_ok, rr_ok, xr, xr_ps, xT_sb = sem("ms"), sem("rr"), sem("xr"), sem("xr_ps"), sem("xT_sb")
        qk_ps, raw_sb, t1_sb, rot_ps, t2_sb, q_sb, k_sb = (sem("qk_ps"), sem("raw_sb"), sem("t1_sb"), sem("rot_ps"),
                                                            sem("t2_sb"), sem("q_sb"), sem("k_sb"))
        v_ps, v_sb, xb = sem("v_ps"), sem("v_sb"), sem("xb")
        sc_ps, maxed, negmax, exped, normed = sem("sc_ps"), sem("maxed"), sem("negmax"), sem("exped"), sem("normed")
        pT_ps, pT_sb, pp_ps, pp_sb, o_ps, o_sb = (sem("pT_ps"), sem("pT_sb"), sem("pp_ps"), sem("pp_sb"),
                                                  sem("o_ps"), sem("o_sb"))
        y_ps, r_sb, var, rstd_ok, x1_ok = sem("y_ps"), sem("r_sb"), sem("var"), sem("rstd"), sem("x1")
        dv, waited, sp_waited = sem("dve_chain"), sem("dve_waited"), sem("sp_waited")
        U = NT * H
        order = [(w, 8 * o + h) for o in range(2) for w in range(NT) for h in range(8)]
        ATTN_LINKS = U + 2 + 1
        LINKS = ATTN_LINKS + x.VECTOR_LINKS
        CONSTS = 13
        X1_READY = lambda b: (x1_ok, b + 1)

        with nc.Block() as block:

            @block.sync
            def _(sp):
                for dst, src in ((ident[:], d["ident"]), (headmask[:], d["headmask"]), (col[:], d["L1_col"]),
                                 (row[:], d["L1_row"].partition_broadcast(P)), (cs[:], d["cossin"]),
                                 (rot[:], d["rot"]), (mask[:], d["mask"]),
                                 (wqkv[:], d["w_qkv"].rearrange("(k p) n -> p k n", p=P)),
                                 (wout[:], d["w_out"].rearrange("(k p) n -> p k n", p=P))):
                    sp.dma_start(dst, src).then_inc(consts, 16)
                sp.wait_ge(zeroed, 2)
                pmk = d["pm_kT"].rearrange("(c u n) k -> u n c k", u=2, n=DH)
                for u in range(2):
                    for w in range(NT):
                        sp.dma_start(kP[u * DH:(u + 1) * DH, :, u, w, 0:PM], pmk[u]).then_inc(consts, 16)
                for h in range(H):
                    sp.dma_start(vpm[(h % 8) * PM:(h % 8 + 1) * PM, h // 8, (h % 8) * DH:(h % 8 + 1) * DH],
                                 d["pm_v"][h]).then_inc(consts, 16)
                x.load_weights(sp)

                def load_x(b):
                    at_least(sp, xb, b)
                    at_least(sp, xr, b)
                    own_wait(sp, sp_waited)
                    sp.dma_start(XIN[:], d["x"][b].rearrange("(t p) n -> p t n", p=P)).then_inc(x_in, 16)

                load_x(0)
                def step(b):
                    load_x(b + 1)
                    x.load_ctx(sp, b)
                    x.store(sp, b)

                step(0)
                with sp.Fori(1, B - 1) as b:
                    step(b)
                x.load_ctx(sp, B - 1)
                x.store(sp, B - 1)
                sp.wait_ge(x.stored, 16 * B)

            ALL_CONSTS = 16 * (9 + 4 + H)

            @block.tensor
            def _(pe):
                pe.wait_ge(consts, ALL_CONSTS)
                pe.wait_ge(x.weights, x.WEIGHTS)

                def front(b):
                    pe.wait_ge(xr, b + 1)
                    at_least(pe, x.kv_sb, b)
                    for t in range(NT):
                        for k in range(KC):
                            last = nc.tensor.transpose(FR0[:, k * S + t * P:k * S + (t + 1) * P],
                                                       XR[:, t, k * P:(k + 1) * P], ident[:])
                    last.then_inc(xr_ps, 1)
                    pe.wait_ge(xT_sb, b + 1)

                    def rotate(c):
                        pe.wait_ge(raw_sb, CH * b + c + 1)
                        if c >= 2:
                            pe.wait_ge(t2_sb, CH * b + c - 1)
                        nc.tensor.matmul(RTB[c % 2][:], rot[:], raw[c % 2][:].rearrange("p a s -> p (a s)"),
                                         start=True, stop=True).then_inc(rot_ps, 1)

                    for c in range(CH):
                        if c >= 2:
                            pe.wait_ge(raw_sb, CH * b + c - 1)
                        for n in range(2):
                            for k in range(KC):
                                last = nc.tensor.matmul(QKB[c % 2][:, n * S:(n + 1) * S],
                                                        wqkv[:, k, n * INNER + c * P:n * INNER + (c + 1) * P],
                                                        xT[:, k, :], start=k == 0, stop=k == KC - 1)
                        last.then_inc(qk_ps, 1)
                        if c % 2 == 0:
                            n = c // 2
                            if n:
                                pe.wait_ge(v_sb, 4 * b + n)
                            else:
                                at_least(pe, x.r_sb, b)
                            for k in range(KC):
                                last = nc.tensor.matmul(FR1[:], xT[:, k, (n // 2) * P:(n // 2 + 1) * P],
                                                        wqkv[:, k, 2 * INNER + (n % 2) * 512:2 * INNER + (n % 2 + 1) * 512],
                                                        start=k == 0, stop=k == KC - 1)
                            last.then_inc(v_ps, 1)
                        if c:
                            rotate(c - 1)
                    rotate(CH - 1)

                def scores(b, n):
                    w, h = order[n]
                    if n == 0:
                        pe.wait_ge(q_sb, CH * b + CH)
                        pe.wait_ge(k_sb, CH * b + CH)
                    if n >= 2:
                        pe.wait_ge(maxed, U * b + n - 1)
                    nc.tensor.matmul(SC[n % 2][:, 0:NK], qT[:, h // 2, w * P:(w + 1) * P], kP[:, h // 2, h % 2, w, :],
                                     start=True, stop=True).then_inc(sc_ps, 1)

                def transposes(b, n):
                    pe.wait_ge(normed, U * b + n + 1)
                    at_least(pe, pT_sb, U * b + n)
                    if n % 8 == 7:
                        if n >= 8:
                            pe.wait_ge(pp_sb, U // 8 * b + n // 8)
                        nc.tensor.transpose(PTB[:, P:2 * P], PP[:, (n // 8) % 2, :], ident[:]).then_inc(pp_ps, 1)
                    nc.tensor.transpose(PTB[:, 0:P], PR[:, n % 2, :], ident[:]).then_inc(pT_ps, 1)

                def outputs(b, m):
                    pe.wait_ge(pT_sb, U * b + 8 * m + 8)
                    pe.wait_ge(pp_sb, U // 8 * b + m + 1)
                    if m == 0:
                        pe.wait_ge(v_sb, 4 * b + 4)
                    at_least(pe, o_sb, U // 8 * b + m)
                    for j in range(8):
                        w, h = order[8 * m + j]
                        dst = PO[(h % 2) * DH:(h % 2 + 1) * DH, (j // 2) * P:(j // 2 + 1) * P]
                        nc.tensor.matmul(dst, v[:, w, h * DH:(h + 1) * DH], PTr[:, j, :], start=True, stop=False)
                        last = nc.tensor.matmul(dst, vpm[:, h // 8, (h % 8) * DH:(h % 8 + 1) * DH], PPT[:, m % 2, :],
                                                start=False, stop=True)
                    last.then_inc(o_ps, 1)

                def attention(b):
                    scores(b, 0)
                    for n in range(1, U + 1):
                        if n < U:
                            scores(b, n)
                        transposes(b, n - 1)
                        if n % 8 == 0:
                            outputs(b, n // 8 - 1)
                    pe.wait_ge(o_sb, U // 8 * (b + 1))
                    for t in range(NT):
                        for c in range(CH):
                            last = nc.tensor.matmul(FR1[:, t * D:(t + 1) * D], OT[:, c, t * P:(t + 1) * P],
                                                    wout[:, c, :], start=c == 0, stop=c == CH - 1)
                    last.then_inc(y_ps, 1)

                def banks_free(b):
                    def wait(pe):
                        pe.wait_ge(r_sb, b + 1)
                    return wait

                def step(b):
                    front(b)
                    attention(b)
                    x.tensor(pe, b, X1_READY(b), banks_free(b))

                step(0)
                with pe.Fori(1, B) as b:
                    step(b)
            @block.scalar
            def _(act):
                act.wait_ge(consts, ALL_CONSTS)
                def step(b):
                    act.wait_ge(xr_ps, b + 1)
                    for k in range(KC):
                        last = nc.scalar.activation(xT[:, k, :], FR0[:, k * S:(k + 1) * S], ACT.Copy,
                                                    scale=col[:, k:k + 1])
                    last.then_inc(xT_sb, 1)
                    for c in range(CH):
                        act.wait_ge(qk_ps, CH * b + c + 1)
                        if c >= 2:
                            act.wait_ge(rot_ps, CH * b + c - 1)
                            act.wait_ge(t1_sb, CH * b + c - 1)
                        nc.scalar.activation(raw[c % 2][:].rearrange("p a s -> p (a s)"), QKB[c % 2][:],
                                             ACT.Copy).then_inc(raw_sb, 1)
                        if c % 2 == 0:
                            n = c // 2
                            act.wait_ge(v_ps, 4 * b + n + 1)
                            nc.scalar.activation(v[:, n // 2, (n % 2) * 512:(n % 2 + 1) * 512], FR1[:],
                                                 ACT.Copy).then_inc(v_sb, 1)

                    def exps(n):
                        act.wait_ge(negmax, U * b + n + 1)
                        nc.scalar.activation(SM[:, n % 2, :], SM[:, n % 2, :], ACT.Exp, bias=nb[:, n % 2:n % 2 + 1],
                                             scale=scale, accum_out=sm[:, n % 2:n % 2 + 1]).then_inc(exped, 1)

                    def copy_pT(n):
                        act.wait_ge(pT_ps, U * b + n + 1)
                        if n >= 8 and n % 8 == 0:
                            act.wait_ge(o_ps, U // 8 * b + n // 8)
                        if n % 8 == 7:
                            nc.scalar.activation(PPT[:, (n // 8) % 2, :], PTB[:, P:2 * P], ACT.Copy).then_inc(pp_sb, 1)
                        nc.scalar.activation(PTr[:, n % 8, :], PTB[:, 0:P], ACT.Copy).then_inc(pT_sb, 1)

                    def copy_o(m):
                        act.wait_ge(o_ps, U // 8 * b + m + 1)
                        w, h = order[8 * m]
                        nc.scalar.activation(OT[:, h // 2:h // 2 + 4, w * P:(w + 1) * P],
                                             PO[:].rearrange("p (c s) -> p c s", c=4), ACT.Copy).then_inc(o_sb, 1)

                    exps(0)
                    for n in range(1, U + 1):
                        if n < U:
                            exps(n)
                        copy_pT(n - 1)
                        if n % 8 == 2 and n > 8:
                            copy_o(n // 8 - 1)
                    copy_o(U // 8 - 1)
                    x.scalar(act, b)

                step(0)
                with act.Fori(1, B) as b:
                    step(b)
            @block.vector
            def _(dve):
                chain = Chain(dve, dv, waited)
                nc.vector.memset(kP[:], 0.0).then_inc(zeroed, 1)
                nc.vector.memset(vpm[:], 0.0).then_inc(zeroed, 1)
                nc.vector.memset(x.wo[:], 0.0).then_inc(x.zeroed, 1)
                nc.vector.memset(x.v[:], 0.0).then_inc(x.zeroed, 1)
                dve.wait_ge(consts, ALL_CONSTS)
                def step(b):
                    chain.start(LINKS * b)
                    dve.wait_ge(x_in, 16 * b + 16)
                    own_wait(dve, waited)
                    for t in range(NT):
                        last = nc.vector.tensor_tensor_reduce(out=sq[:, t, :], in0=XIN[:, t, :], in1=XIN[:, t, :],
                                                              scale=1.0, scalar=0.0, op0=ALU.mult, op1=ALU.add,
                                                              accum_out=ss[:, t:t + 1])
                    chain.link(last)
                    nc.vector.tensor_scalar(ms[:], ss[:], 1.0 / D, RMS_EPS, ALU.mult, ALU.add).then_inc(ms_ok, 1)
                    dve.wait_ge(rr_ok, b + 1)
                    for t in range(NT):
                        last = nc.vector.tensor_scalar(XR[:, t, :], XIN[:, t, :], rr[:, t:t + 1], None, ALU.mult)
                    last.then_inc(xr, 1)
                    for c in range(CH):
                        if c >= 2:
                            dve.wait_ge(q_sb, CH * b + c - 1)
                        dve.wait_ge(rot_ps, CH * b + c + 1)
                        nc.vector.tensor_tensor(t2[c % 2][:].rearrange("p a s -> p (a s)"), RTB[c % 2][:],
                                                cs[:, 1, :, :].rearrange("p a s -> p (a s)"), ALU.mult).then_inc(t2_sb, 1)
                        dve.wait_ge(t2_sb, CH * b + c + 1)
                        dve.wait_ge(t1_sb, CH * b + c + 1)
                        for u in range(2):
                            r = slice(u * DH, (u + 1) * DH)
                            last = nc.vector.tensor_tensor(kP[r, c, u, :, PM:NK],
                                                           t1[c % 2][r, 1, :].rearrange("p (w s) -> p w s", w=NT),
                                                           t2[c % 2][r, 1, :].rearrange("p (w s) -> p w s", w=NT), ALU.add)
                        last.then_inc(k_sb, 1)

                    def maxima(n):
                        dve.wait_ge(sc_ps, U * b + n + 1)
                        own_wait(dve, waited)
                        nc.vector.tensor_tensor_reduce(out=SM[:, n % 2, :], in0=SC[n % 2][:, 0:NK], in1=mask[:],
                                                       scale=1.0, scalar=-3.0e38, op0=ALU.add, op1=ALU.max,
                                                       accum_out=mx[:, n % 2:n % 2 + 1]).then_inc(maxed, 1)
                        dve.wait_ge(maxed, U * b + n + 1)
                        nc.vector.tensor_scalar(nb[:, n % 2:n % 2 + 1], mx[:, n % 2:n % 2 + 1], -scale, None,
                                                ALU.mult).then_inc(negmax, 1)

                    def norm(n):
                        dve.wait_ge(exped, U * b + n + 1)
                        chain.link(nc.vector.reciprocal(rs[:, n % 2:n % 2 + 1], sm[:, n % 2:n % 2 + 1]))
                        if n >= 2:
                            dve.wait_ge(pT_ps, U * b + n - 1)
                        if n % 8 == 0 and n >= 16:
                            dve.wait_ge(pp_ps, U // 8 * b + n // 8 - 1)
                        nc.vector.tensor_scalar(PP[:, (n // 8) % 2, (n % 8) * PM:(n % 8 + 1) * PM], SM[:, n % 2, 0:PM],
                                                rs[:, n % 2:n % 2 + 1], None, ALU.mult)
                        nc.vector.tensor_scalar(PR[:, n % 2, :], SM[:, n % 2, PM:NK], rs[:, n % 2:n % 2 + 1],
                                                None, ALU.mult).then_inc(normed, 1)

                    maxima(0)
                    for n in range(1, U + 1):
                        if n < U:
                            maxima(n)
                        norm(n - 1)
                    dve.wait_ge(y_ps, b + 1)
                    dve.wait_ge(xb, b + 1)
                    nc.vector.tensor_tensor(R[:].rearrange("p t n -> p (t n)"), FR1[:],
                                            XB[:].rearrange("p t n -> p (t n)"), ALU.add).then_inc(r_sb, 1)
                    dve.wait_ge(r_sb, b + 1)
                    layernorm_stats(nc, chain, R, st, mv, ve, var, LN_EPS)
                    dve.wait_ge(rstd_ok, b + 1)
                    layernorm_apply(nc, R, mv, rstd, X1).then_inc(x1_ok, 1)
                    x.vector(dve, b, chain)
                    assert chain.n == LINKS, (chain.n, LINKS)

                step(0)
                with dve.Fori(1, B) as b:
                    step(b)
            @block.gpsimd
            def _(pool):
                nc.gpsimd.memset(neghalf[:], -0.5).then_inc(hv, 1)
                pool.wait_ge(hv, 1)
                pool.wait_ge(consts, ALL_CONSTS)
                def step(b):
                    pool.wait_ge(ms_ok, b + 1)
                    nc.gpsimd.tensor_tensor(rr[:], ms[:], neghalf[:], ALU.pow).then_inc(rr_ok, 1)
                    at_least(pool, r_sb, b)
                    nc.gpsimd.tensor_tensor(XB[:], XIN[:], broadcast_mid(row[:, 0, :], NT), ALU.add).then_inc(xb, 1)

                    def add_queries(c):
                        pool.wait_ge(t1_sb, CH * b + c + 1)
                        pool.wait_ge(t2_sb, CH * b + c + 1)
                        nc.gpsimd.tensor_tensor(qT[:, c, :], t1[c % 2][:, 0, :], t2[c % 2][:, 0, :],
                                                ALU.add).then_inc(q_sb, 1)

                    for c in range(CH):
                        pool.wait_ge(raw_sb, CH * b + c + 1)
                        if c >= 2:
                            pool.wait_ge(k_sb, CH * b + c - 1)
                            pool.wait_ge(q_sb, CH * b + c - 1)
                        nc.gpsimd.tensor_tensor(t1[c % 2][:], raw[c % 2][:], cs[:, 0, :, :], ALU.mult).then_inc(t1_sb, 1)
                        if c:
                            add_queries(c - 1)
                    add_queries(CH - 1)
                    pool.wait_ge(var, b + 1)
                    nc.gpsimd.tensor_tensor(rstd[:], ve[:], neghalf[:], ALU.pow).then_inc(rstd_ok, 1)
                    x.pool(pool, b, X1_READY(b))

                step(0)
                with pool.Fori(1, B) as b:
                    step(b)
        al.end()


def decoder(nc, d):
    x2 = nc.dram_tensor("after_L0_xattn", (B, S, D), F32, kind="Internal").ap()
    x3 = nc.dram_tensor("after_L0_ffn", (B, S, D), F32, kind="Internal").ap()
    x5 = nc.dram_tensor("after_L1_xattn", (B, S, D), F32, kind="Internal").ap()
    flat = lambda ap: ap.rearrange("b s n -> (b s) n")
    cross = lambda layer: {n: d[f"{layer}_xattn_{n}"] for n in ("Wq", "Wk", "Wv", "Wo")}
    router = lambda layer: {"ident": d["ident"], "before": d["before"], "iota": d["iota"],
                            **{n: d[f"{layer}_ffn_{n}"] for n in ("Wr", "br", "W1", "b1", "W2", "b2")}}
    relative_attention_phase(nc, {**d, "x2": x2, "L0_xattn": cross("L0")})
    experts_phase(nc, {**router("L0"), "x": flat(x2), "out": flat(x3)}, "b_", 1, 512, ACT.Relu, False)
    segment_attention_phase(nc, {**d, "x": x3, "x5": x5, "L1_xattn": cross("L1")})
    experts_phase(nc, {**router("L1"), "gb": d["L1_gb"], "x": flat(x5), "out": flat(d["out"])},
                  "e_", 2, 1024, ACT.Gelu, True)


def constants():
    f = np.float32
    c = {"ident": np.eye(P, dtype=f),
         "before": (np.arange(P)[:, None] < np.arange(P)).astype(f),
         "headmask": (np.arange(P)[:, None] // HD == np.arange(HC)).astype(f),
         "iota": np.tile(np.concatenate([np.arange(E8), P * np.arange(most_tiles(2))]).astype(f), (P, 1))}
    buckets, furthest = 64, 128
    mid = buckets // 2
    r = np.arange(1 - S, S)
    far = np.maximum(np.abs(r), mid - 1).astype(f)
    log = np.ceil(np.log(far / f(mid)) / f(np.log((furthest - 1) / mid)) * f(mid - 1)) + mid
    bucket = np.clip(np.where(far <= mid, r, log * np.sign(r)).astype(int) + buckets, 0, 2 * buckets - 1)
    onehot = (np.arange(P)[:, None] == bucket).astype(f)
    c["onehot"] = np.concatenate([onehot[:, ::-1], onehot], 1)
    inv = (f(1) / f(10000.0) ** (np.arange(0, DH, 2, dtype=f) / f(DH))).astype(f)
    angle = np.arange(S, dtype=f)[:, None] * inv
    both = [np.tile(np.repeat(g(angle), 2, -1).T, (P // DH, 1)) for g in (np.cos, np.sin)]
    c["cossin"] = np.stack([np.stack([g, g], 1) for g in both], 1).astype(f)
    rot = np.zeros((P, P), f)
    even = np.arange(0, P, 2)
    rot[even + 1, even], rot[even, even + 1] = -1, 1
    c["rot"] = rot
    c["mask"] = np.zeros((P, PM + P), f)
    c["mask"][:, PM:] = np.where(np.arange(P) <= np.arange(P)[:, None], 0, -3e38)
    return c


def laid_out(v):
    col = lambda n: v[n].reshape(KC, P).T
    out = dict(constants())
    for n in ("L0_attn_Wq", "L0_attn_Wk", "L0_attn_Wv", "L0_attn_Wo", "L0_attn_Wpk", "L0_attn_Wpq", "L0_attn_rel_emb"):
        out[n.replace("attn_", "")] = v[n]
    for layer in ("L0", "L1"):
        for n in ("Wq", "Wk", "Wv", "Wo"):
            out[f"{layer}_xattn_{n}"] = v[f"{layer}_xattn_{n}"]
        out[f"{layer}_ffn_b1"] = v[f"{layer}_ffn_b1"].reshape(E8, -1, P).transpose(0, 2, 1)
        out[f"{layer}_ffn_b2"] = v[f"{layer}_ffn_b2"]
    out["L0_ffn_Wr"], out["L1_ffn_Wr"] = v["L0_ffn_Wr"], v["L1_ffn_Wg"].T
    out["L0_ffn_br"], out["L1_ffn_br"] = v["L0_ffn_br"], v["L1_ffn_bg"]
    for n in ("W1", "W2"):
        out[f"L0_ffn_{n}"] = v[f"L0_ffn_{n}"]
        out[f"L1_ffn_{n}"] = v[f"L1_ffn_{n}"].transpose(0, 2, 1)
    out["L0_col"] = np.concatenate([col("L0_attn_bq"), col("L0_attn_bk"), col("L0_xattn_bq"), col("L0_xattn_bk")], 1)
    out["L0_row"] = np.stack([v["L0_attn_bv"], v["L0_attn_bv"], v["L0_attn_bo"], v["L0_xattn_bv"], v["L0_xattn_bo"]])
    out["L0_prow"] = np.stack([v["L0_attn_ln_g"], v["L0_attn_ln_b"], v["L0_attn_bpk"], v["L0_attn_bpq"]])
    out["L1_col"] = np.concatenate([col("L1_attn_norm_w"), col("L1_xattn_bq"), col("L1_xattn_bk")], 1)
    out["L1_row"] = np.stack([v["L1_attn_b_out"], v["L1_xattn_bv"], v["L1_xattn_bo"]])
    out["L1_gb"] = np.stack([v["L1_ffn_gamma"], v["L1_ffn_beta"]])
    out["w_qkv"], out["w_out"] = v["L1_attn_w_qkv"], v["L1_attn_w_out"]
    out["pm_kT"] = v["L1_attn_pm_k"].transpose(0, 2, 1).reshape(INNER, PM)
    out["pm_v"] = v["L1_attn_pm_v"]
    out["ctxT"] = v["ctx_768"].transpose(0, 2, 1)
    out["x"] = v["x"]
    return out


def kernel(**inputs):
    from concourse import bacc
    from concourse.bass_utils import run_bass_kernel_spmd

    nc = bacc.Bacc("TRN2", target_bir_lowering=False, num_devices=1)
    arrays, d = {}, {}
    for name, a in laid_out({n: np.asarray(a) for n, a in inputs.items()}).items():
        a = np.ascontiguousarray(a)
        arrays[f"in_{name}"] = a
        d[name] = nc.dram_tensor(f"in_{name}", a.shape, mybir.dt.from_np(a.dtype), kind="ExternalInput").ap()
    d["out"] = nc.dram_tensor("out", (B, S, D), F32, kind="ExternalOutput").ap()
    decoder(nc, d)
    return run_bass_kernel_spmd(nc, [arrays], core_ids=[0]).results[0]["out"]
```

```python
from contextlib import ExitStack

import numpy as np

import concourse.bass as bass
from concourse import mybir

F32 = mybir.dt.float32
I32 = mybir.dt.int32
U32 = mybir.dt.uint32
ALU = mybir.AluOpType
ACT = mybir.ActivationFunctionType
AXX = mybir.AxisListType.X

P = 128
B, S, D = 8, 256, 256
T = B * S
KC = D // P
NT = S // P
H, HD = 16, 16
HG = 4
NG = H // HG
HC = P // HD
CK, CD = 77, 192
CC = CD // 2
REL = 2 * S - 1
WIN = S + P - 1
CLAMP = 10000.0
LN_EPS = 1e-5


def at_least(eng, sem, value):
    if not (isinstance(value, int) and value <= 0):
        eng.wait_ge(sem, value)


def own_wait(eng, sem):
    eng.sem_inc(sem, 1)


def wait_alone(eng, sem, awaited, value):
    if not (isinstance(value, int) and value <= 0):
        eng.wait_ge(awaited, value)
        own_wait(eng, sem)


def repeated(ap, n):
    return bass.AP(ap.tensor, ap.offset, [ap.ap[0], [0, n]])


class Chain:

    def __init__(self, eng, sem, waited=None):
        self.eng, self.sem, self.waited, self.n, self.base = eng, sem, waited, 0, 0

    def start(self, base):
        self.base, self.n = base, 0

    def link(self, ins):
        ins.then_inc(self.sem, 1)
        self.n += 1
        self.eng.wait_ge(self.sem, self.base + self.n)


def broadcast_mid(ap, n):
    return bass.AP(ap.tensor, ap.offset, [ap.ap[0], [0, n], ap.ap[1]])


def broadcast_last(ap, n):
    return bass.AP(ap.tensor, ap.offset, [ap.ap[0], ap.ap[1], [0, n]])


def exists(b):
    return not isinstance(b, int) or 0 <= b < B


def lagged(b, n, count, lag, do):
    batches, unit = divmod(n - lag, count)
    if exists(b + batches):
        do(b + batches, unit)


class Alloc:

    def __init__(self, nc, phase, prefix):
        self.nc, self.phase, self.prefix = nc, phase, prefix
        self.sems = []

    def sb(self, name, shape, dt=F32):
        return self.phase.enter_context(self.nc.sbuf_tensor(self.prefix + name, shape, dt))

    def bank(self, name):
        return self.phase.enter_context(self.nc.psum_tensor(self.prefix + name, [P, 512], F32))

    def sem(self, name):
        self.sems.append(self.nc.alloc_semaphore(name=self.prefix + name))
        return self.sems[-1]

    def end(self):
        self.nc.all_engine_barrier()
        self.nc.clear_and_free_semaphores(self.sems)
        self.nc.all_engine_barrier()


class Cross:

    STEPS = 16
    SCORES = range(2, 6)
    PAIRS = range(9, 13)
    OUTPUTS = range(10, 14)
    VECTOR_LINKS = 2 * NT + 2

    def __init__(self, al, a, w, clip, x1_ok, banks):
        self.nc, self.a, self.clip, self.x1_ok = al.nc, a, clip, x1_ok
        self.w = w
        self.FR = banks
        self.wq = al.sb("xwq", [P, KC, D])
        self.wk = al.sb("xwk", [CC, 2, D])
        self.wv = al.sb("xwv", [CC, 2, D])
        self.wo = al.sb("xwo", [P, NG, D])
        self.ctxT = al.sb("ctxT", [CC, 2, CK])
        self.x1T = al.sb("x1T", [P, KC, S])
        self.OT = al.sb("xOT", [P, NG, S])
        self.R = al.sb("xR", [P, NT, D])
        self.PT = al.sb("xPT", [CK, 2, HG, S])
        self.qT = al.sb("xqT", [P, KC, S])
        self.kM = al.sb("xkM", [P, KC, HC * CK])
        self.v = al.sb("xv", [CK, H, 32])
        self.SX = al.sb("SX", [P, NT, H * CK])
        self.mx = al.sb("xmx", [P, NT, H])
        self.sm = al.sb("xsm", [P, NT, H])
        self.rs = al.sb("xrs", [P, NT, H])
        self.X1B = al.sb("X1B", [P, NT, D])
        self.st = al.sb("xst", [P, NT, 6])
        self.mv = al.sb("xmv", [P, NT, 2])
        self.ve = al.sb("xve", [P, NT])
        self.rstd = al.sb("xrstd", [P, NT])
        self.X2 = al.sb("X2", [P, NT, D])
        s = al.sem
        self.sp_waited = s("x_sp_waited")
        self.weights = s("x_weights")
        self.zeroed = s("x_zeroed")
        self.ctx_in = s("x_ctx_in")
        self.x1T_ps = s("x_x1T_ps")
        self.x1T_sb = s("x_x1T_sb")
        self.q_ps = s("x_q_ps")
        self.q_sb = s("x_q_sb")
        self.kv_ps = s("x_kv_ps")
        self.kv_sb = s("x_kv_sb")
        self.sc_ps = s("x_sc_ps")
        self.sc_sb = s("x_sc_sb")
        self.shifted = s("x_shifted")
        self.exped = s("x_exped")
        self.recip = s("x_recip")
        self.normed = s("x_normed")
        self.pT_ps = s("x_pT_ps")
        self.pT_sbA = s("x_pT_sbA")
        self.pT_sbV = s("x_pT_sbV")
        self.o_ps = s("x_o_ps")
        self.o_sb = s("x_o_sb")
        self.y_ps = s("x_y_ps")
        self.x1b = s("x_x1b")
        self.r_sb = s("x_r_sb")
        self.var = s("x_var")
        self.rstd_ok = s("x_rstd")
        self.x2 = s("x_x2")
        self.stored = s("x_stored")

    def load_weights(self, sp):
        w = self.w
        sp.dma_start(self.wq[:], w["Wq"].rearrange("(k p) n -> p k n", p=P)).then_inc(self.weights, 16)
        sp.dma_start(self.wk[:], w["Wk"].rearrange("(k p) n -> p k n", p=CC)).then_inc(self.weights, 16)
        sp.dma_start(self.wv[:], w["Wv"].rearrange("(k p) n -> p k n", p=CC)).then_inc(self.weights, 16)
        sp.wait_ge(self.zeroed, 2)
        wo = w["Wo"].rearrange("(g j i) n -> j i g n", j=HG, i=HD)
        for j in range(HG):
            sp.dma_start(self.wo[32 * j:32 * j + HD, :, :], wo[j]).then_inc(self.weights, 16)

    WEIGHTS = (3 + HG) * 16

    def load_ctx(self, sp, b):
        at_least(sp, self.kv_ps, b)
        own_wait(sp, self.sp_waited)
        sp.dma_start(self.ctxT[:], self.a["ctxT"][b].rearrange("(k p) n -> p k n", p=CC)).then_inc(self.ctx_in, 16)

    def store(self, sp, b):
        sp.wait_ge(self.x2, b + 1)
        own_wait(sp, self.sp_waited)
        sp.dma_start(self.a["x2_out"][b].rearrange("(t p) n -> p t n", p=P), self.X2[:]).then_inc(self.stored, 16)

    def tensor(self, pe, b, step):
        nc, (FR0, FR1) = self.nc, self.FR
        if step == 0:
            pe.wait_ge(self.x1_ok, b + 1)
            for t in range(NT):
                for k in range(KC):
                    last = nc.tensor.transpose(FR0[:, k * S + t * P:k * S + (t + 1) * P],
                                               self.a["X1"][:, t, k * P:(k + 1) * P], self.a["ident"][:])
            last.then_inc(self.x1T_ps, 1)
        if step == 1:
            pe.wait_ge(self.ctx_in, b * 16 + 16)
            pe.wait_ge(self.x1T_sb, b + 1)
            at_least(pe, self.r_sb, b)
            for c in range(KC):
                for k in range(KC):
                    last = nc.tensor.matmul(FR1[:, c * S:(c + 1) * S], self.wq[:, k, c * P:(c + 1) * P],
                                            self.x1T[:, k, :], start=k == 0, stop=k == KC - 1)
            last.then_inc(self.q_ps, 1)
            for c in range(KC):
                for k in range(2):
                    nc.tensor.matmul(FR0[:, c * CK:(c + 1) * CK], self.wk[:, k, c * P:(c + 1) * P],
                                     self.ctxT[:, k, :], start=k == 0, stop=k == 1)
            for k in range(2):
                last = nc.tensor.matmul(FR0[0:CK, S:S + D], self.ctxT[:, k, :], self.wv[:, k, :],
                                        start=k == 0, stop=k == 1)
            last.then_inc(self.kv_ps, 1)
        if step in self.SCORES:
            for i in range(2 * (step - 2), 2 * (step - 2) + 2):
                t, q = i // 4, i % 4
                if i == 0:
                    pe.wait_ge(self.kv_sb, b + 1)
                    pe.wait_ge(self.q_sb, b + 1)
                if i >= 2:
                    pe.wait_ge(self.sc_sb, 8 * b + i - 1)
                nc.tensor.matmul(self.FR[i % 2][:, 0:4 * CK], self.qT[:, q // 2, t * P:(t + 1) * P],
                                 self.kM[:, q // 2, (q % 2) * 4 * CK:(q % 2 + 1) * 4 * CK],
                                 start=True, stop=True).then_inc(self.sc_ps, 1)
        if step in self.OUTPUTS:
            g = step - 10
            pe.wait_ge(self.pT_sbA, 4 * b + g + 1)
            pe.wait_ge(self.pT_sbV, 4 * b + g + 1)
            for j in range(HG):
                last = nc.tensor.matmul(FR0[32 * j:32 * j + 32, 0:S], self.v[:, HG * g + j, :],
                                        self.PT[:, g % 2, j, :], start=True, stop=True)
            last.then_inc(self.o_ps, 1)
        if step in self.PAIRS:
            for hp in range(2 * (step - 9), 2 * (step - 9) + 2):
                if hp == 0:
                    pe.wait_ge(self.normed, 2 * b + 2)
                elif hp % 2 == 1 and hp > 1:
                    pe.wait_ge(self.o_sb, 4 * b + hp // 2)
                for u in range(2):
                    for t in range(NT):
                        h = 2 * hp + u
                        last = nc.tensor.transpose(
                            self.FR[1 - hp % 2][0:CK, u * S + t * P:u * S + (t + 1) * P],
                            self.SX[:, t, h * CK:(h + 1) * CK], self.a["ident"][:])
                last.then_inc(self.pT_ps, 1)
        if step == 14:
            pe.wait_ge(self.o_sb, 4 * b + 4)
            for t in range(NT):
                for g in range(NG):
                    last = nc.tensor.matmul(FR1[:, t * D:(t + 1) * D], self.OT[:, g, t * P:(t + 1) * P],
                                            self.wo[:, g, :], start=g == 0, stop=g == NG - 1)
            last.then_inc(self.y_ps, 1)

    def scalar(self, act, b, step):
        nc, (FR0, FR1) = self.nc, self.FR
        if step == 0:
            act.wait_ge(self.x1T_ps, b + 1)
            nc.scalar.activation(self.x1T[:].rearrange("p k n -> p (k n)"), FR0[:], ACT.Copy).then_inc(self.x1T_sb, 1)
        if step == 1:
            act.wait_ge(self.q_ps, b + 1)
            for c in range(KC):
                last = nc.scalar.activation(self.qT[:, c, :], FR1[:, c * S:(c + 1) * S], ACT.Identity,
                                            bias=self.a["xbq"][:, c:c + 1])
            last.then_inc(self.q_sb, 1)
        if step in self.SCORES and not self.clip:
            for i in range(2 * (step - 2), 2 * (step - 2) + 2):
                t, q = i // 4, i % 4
                act.wait_ge(self.sc_ps, 8 * b + i + 1)
                nc.scalar.activation(self.SX[:, t, q * 4 * CK:(q + 1) * 4 * CK], self.FR[i % 2][:, 0:4 * CK],
                                     ACT.Copy).then_inc(self.sc_sb, 1)
        if step in (5, 7):
            t = (step - 5) // 2
            act.wait_ge(self.shifted, 2 * b + t + 1)
            nc.scalar.activation(self.SX[:, t, :], self.SX[:, t, :], ACT.Exp,
                                 scale=float(HD) ** -0.5).then_inc(self.exped, 1)
        if step in self.OUTPUTS:
            g = step - 10
            act.wait_ge(self.o_ps, 4 * b + g + 1)
            nc.scalar.activation(self.OT[:, g, :], FR0[:, 0:S], ACT.Copy).then_inc(self.o_sb, 1)
        if step in self.PAIRS:
            g = step - 9
            act.wait_ge(self.pT_ps, 8 * b + 2 * g + 1)
            nc.scalar.activation(self.PT[:, g % 2, 0:2, :].rearrange("p h n -> p (h n)"),
                                 FR1[0:CK, :], ACT.Copy).then_inc(self.pT_sbA, 1)

    def vector(self, dve, b, step, chain):
        nc, a, (FR0, FR1) = self.nc, self.a, self.FR
        lim = CLAMP / float(HD) ** -0.5
        heads = lambda t: self.SX[:, t, :].rearrange("p (h n) -> p h n", h=H)
        if step == 1:
            dve.wait_ge(self.kv_ps, b + 1)
            for c in range(KC):
                nc.vector.scalar_tensor_tensor(
                    out=self.kM[:, c, :].rearrange("p (h n) -> p h n", h=HC),
                    in0=broadcast_mid(FR0[:, c * CK:(c + 1) * CK], HC), scalar=a["xbk"][:, c:c + 1],
                    in1=broadcast_last(a["headmask"][:, 0:HC], CK), op0=ALU.add, op1=ALU.mult)
            nc.vector.tensor_tensor(self.v[:, :, 0:HD], FR0[0:CK, S:S + D].rearrange("p (h n) -> p h n", h=H),
                                    a["xbv"][0:CK, :].rearrange("p (h n) -> p h n", h=H),
                                    ALU.add).then_inc(self.kv_sb, 1)
        if step in self.SCORES and self.clip:
            for i in range(2 * (step - 2), 2 * (step - 2) + 2):
                t, q = i // 4, i % 4
                dve.wait_ge(self.sc_ps, 8 * b + i + 1)
                nc.vector.tensor_scalar(self.SX[:, t, q * 4 * CK:(q + 1) * 4 * CK], self.FR[i % 2][:, 0:4 * CK],
                                        lim, -lim, ALU.min, ALU.max).then_inc(self.sc_sb, 1)
        if step in (3, 5):
            t = (step - 3) // 2
            dve.wait_ge(self.sc_sb, 8 * b + 4 * t + 4)
            chain.link(nc.vector.tensor_reduce(self.mx[:, t, :], heads(t), AXX, ALU.max))
            nc.vector.tensor_tensor(heads(t), heads(t), broadcast_last(self.mx[:, t, :], CK),
                                    ALU.subtract).then_inc(self.shifted, 1)
        if step in (6, 8):
            t = (step - 6) // 2
            dve.wait_ge(self.exped, 2 * b + t + 1)
            chain.link(nc.vector.tensor_reduce(self.sm[:, t, :], heads(t), AXX, ALU.add))
            nc.vector.reciprocal(self.rs[:, t, :], self.sm[:, t, :]).then_inc(self.recip, 1)
        if step in self.PAIRS:
            g = step - 9
            dve.wait_ge(self.pT_ps, 8 * b + 2 * g + 2)
            nc.vector.tensor_copy(self.PT[:, g % 2, 2:4, :].rearrange("p h n -> p (h n)"),
                                  FR0[0:CK, :]).then_inc(self.pT_sbV, 1)
        if step == 14:
            dve.wait_ge(self.y_ps, b + 1)
            dve.wait_ge(self.x1b, b + 1)
            nc.vector.tensor_tensor(self.R[:].rearrange("p t n -> p (t n)"), FR1[:],
                                    self.X1B[:].rearrange("p t n -> p (t n)"), ALU.add).then_inc(self.r_sb, 1)
            dve.wait_ge(self.r_sb, b + 1)
            layernorm_stats(nc, chain, self.R, self.st, self.mv, self.ve, self.var, LN_EPS)
        if step == 15:
            dve.wait_ge(self.rstd_ok, b + 1)
            at_least(dve, self.stored, 16 * b)
            layernorm_apply(nc, self.R, self.mv, self.rstd, self.X2).then_inc(self.x2, 1)

    def pool(self, pool, b, step):
        nc, a = self.nc, self.a
        if step == 0:
            pool.wait_ge(self.x1_ok, b + 1)
            at_least(pool, self.r_sb, b)
            nc.gpsimd.tensor_tensor(self.X1B[:], a["X1"][:], broadcast_mid(a["xbo"], NT),
                                    ALU.add).then_inc(self.x1b, 1)
        if step in (7, 8):
            t = step - 7
            pool.wait_ge(self.recip, 2 * b + t + 1)
            v = self.SX[:, t, :].rearrange("p (h n) -> p h n", h=H)
            nc.gpsimd.tensor_tensor(v, v, broadcast_last(self.rs[:, t, :], CK), ALU.mult).then_inc(self.normed, 1)
        if step == 14:
            pool.wait_ge(self.var, b + 1)
            nc.gpsimd.tensor_tensor(self.rstd[:], self.ve[:], a["neghalf"][:, 0:NT], ALU.pow).then_inc(self.rstd_ok, 1)


def layernorm_stats(nc, chain, R, st, mv, ve, var, eps):
    for t in range(NT):
        last = nc.vector.bn_stats(st[:, t, :], R[:, t, :])
    chain.link(last)
    own_wait(chain.eng, chain.waited)
    for t in range(NT):
        last = nc.vector.bn_aggr(mv[:, t, :], st[:, t, :])
    chain.link(last)
    nc.vector.tensor_scalar(ve[:], mv[:, :, 1], eps, None, ALU.add).then_inc(var, 1)


def layernorm_apply(nc, R, mv, rstd, out):
    for t in range(NT):
        last = nc.vector.tensor_scalar(out[:, t, :], R[:, t, :], mv[:, t, 0:1], rstd[:, t:t + 1],
                                       ALU.subtract, ALU.mult)
    return last


def relative_attention_phase(nc, d):
    with ExitStack() as phase:
        al = Alloc(nc, phase, "a_")
        sb, sem = al.sb, al.sem
        scale = float(3 * HD) ** -0.5
        table_scale = float(3 * HD / (2 * HD)) ** 0.5

        FR0, FR1, BD0, BD1, SC0, SC1, PTB, PO = [al.bank(n) for n in
                                                 ("FR0", "FR1", "BD0", "BD1", "SC0", "SC1", "PTB", "PO")]
        BD, SC = [BD0, BD1], [SC0, SC1]
        RING = 4

        ident = sb("ident", [P, P])
        headmask = sb("headmask", [P, HC])
        col = sb("col", [P, 8])
        row = sb("row", [P, 5, D])
        neghalf = sb("neghalf", [P, NT])
        wq = sb("wq", [P, KC, D])
        wk = sb("wk", [P, KC, D])
        wv = sb("wv", [P, KC, D])
        wo = sb("wo", [P, NG, D])
        E = [sb("E1", [P, KC, REL]), sb("E2", [P, KC, REL])]
        XIN = sb("XIN", [P, NT, D])
        XB = sb("XB", [P, NT, D])
        xT = sb("xT", [P, KC, S])
        qM = sb("qM", [P, H, S])
        kT = sb("kT", [P, KC, S])
        kM = sb("kM", [P, H, S])
        v = sb("v", [P, NT, H, 32])
        ST = [sb(f"stage{k}", [P, RING, NT, WIN]) for k in range(2)]
        SK = [sb(f"skewed{k}", [P, RING, NT, S]) for k in range(2)]
        SM = sb("SM", [P, RING, NT, S])
        nb = sb("nb", [P, RING, NT])
        sm = sb("sm", [P, RING, NT])
        rs = sb("rs", [P, RING, NT])
        OT = sb("OT", [P, NG, S])
        R = sb("R", [P, NT, D])
        st = sb("st", [P, NT, 6])
        mv = sb("mv", [P, NT, 2])
        ve = sb("ve", [P, NT])
        rstd = sb("rstd", [P, NT])
        X1 = sb("X1", [P, NT, D])
        remb = SM[:, 0, 0, :]
        rows = [SM[:, 1, 0, :], SM[:, 1, 1, :]]
        prow = ST[0][:].rearrange("p h i w -> p (h i w)")[:, 0:4 * D].rearrange("p (r n) -> p r n", r=4)

        scratch = [nc.dram_tensor(f"a_band{k}", (RING, NT, P, WIN), F32, kind="Internal").ap() for k in range(2)]

        a = {"ident": ident, "headmask": headmask, "neghalf": neghalf, "X1": X1,
             "ctxT": d["ctxT"], "x2_out": d["x2"],
             "xbq": col[:, 4:6], "xbk": col[:, 6:8], "xbv": row[:, 3, :], "xbo": row[:, 4, :]}
        PTr = sb("PTr", [P, 2, NT, S])

        consts = sem("consts")
        weights = sem("weights")
        zeroed = sem("zeroed")
        tv = sem("table_vector")
        tp = sem("table_pool")
        tt = sem("table_tensor")
        x_in, sp_waited = sem("x_in"), sem("sp_waited")
        xT_ps, xT_sb = sem("xT_ps"), sem("xT_sb")
        q_ps, k_ps, v_ps = sem("q_ps"), sem("k_ps"), sem("v_ps")
        q_sb, k_sb, v_sb, kM_sb = sem("q_sb"), sem("k_sb"), sem("v_sb"), sem("kM_sb")
        xb_in, xb = sem("xb_in"), sem("xb")
        band_ps = [sem("band_ps0"), sem("band_ps1")]
        band_sb = [sem("band_sb0"), sem("band_sb1")]
        band_out = [sem("band_out_even"), sem("band_out_odd")]
        band_in = [[sem("keys_in_even"), sem("keys_in_odd")], [sem("queries_in_even"), sem("queries_in_odd")]]
        sc_ps = sem("sc_ps")
        maxed = sem("maxed")
        exped = sem("exped")
        normed = sem("normed")
        pT_ps, pT_sb = sem("pT_ps"), sem("pT_sb")
        o_ps, o_sb = sem("o_ps"), sem("o_sb")
        y_ps, r_sb, var, rstd_ok, x1_ok = sem("y_ps"), sem("r_sb"), sem("var"), sem("rstd"), sem("x1")
        dv, waited = sem("dve_chain"), sem("dve_waited")
        x = Cross(al, a, d["L0_xattn"], True, x1_ok, [FR0, FR1])

        LINKS = H + 2 + x.VECTOR_LINKS

        LEAD, NORM, TRANSPOSE, OUTPUT = 5, 1, 2, 3
        CHUNK1, PROJECT, RESULT, VALUES1 = 0, 3, 4, 5
        INPUT, CHUNK0, VALUES0 = 7, 8, 12
        CROSS_LAG = H + 5

        NEAR = [slice(0, S), slice(WIN - S, WIN)]
        FAR = [slice(S, WIN), slice(0, WIN - S)]

        def cross(b, n, do):
            lagged(b, n, H, CROSS_LAG, do)

        with nc.Block() as block:

            @block.sync
            def _(sp):
                for dst, src in ((ident[:], d["ident"]), (headmask[:], d["headmask"]), (col[:], d["L0_col"]),
                                 (remb, d["L0_rel_emb"]),
                                 (row[:], d["L0_row"].partition_broadcast(P)),
                                 (prow, d["L0_prow"].partition_broadcast(P)),
                                 (qM[:, 0:4, :].rearrange("p h n -> p (h n)")[:, 0:2 * REL], d["onehot"])):
                    sp.dma_start(dst, src).then_inc(consts, 16)
                for dst, src in ((kM[:, 0:2, :], d["L0_Wpk"]), (kM[:, 2:4, :], d["L0_Wpq"]), (wq[:], d["L0_Wq"]),
                                 (wk[:], d["L0_Wk"]), (wv[:], d["L0_Wv"])):
                    sp.dma_start(dst, src.rearrange("(k p) n -> p k n", p=P)).then_inc(weights, 16)
                sp.wait_ge(zeroed, 2)
                w4 = d["L0_Wo"].rearrange("(g j i) n -> j i g n", j=HG, i=HD)
                for j in range(HG):
                    sp.dma_start(wo[32 * j:32 * j + HD, :, :], w4[j]).then_inc(weights, 16)
                x.load_weights(sp)

                def load_x(b):
                    wait_alone(sp, sp_waited, xT_ps, b)
                    sp.dma_start(XIN[:], d["x"][b].rearrange("(t p) n -> p t n", p=P)).then_inc(x_in, 16)

                def load_residual(b):
                    wait_alone(sp, sp_waited, r_sb, b)
                    sp.dma_start(XB[:], d["x"][b].rearrange("(t p) n -> p t n", p=P)).then_inc(xb_in, 16)

                def bands_out(b, h):
                    for i in range(2):
                        wait_alone(sp, sp_waited, band_sb[i], 32 * b + 2 * h + 2)
                    for k in range(2):
                        wait_alone(sp, sp_waited, band_in[k][h % 2], 16 * (8 * b + h // 2 - 1))
                    for k in range(2):
                        sp.dma_start(scratch[k][h % RING].rearrange("n p w -> p n w"),
                                     ST[k][:, h % RING]).then_inc(band_out[h % 2], 16)

                def bands_back(b, h):
                    wait_alone(sp, sp_waited, band_out[h % 2], 32 * (8 * b + h // 2 + 1))
                    wait_alone(sp, sp_waited, maxed, 16 * b + h + 1 - RING)
                    wait_alone(sp, sp_waited, sc_ps, 16 * b + h + 1 - RING)
                    for k in range(2):
                        wait_alone(sp, sp_waited, band_in[k][h % 2], 16 * (8 * b + h // 2))
                    for k in range(2):
                        base = scratch[k][h % RING]
                        src = bass.AP(base.tensor, base.offset + P - 1, [[WIN - 1, P], [P * WIN, NT], [1, S]])
                        sp.dma_start(SK[k][:, h % RING], src).then_inc(band_in[k][h % 2], 16)

                def step(b, slots=range(H)):
                    for n in slots:
                        lagged(b, n, H, -LEAD, bands_out)
                        lagged(b, n, H, 1 - LEAD, bands_back)
                        if n == 2 and exists(b + 1):
                            load_x(b + 1)
                        if n == PROJECT + 2 and exists(b):
                            load_residual(b)
                        if n == 8 and exists(b):
                            x.load_ctx(sp, b)
                        if n == 8 and exists(b - 2):
                            x.store(sp, b - 2)

                load_x(0)
                step(-1, range(INPUT, H))
                step(0)
                step(1)
                step(2)
                with sp.Fori(3, B - 1) as b:
                    step(b)
                for b in range(B - 1, B + 2):
                    step(b)
                sp.wait_ge(x.stored, 16 * B)

            @block.tensor
            def _(pe):
                pe.wait_ge(consts, 112)
                pe.wait_ge(weights, (5 + HG) * 16)
                pe.wait_ge(x.weights, x.WEIGHTS)
                pe.wait_ge(tv, 5)
                for k in range(KC):
                    last = nc.tensor.transpose(FR0[:, k * P:(k + 1) * P], remb[:, k * P:(k + 1) * P], ident[:])
                last.then_inc(tt, 1)
                pe.wait_ge(tv, 6)
                for n in range(2):
                    for k in range(KC):
                        last = nc.tensor.matmul(FR1[:, n * D:(n + 1) * D], xT[:, k, 0:P], kM[:, 2 * n + k, :],
                                                start=k == 0, stop=k == KC - 1)
                last.then_inc(tt, 1)
                pe.wait_ge(tv, 8)
                onehot = qM[:, 0:4, :].rearrange("p h n -> p (h n)")
                for n in range(2):
                    for c in range(KC):
                        last = nc.tensor.matmul([BD0, BD1, SC0, SC1][2 * n + c][:, 0:REL],
                                                rows[n][:, c * P:(c + 1) * P], onehot[:, n * REL:(n + 1) * REL],
                                                start=True, stop=True)
                last.then_inc(tt, 1)
                pe.wait_ge(tv, 9)

                def banks_copied(b, n):
                    if n == CHUNK1 + 1 and exists(b):
                        pe.wait_ge(q_sb, 2 * b + 2)
                        pe.wait_ge(k_sb, 2 * b + 2)
                    if n == PROJECT + 1 and exists(b - 1):
                        pe.wait_ge(r_sb, b)
                    if n == VALUES1 + 1 and exists(b):
                        pe.wait_ge(v_sb, 2 * b + 2)
                    if n == INPUT + 1 and exists(b + 1):
                        pe.wait_ge(xT_sb, b + 2)
                    if n == CHUNK0 + 1 and exists(b + 1):
                        pe.wait_ge(q_sb, 2 * b + 3)
                        pe.wait_ge(k_sb, 2 * b + 3)
                    if n == VALUES0 + 1 and exists(b + 1):
                        pe.wait_ge(v_sb, 2 * b + 3)

                def bands_copied(b, n, banks):
                    for i in banks:
                        count = 32 * b + 2 * (n + LEAD + 1)
                        at_least(pe, band_sb[i], min(count, 32 * B) if isinstance(b, int) else count)

                def band(k):
                    def do(b, h):
                        if h % HC == 0:
                            pe.wait_ge(kM_sb if k else q_sb, 2 * b + h // HC + 1)
                        for i in range(NT):
                            at_least(pe, band_sb[i], 32 * b + 2 * h + k)
                            near = NEAR[i]
                            nc.tensor.matmul(BD[i][:, 0:S], (kM if k else qM)[:, h, i * P:(i + 1) * P],
                                             E[k][:, h // HC, P - P * i + near.start:P - P * i + near.stop],
                                             start=True, stop=True).then_inc(band_ps[i], 1)
                    return do

                def scores(b, h):
                    if h % HC == 0:
                        pe.wait_ge(k_sb, 2 * b + h // HC + 1)
                    pe.wait_ge(band_in[1][h % 2], 16 * (8 * b + h // 2 + 1))
                    at_least(pe, maxed, 16 * b + h - 1)
                    for i in range(NT):
                        for j in range(NT):
                            nc.tensor.matmul(SC[h % 2][:, i * S + j * P:i * S + (j + 1) * P],
                                             SK[1][:, h % RING, j, i * P:(i + 1) * P], ident[:],
                                             start=j == 0, stop=False, skip_group_check=True)
                        last = nc.tensor.matmul(SC[h % 2][:, i * S:(i + 1) * S], qM[:, h, i * P:(i + 1) * P],
                                                kT[:, h // HC, :], start=False, stop=True, skip_group_check=True)
                    last.then_inc(sc_ps, 1)

                def transposes(b, h):
                    pe.wait_ge(normed, 16 * b + h + 1)
                    at_least(pe, pT_sb, 16 * b + h)
                    for j in range(NT):
                        for i in range(NT):
                            last = nc.tensor.transpose(PTB[:, j * S + i * P:j * S + (i + 1) * P],
                                                       SM[:, h % RING, i, j * P:(j + 1) * P], ident[:])
                    last.then_inc(pT_ps, 1)

                def outputs(b, h):
                    pe.wait_ge(pT_sb, 16 * b + h + 1)
                    g, j = h // HG, h % HG
                    if h % HC == 0:
                        pe.wait_ge(v_sb, 2 * b + h // HC + 1)
                    if j == 0:
                        at_least(pe, o_sb, 4 * b + g)
                    for t in range(NT):
                        last = nc.tensor.matmul(PO[32 * j:32 * j + 32, 0:S], v[:, t, h, :], PTr[:, h % 2, t, :],
                                                start=t == 0, stop=t == NT - 1)
                    last.then_inc(o_ps, 1)

                def project(b):
                    bands_copied(b + 1, PROJECT, [1])
                    pe.wait_ge(o_sb, 4 * b + NG)
                    for t in range(NT):
                        for g in range(NG):
                            last = nc.tensor.matmul(BD1[:, t * D:(t + 1) * D], OT[:, g, t * P:(t + 1) * P],
                                                    wo[:, g, :], start=g == 0, stop=g == NG - 1)
                    last.then_inc(y_ps, 1)

                def front_input(b):
                    bands_copied(b - 1, INPUT, [0])
                    pe.wait_ge(x_in, 16 * b + 16)
                    for t in range(NT):
                        for k in range(KC):
                            last = nc.tensor.transpose(BD0[:, k * S + t * P:k * S + (t + 1) * P],
                                                       XIN[:, t, k * P:(k + 1) * P], ident[:])
                    last.then_inc(xT_ps, 1)

                def chunk(b, c):
                    bands_copied(b if c else b - 1, CHUNK1 if c else CHUNK0, [0, 1])
                    pe.wait_ge(xT_sb, b + 1)
                    for k in range(KC):
                        last = nc.tensor.matmul(BD1[:, 0:S], wq[:, k, c * P:(c + 1) * P], xT[:, k, :],
                                                start=k == 0, stop=k == KC - 1)
                    last.then_inc(q_ps, 1)
                    for k in range(KC):
                        last = nc.tensor.matmul(BD0[:, 0:S], wk[:, k, c * P:(c + 1) * P], xT[:, k, :],
                                                start=k == 0, stop=k == KC - 1)
                    last.then_inc(k_ps, 1)

                def values(b, c):
                    bands_copied(b if c else b - 1, VALUES1 if c else VALUES0, [1])
                    for t in range(NT):
                        for k in range(KC):
                            last = nc.tensor.matmul(BD1[:, t * P:(t + 1) * P], xT[:, k, t * P:(t + 1) * P],
                                                    wv[:, k, c * P:(c + 1) * P], start=k == 0, stop=k == KC - 1)
                    last.then_inc(v_ps, 1)

                def step(b, slots=range(H)):
                    for n in slots:
                        banks_copied(b, n)
                        lagged(b, n, H, -LEAD, band(0))
                        lagged(b, n, H, 0, scores)
                        lagged(b, n, H, -LEAD, band(1))
                        lagged(b, n, H, TRANSPOSE, transposes)
                        lagged(b, n, H, OUTPUT, outputs)
                        if n == PROJECT and exists(b - 1):
                            project(b - 1)
                        if n == CHUNK1 and exists(b):
                            chunk(b, 1)
                        if n == VALUES1 and exists(b):
                            values(b, 1)
                        if n == INPUT and exists(b + 1):
                            front_input(b + 1)
                        if n == CHUNK0 and exists(b + 1):
                            chunk(b + 1, 0)
                        if n == VALUES0 and exists(b + 1):
                            values(b + 1, 0)
                        cross(b, n, lambda b, k: x.tensor(pe, b, k))

                step(-1, range(INPUT, H))
                step(0)
                step(1)
                step(2)
                with pe.Fori(3, B - 1) as b:
                    step(b)
                for b in range(B - 1, B + 2):
                    step(b)

            @block.scalar
            def _(act):
                act.wait_ge(consts, 112)

                def front_input(b):
                    act.wait_ge(xT_ps, b + 1)
                    at_least(act, v_ps, 2 * b)
                    nc.scalar.activation(xT[:].rearrange("p k n -> p (k n)"), BD0[:], ACT.Copy).then_inc(xT_sb, 1)

                def chunk(b, c):
                    act.wait_ge(k_ps, 2 * b + c + 1)
                    at_least(act, sc_ps, 16 * (b - 1) + HC * (c + 1))
                    at_least(act, kM_sb, 2 * b + c - 1)
                    nc.scalar.activation(kT[:, c, :], BD0[:, 0:S], ACT.Identity,
                                         bias=col[:, 2 + c:3 + c]).then_inc(k_sb, 1)

                def stage(k):
                    def do(b, h):
                        at_least(act, band_out[h % 2], 32 * (8 * b + h // 2 - 1))
                        act.wait_ge(band_ps[0], 32 * b + 2 * h + k + 1)
                        nc.scalar.activation(ST[k][:, h % RING, 0, NEAR[0]], BD0[:, 0:S], ACT.Copy)
                        nc.scalar.activation(ST[k][:, h % RING, 0, FAR[0]], repeated(BD0[:, S - 1:S], WIN - S),
                                             ACT.Copy).then_inc(band_sb[0], 1)
                    return do

                def exps(b, h):
                    act.wait_ge(maxed, 16 * b + h + 1)
                    r = h % RING
                    for i in range(NT):
                        last = nc.scalar.activation(SM[:, r, i, :], SM[:, r, i, :], ACT.Exp, bias=nb[:, r, i:i + 1],
                                                    scale=-1.0, accum_out=sm[:, r, i:i + 1])
                    last.then_inc(exped, 1)

                def copy_pT(b, h):
                    act.wait_ge(pT_ps, 16 * b + h + 1)
                    at_least(act, o_ps, 16 * b + h - 1)
                    nc.scalar.activation(PTr[:, h % 2, :, :].rearrange("p t s -> p (t s)"), PTB[:],
                                         ACT.Copy).then_inc(pT_sb, 1)

                def copy_o(b, h):
                    if h % HG != HG - 1:
                        return
                    g = h // HG
                    act.wait_ge(o_ps, 16 * b + h + 1)
                    at_least(act, y_ps, b)
                    nc.scalar.activation(OT[:, g, :], PO[:, 0:S], ACT.Copy).then_inc(o_sb, 1)

                def step(b, slots=range(H)):
                    for n in slots:
                        lagged(b, n, H, -LEAD, stage(0))
                        lagged(b, n, H, -LEAD, stage(1))
                        lagged(b, n, H, 0, exps)
                        lagged(b, n, H, TRANSPOSE, copy_pT)
                        lagged(b, n, H, OUTPUT, copy_o)
                        if n == CHUNK1 and exists(b):
                            chunk(b, 1)
                        if n == INPUT and exists(b + 1):
                            front_input(b + 1)
                        if n == CHUNK0 and exists(b + 1):
                            chunk(b + 1, 0)
                        cross(b, n, lambda b, k: x.scalar(act, b, k))

                step(-1, range(INPUT, H))
                step(0)
                step(1)
                step(2)
                with act.Fori(3, B - 1) as b:
                    step(b)
                for b in range(B - 1, B + 2):
                    step(b)

            @block.vector
            def _(dve):
                chain = Chain(dve, dv, waited)
                nc.vector.memset(wo[:], 0.0).then_inc(zeroed, 1)
                nc.vector.memset(v[:], 0.0).then_inc(zeroed, 1)
                nc.vector.memset(x.wo[:], 0.0).then_inc(x.zeroed, 1)
                nc.vector.memset(x.v[:], 0.0).then_inc(x.zeroed, 1)
                dve.wait_ge(consts, 112)
                nc.vector.bn_stats(st[:, 0, :], remb).then_inc(tv, 1)
                dve.wait_ge(tv, 1)
                nc.vector.bn_aggr(mv[:, 0, :], st[:, 0, :]).then_inc(tv, 1)
                dve.wait_ge(tv, 2)
                nc.vector.tensor_scalar(ve[:, 0:1], mv[:, 0, 1:2], LN_EPS, None, ALU.add).then_inc(tv, 1)
                dve.wait_ge(tp, 2)
                nc.vector.tensor_scalar(remb, remb, mv[:, 0, 0:1], rstd[:, 0:1], ALU.subtract,
                                        ALU.mult).then_inc(tv, 1)
                dve.wait_ge(tv, 4)
                nc.vector.tensor_tensor(remb, remb, prow[:, 0, :], ALU.mult).then_inc(zeroed, 1)
                dve.wait_ge(zeroed, 3)
                nc.vector.tensor_tensor(remb, remb, prow[:, 1, :], ALU.add).then_inc(tv, 1)
                dve.wait_ge(tt, 1)
                nc.vector.tensor_copy(xT[:, :, 0:P], FR0[:, 0:D].rearrange("p (k n) -> p k n", k=KC)).then_inc(tv, 1)
                dve.wait_ge(tt, 2)
                for n in range(2):
                    nc.vector.tensor_tensor(rows[n], FR1[:, n * D:(n + 1) * D], prow[:, 2 + n, :],
                                            ALU.add).then_inc(tv, 1)
                dve.wait_ge(tt, 3)
                for n in range(2):
                    for c in range(KC):
                        last = nc.vector.tensor_scalar(E[n][:, c, :], [BD0, BD1, SC0, SC1][2 * n + c][:, 0:REL],
                                                       table_scale, None, ALU.mult)
                last.then_inc(tv, 1)

                def chunk(b, c):
                    dve.wait_ge(q_ps, 2 * b + c + 1)
                    at_least(dve, sc_ps, 16 * (b - 1) + HC * (c + 1))
                    nc.vector.scalar_tensor_tensor(
                        out=qM[:, c * HC:(c + 1) * HC, :], in0=broadcast_mid(BD1[:, 0:S], HC),
                        scalar=col[:, c:c + 1], in1=broadcast_last(headmask[:], S), op0=ALU.add,
                        op1=ALU.mult).then_inc(q_sb, 1)

                def values(b, c):
                    dve.wait_ge(v_ps, 2 * b + c + 1)
                    at_least(dve, o_ps, 16 * (b - 1) + HC * (c + 1))
                    nc.vector.tensor_tensor(
                        v[:, :, c * HC:(c + 1) * HC, 0:HD], BD1[:, 0:S].rearrange("p (t h n) -> p t h n", t=NT, n=HD),
                        row[:, 0:2, c * P:(c + 1) * P].rearrange("p t (h n) -> p t h n", n=HD),
                        ALU.add).then_inc(v_sb, 1)

                def stage(k):
                    def do(b, h):
                        at_least(dve, band_out[h % 2], 32 * (8 * b + h // 2 - 1))
                        dve.wait_ge(band_ps[1], 32 * b + 2 * h + k + 1)
                        nc.vector.tensor_copy(ST[k][:, h % RING, 1, NEAR[1]], BD1[:, 0:S])
                        nc.vector.tensor_copy(ST[k][:, h % RING, 1, FAR[1]],
                                              repeated(BD1[:, 0:1], WIN - S)).then_inc(band_sb[1], 1)
                    return do

                def maxima(b, h):
                    r = h % RING
                    dve.wait_ge(band_in[0][h % 2], 16 * (8 * b + h // 2 + 1))
                    dve.wait_ge(sc_ps, 16 * b + h + 1)
                    at_least(dve, pT_ps, 16 * b + h + 1 - RING)
                    own_wait(dve, waited)
                    for i in range(NT):
                        last = nc.vector.tensor_tensor_reduce(
                            out=SM[:, r, i, :], in0=SC[h % 2][:, i * S:(i + 1) * S],
                            in1=SK[0][:, r, i, :], scale=-scale, scalar=3.0e38, op0=ALU.add, op1=ALU.min,
                            accum_out=nb[:, r, i:i + 1])
                    last.then_inc(maxed, 1)

                def norm(b, h):
                    r = h % RING
                    dve.wait_ge(exped, 16 * b + h + 1)
                    chain.link(nc.vector.reciprocal(rs[:, r, :], sm[:, r, :]))
                    for i in range(NT):
                        last = nc.vector.tensor_scalar(SM[:, r, i, :], SM[:, r, i, :], rs[:, r, i:i + 1],
                                                       None, ALU.mult)
                    last.then_inc(normed, 1)

                def residual(b):
                    dve.wait_ge(y_ps, b + 1)
                    dve.wait_ge(xb, b + 1)
                    nc.vector.tensor_tensor(R[:].rearrange("p t n -> p (t n)"), BD1[:],
                                            XB[:].rearrange("p t n -> p (t n)"), ALU.add).then_inc(r_sb, 1)
                    dve.wait_ge(r_sb, b + 1)
                    layernorm_stats(nc, chain, R, st, mv, ve, var, LN_EPS)

                def result(b):
                    dve.wait_ge(rstd_ok, b + 1)
                    at_least(dve, x.x1T_ps, b)
                    at_least(dve, x.x1b, b)
                    layernorm_apply(nc, R, mv, rstd, X1).then_inc(x1_ok, 1)

                def step(b, slots=range(H)):
                    for n in slots:
                        lagged(b, n, H, -LEAD, stage(0))
                        lagged(b, n, H, 0, maxima)
                        lagged(b, n, H, -LEAD, stage(1))
                        lagged(b, n, H, NORM, norm)
                        if n == PROJECT and exists(b - 1):
                            residual(b - 1)
                        if n == RESULT and exists(b - 1):
                            result(b - 1)
                        if n == CHUNK1 and exists(b):
                            chunk(b, 1)
                        if n == VALUES1 and exists(b):
                            values(b, 1)
                        if n == CHUNK0 and exists(b + 1):
                            chunk(b + 1, 0)
                        if n == VALUES0 and exists(b + 1):
                            values(b + 1, 0)
                        cross(b, n, lambda b, k: x.vector(dve, b, k, chain))

                step(-1, range(INPUT, H))
                step(0)
                step(1)
                step(2)
                start = chain.n
                with dve.Fori(3, B - 1) as b:
                    chain.start(start + LINKS * (b - 3))
                    step(b)
                    assert chain.n == LINKS, (chain.n, LINKS)
                chain.start(start + LINKS * (B - 4))
                for b in range(B - 1, B + 2):
                    step(b)

            @block.gpsimd
            def _(pool):
                nc.gpsimd.memset(neghalf[:], -0.5).then_inc(tp, 1)
                pool.wait_ge(tp, 1)
                pool.wait_ge(tv, 3)
                nc.gpsimd.tensor_tensor(rstd[:, 0:1], ve[:, 0:1], neghalf[:, 0:1], ALU.pow).then_inc(tp, 1)
                pool.wait_ge(tt, 3)

                def add_bias(b):
                    pool.wait_ge(xb_in, 16 * b + 16)
                    nc.gpsimd.tensor_tensor(XB[:], XB[:], broadcast_mid(row[:, 2, :], NT), ALU.add).then_inc(xb, 1)

                def chunk(b, c):
                    pool.wait_ge(k_sb, 2 * b + c + 1)
                    at_least(pool, sc_ps, 16 * (b - 1) + HC * (c + 1))
                    nc.gpsimd.tensor_tensor(kM[:, c * HC:(c + 1) * HC, :], broadcast_mid(kT[:, c, :], HC),
                                            broadcast_last(headmask[:], S), ALU.mult).then_inc(kM_sb, 1)

                def deviation(b):
                    pool.wait_ge(var, b + 1)
                    nc.gpsimd.tensor_tensor(rstd[:], ve[:], neghalf[:], ALU.pow).then_inc(rstd_ok, 1)

                def step(b, slots=range(H)):
                    for n in slots:
                        if n == PROJECT and exists(b - 1):
                            deviation(b - 1)
                        if n == CHUNK1 and exists(b):
                            chunk(b, 1)
                        if n == PROJECT + 4 and exists(b):
                            add_bias(b)
                        if n == CHUNK0 and exists(b + 1):
                            chunk(b + 1, 0)
                        cross(b, n, lambda b, k: x.pool(pool, b, k))

                step(-1, range(INPUT, H))
                step(0)
                step(1)
                step(2)
                with pool.Fori(3, B - 1) as b:
                    step(b)
                for b in range(B - 1, B + 2):
                    step(b)
        al.end()

E8 = 8


def most_tiles(top):
    return (T * top + E8 * (P - 1)) // P


def experts_phase(nc, d, name, top, DF, func, normed):
    TT = T // P
    GT = 4
    GROUPS = TT // GT
    ROOM = T + P
    group = lambda g: slice(GT * g, GT * (g + 1))
    FC = DF // P
    MT = most_tiles(top)
    with ExitStack() as phase:
        al = Alloc(nc, phase, name)
        sb, sem = al.sb, al.sem
        ident = sb("ident", [P, P])
        before = sb("before", [P, P])
        ones = sb("ones", [P, P])
        iota = sb("iota", [P, E8 + MT])
        neghalf = sb("neghalf", [P, TT])
        X = sb("X", [P, TT, D])
        XN = sb("XN", [P, TT, D]) if normed else X
        xT = sb("xT", [P, 2, KC, P])
        wr = sb("wr", [P, KC, E8])
        br = sb("br", [P, E8])
        gb = sb("gb", [P, 2, D]) if normed else None
        LG = sb("LG", [P, TT, E8])
        V8 = sb("V8", [P, TT, E8])
        I8 = sb("I8", [P, TT, E8], U32)
        IF = sb("IF", [P, TT, E8])
        EX = sb("EX", [P, TT, E8])
        V2 = sb("V2", [P, TT])
        SE = sb("SE", [P, TT])
        G = sb("G", [P, top, TT])
        OH = [sb(f"OH{k}", [P, TT, E8]) for k in range(top)]
        OHS = sb("OHS", [P, TT, E8]) if top > 1 else OH[0]
        TP = sb("TP", [P, TT + 1, E8])
        NI = sb("NI", [P, E8], I32)
        NF = sb("NF", [P, E8])
        OFF = sb("OFF", [P, E8 + 1])
        BASE = sb("BASE", [P, E8])
        PB = sb("PB", [P, TT, E8])
        SEL = sb("SEL", [P, TT, E8])
        PF = sb("PF", [P, top, TT])
        POS = sb("POS", [P, top, TT], U32)
        YPOS = sb("YPOS", [P, top, TT], U32)
        SHIFT = sb("SHIFT", [P, E8])
        CMP = sb("CMP", [P, MT, E8 - 1])
        EF = sb("EF", [P, MT])
        EI = sb("EI", [P, MT], I32)
        RF = sb("RF", [P, MT])
        RI = sb("RI", [P, MT], I32)
        LAST = sb("LAST", [P, 1])
        SKIP = sb("SKIP", [P, E8])
        ZF = sb("ZF", [P, E8])
        ZI = sb("ZI", [P, E8], I32)
        NEW = sb("NEW", [P, MT], I32)
        NEF = sb("NEF", [P, MT])
        Z = sb("Z", [P, D])
        W1 = [sb(f"W1_{i}", [P, KC, DF]) for i in range(2)]
        W2 = [sb(f"W2_{i}", [P, FC, D]) for i in range(2)]
        B1 = [sb(f"B1_{i}", [P, FC]) for i in range(2)]
        B2 = [sb(f"B2_{i}", [P, D]) for i in range(2)]
        XS = [sb(f"XS{i}", [P, D]) for i in range(2)]
        XST = [sb(f"XST{i}", [P, KC, P]) for i in range(2)]
        HT = [sb(f"HT{i}", [P, FC, P]) for i in range(2)]
        YS = [sb(f"YS{i}", [P, D]) for i in range(2)]
        YG = sb("YG", [P, top, TT, D])
        st = sb("st", [P, TT, 6])
        mv = sb("mv", [P, TT, 2])
        ve = sb("ve", [P, TT])
        rstd = sb("rstd", [P, TT])
        OUT = XN if normed else sb("OUT", [P, TT, D])

        banks = [al.bank(f"ps{i}") for i in range(8)]
        psT = banks[0:2]
        psH = banks[2:6]
        psY = banks[6:8]
        psL = banks[2:4]
        psR = banks[4:6]
        GE = GT * E8

        xs = nc.dram_tensor(name + "sorted", (E8 * ROOM, D), F32, kind="Internal").ap()
        ys = nc.dram_tensor(name + "results", (MT * P, D), F32, kind="Internal").ap()

        consts, zeros_out = sem("consts"), sem("zeros_out")
        x_in = [sem(f"x_in{g}") for g in range(GROUPS)]
        ez, eh = sem("zero_row"), sem("neghalf")
        rt_ps, rt_sb = sem("rt_ps"), sem("rt_sb")
        lg_ps, lg_sb, lg, ex, ranks = sem("lg_ps"), sem("lg_sb"), sem("lg"), sem("ex"), sem("ranks")
        oh, routed, placed, scattered = sem("oh"), sem("routed"), sem("placed"), sem("scattered")
        xn, var, rstd_ok = sem("xn"), sem("var"), sem("rstd")
        xs_in = [sem(f"xs_in{i}") for i in range(2)]
        w1_in = [sem(f"w1_in{i}") for i in range(2)]
        w2_in = [sem(f"w2_in{i}") for i in range(2)]
        xsT_ps, xsT_sb = sem("xsT_ps"), sem("xsT_sb")
        h_ps, h_sb, y_ps, y_sb = sem("h_ps"), sem("h_sb"), sem("y_ps"), sem("y_sb")
        y_out = [sem(f"y_out{i}") for i in range(2)]
        gathered = [sem(f"gathered{g}") for g in range(GROUPS)]
        out_ok, stored = sem("out"), sem("stored")
        dv, sp_waited, pool_waited = sem("dve_chain"), sem("sp_waited"), sem("pool_waited")
        STATS = GROUPS if normed else 0
        NB = FC // 4
        W1_PARTS, W2_PARTS = 2, 2
        assert MT % 2

        with nc.Block() as block:

            @block.sync
            def _(sp):
                for g in range(GROUPS):
                    sp.dma_start(X[:, group(g), :],
                                 d["x"].rearrange("(t p) n -> p t n", p=P)[:, group(g), :]).then_inc(x_in[g], 16)
                loads = [(ident[:], d["ident"]), (before[:], d["before"]), (iota[:], d["iota"][:, 0:E8 + MT]),
                         (wr[:], d["Wr"].rearrange("(k p) n -> p k n", p=P)),
                         (br[:], d["br"].partition_broadcast(P))]
                loads += [(gb[:], d["gb"].partition_broadcast(P))] if normed else [(V8[:, 0, :], d["iota"][:, 0:E8])]
                for dst, src in loads:
                    sp.dma_start(dst, src).then_inc(consts, 16)
                sp.wait_ge(ez, 1)
                sp.wait_ge(routed, 1)
                for e in range(E8):
                    row = sp.value_load(ZI[0:1, e:e + 1], min_val=0, max_val=E8 * ROOM - P)
                    sp.dma_start(xs[bass.ds(row, P), :], Z[:]).then_inc(zeros_out, 16)
                def first(n, i):
                    e = sp.value_load(EI[0:1, bass.ds(n, 1)], min_val=0, max_val=E8 - 1)
                    fresh = sp.value_load(NEW[0:1, bass.ds(n, 1)], min_val=0, max_val=1)
                    sp.dma_start(W1[i][:], d["W1"][e].rearrange("(k p) n -> p k n", p=P), cond=fresh,
                                 cond_hint=True).then_inc(w1_in[i], 16)
                    sp.dma_start(B1[i][:], d["b1"][e]).then_inc(w1_in[i], 16)

                def rows(n, i):
                    row = sp.value_load(RI[0:1, bass.ds(n, 1)], min_val=0, max_val=E8 * ROOM - P)
                    sp.dma_start(XS[i][:], xs[bass.ds(row, P), :]).then_inc(xs_in[i], 16)

                for n in range(2):
                    first(n, n)
                sp.wait_ge(zeros_out, 16 * E8)
                sp.wait_ge(scattered, 16 * TT * top)
                for n in range(2):
                    rows(n, n)

                def tile(n, i):
                    sp.wait_ge(xsT_ps, n - 1)
                    own_wait(sp, sp_waited)
                    rows(n, i)
                    sp.wait_ge(h_ps, NB * (n - 1))
                    sp.wait_ge(h_sb, NB * (n - 1))
                    own_wait(sp, sp_waited)
                    first(n, i)

                with sp.Fori(1, MT // 2) as m:
                    for i in range(2):
                        tile(2 * m + i, i)
                tile(MT - 1, 0)
                for g in range(GROUPS):
                    sp.wait_ge(out_ok, g + 1)
                    sp.dma_start(d["out"].rearrange("(t p) n -> p t n", p=P)[:, group(g), :],
                                 OUT[:, group(g), :]).then_inc(stored, 16)
                sp.wait_ge(stored, 16 * GROUPS)

            @block.tensor
            def _(pe):
                pe.wait_ge(consts, 96)

                def logits(t):
                    g = t // GT
                    pe.wait_ge(rt_sb, t + 1)
                    if t % GT == 0 and g >= 2:
                        pe.wait_ge(lg_sb, g - 1)
                    for k in range(KC):
                        last = nc.tensor.matmul(psL[g % 2][:, (t % GT) * E8:(t % GT + 1) * E8], xT[:, t % 2, k, :],
                                                wr[:, k, :], start=k == 0, stop=k == KC - 1)
                    if t % GT == GT - 1:
                        last.then_inc(lg_ps, 1)

                def count(g):
                    pe.wait_ge(oh, g + 1)
                    if g >= 2:
                        pe.wait_ge(placed, g - 1)
                    flat = OHS[:, group(g), :].rearrange("p t e -> p (t e)")
                    nc.tensor.matmul(psR[g % 2][:, 0:GE], before[:], flat, start=True, stop=True)
                    nc.tensor.matmul(psR[g % 2][:, GE:2 * GE], ones[:], flat, start=True, stop=True).then_inc(ranks, 1)

                for t in range(TT):
                    if normed and t % GT == 0:
                        pe.wait_ge(xn, t // GT + 1)
                    if t % GT == 0:
                        pe.wait_ge(x_in[t // GT], 16)
                    if t >= 2:
                        pe.wait_ge(rt_sb, t - 1)
                    for k in range(KC):
                        last = nc.tensor.transpose(psT[t % 2][:, k * P:(k + 1) * P], XN[:, t, k * P:(k + 1) * P], ident[:])
                    last.then_inc(rt_ps, 1)
                    if t >= 1:
                        logits(t - 1)
                    if t % GT == GT - 1 and t >= GT:
                        count(t // GT - 1)
                logits(TT - 1)
                count(GROUPS - 1)

                def transposes(n, i, j):
                    pe.wait_ge(xs_in[i], 16 * (j + 1))
                    at_least(pe, xsT_sb, n - 1)
                    for k in range(KC):
                        last = nc.tensor.transpose(psT[i][:, k * P:(k + 1) * P], XS[i][:, k * P:(k + 1) * P], ident[:])
                    last.then_inc(xsT_ps, 1)

                def up(n, i, j):
                    pe.wait_ge(w1_in[i], 16 * W1_PARTS * (j + 1))
                    pe.wait_ge(xsT_sb, n + 1)
                    for f in range(FC):
                        bank = psH[(i * NB + f // 4) % 4]
                        if f % 4 == 0:
                            at_least(pe, h_sb, (n - 4 // NB + 1) * NB if NB * 2 > 4 else NB * (n - 1))
                        for k in range(KC):
                            last = nc.tensor.matmul(bank[:, (f % 4) * P:(f % 4 + 1) * P], W1[i][:, k, f * P:(f + 1) * P],
                                                    XST[i][:, k, :], start=k == 0, stop=k == KC - 1)
                        if f % 4 == 3:
                            last.then_inc(h_ps, 1)

                def down(n, i, j):
                    pe.wait_ge(h_sb, NB * (n + 1))
                    pe.wait_ge(w2_in[i], 16 * W2_PARTS * (j + 1))
                    at_least(pe, y_sb, n - 1)
                    for f in range(FC):
                        last = nc.tensor.matmul(psY[i][:, 0:D], HT[i][:, f, :], W2[i][:, f, :],
                                                start=f == 0, stop=f == FC - 1)
                    last.then_inc(y_ps, 1)

                transposes(0, 0, 0)
                up(0, 0, 0)
                transposes(1, 1, 0)
                up(1, 1, 0)
                transposes(2, 0, 1)
                down(0, 0, 0)
                with pe.Fori(1, MT // 2) as m:
                    up(2 * m, 0, m)
                    transposes(2 * m + 1, 1, m)
                    down(2 * m - 1, 1, m - 1)
                    up(2 * m + 1, 1, m)
                    transposes(2 * m + 2, 0, m + 1)
                    down(2 * m, 0, m)
                up(MT - 1, 0, MT // 2)
                down(MT - 2, 1, MT // 2 - 1)
                down(MT - 1, 0, MT // 2)

            @block.scalar
            def _(act):
                for t in range(TT):
                    act.wait_ge(rt_ps, t + 1)
                    nc.scalar.activation(xT[:, t % 2, :, :].rearrange("p k n -> p (k n)"), psT[t % 2][:, 0:D],
                                         ACT.Copy).then_inc(rt_sb, 1)
                act.wait_ge(lg, 2)
                nc.scalar.activation(EX[:].rearrange("p t e -> p (t e)"), EX[:].rearrange("p t e -> p (t e)"),
                                     ACT.Exp).then_inc(ex, 1)
                nc.scalar.activation(V2[:], V2[:], ACT.Exp).then_inc(ex, 1)

                def copy_rows(n, i):
                    act.wait_ge(xsT_ps, n + 1)
                    nc.scalar.activation(XST[i][:].rearrange("p k n -> p (k n)"), psT[i][:, 0:D],
                                         ACT.Copy).then_inc(xsT_sb, 1)

                def up(n, i, j):
                    act.wait_ge(w1_in[i], 16 * W1_PARTS * (j + 1))
                    at_least(act, y_ps, n - 1)
                    for f in range(FC):
                        bank = psH[(i * NB + f // 4) % 4]
                        if f % 4 == 0:
                            act.wait_ge(h_ps, NB * n + f // 4 + 1)
                        last = nc.scalar.activation(HT[i][:, f, :], bank[:, (f % 4) * P:(f % 4 + 1) * P], func,
                                                    bias=B1[i][:, f:f + 1])
                        if f % 4 == 3:
                            last.then_inc(h_sb, 1)

                copy_rows(0, 0)
                for n in range(2):
                    up(n, n, 0)
                    copy_rows(n + 1, (n + 1) % 2)
                with act.Fori(1, MT // 2) as m:
                    for i in range(2):
                        up(2 * m + i, i, m)
                        copy_rows(2 * m + i + 1, 1 - i)
                up(MT - 1, 0, MT // 2)

            @block.vector
            def _(dve):
                chain = Chain(dve, dv)
                nc.vector.memset(Z[:], 0.0).then_inc(ez, 1)
                nc.vector.memset(ones[:], 1.0)
                chain.link(nc.vector.memset(TP[:, 0, :], 0.0))
                nc.vector.memset(OFF[:, 0:1], 0.0)
                dve.wait_ge(consts, 96)
                chain.link(nc.vector.tensor_scalar(BASE[:], iota[:, 0:E8], float(ROOM), None, ALU.mult))

                def stats(g):
                    dve.wait_ge(x_in[g], 16)
                    for t in range(GT * g, GT * (g + 1)):
                        last = nc.vector.bn_stats(st[:, t, :], X[:, t, :])
                    chain.link(last)
                    for t in range(GT * g, GT * (g + 1)):
                        last = nc.vector.bn_aggr(mv[:, t, :], st[:, t, :])
                    chain.link(last)
                    nc.vector.tensor_scalar(ve[:, group(g)], mv[:, group(g), 1], LN_EPS, None, ALU.add).then_inc(var, 1)

                def normalise(g):
                    dve.wait_ge(rstd_ok, g + 1)
                    for t in range(GT * g, GT * (g + 1)):
                        last = nc.vector.tensor_scalar(XN[:, t, :], X[:, t, :], mv[:, t, 0:1], rstd[:, t:t + 1],
                                                       ALU.subtract, ALU.mult)
                    chain.link(last)
                    part = XN[:, group(g), :]
                    chain.link(nc.vector.tensor_tensor(part, part, broadcast_mid(gb[:, 0, :], GT), ALU.mult))
                    nc.vector.tensor_tensor(part, part, broadcast_mid(gb[:, 1, :], GT), ALU.add).then_inc(xn, 1)

                def choose(g):
                    dve.wait_ge(lg_ps, g + 1)
                    nc.vector.tensor_tensor(LG[:, group(g), :], psL[g % 2][:, 0:GE].rearrange("p (t e) -> p t e", e=E8),
                                            broadcast_mid(br[:], GT), ALU.add).then_inc(lg_sb, 1)
                    dve.wait_ge(lg_sb, g + 1)
                    for t in range(GT * g, GT * (g + 1)):
                        last = nc.vector.max(V8[:, t, :], LG[:, t, :])
                    chain.link(last)
                    for t in range(GT * g, GT * (g + 1)):
                        last = nc.vector.max_index(I8[:, t, :], V8[:, t, :], LG[:, t, :])
                    chain.link(last)
                    chain.link(nc.vector.tensor_copy(IF[:, group(g), :], I8[:, group(g), :]))
                    for k in range(top):
                        last = nc.vector.tensor_tensor(OH[k][:, group(g), :], broadcast_mid(iota[:, 0:E8], GT),
                                                       broadcast_last(IF[:, group(g), k], E8), ALU.is_equal)
                    if top > 1:
                        chain.link(last)
                        last = nc.vector.tensor_tensor(OHS[:, group(g), :], OH[0][:, group(g), :],
                                                       OH[1][:, group(g), :], ALU.add)
                    last.then_inc(oh, 1)

                def place(g):
                    dve.wait_ge(ranks, g + 1)
                    for t in range(GT):
                        chain.link(nc.vector.tensor_tensor(TP[:, GT * g + t + 1, :], TP[:, GT * g + t, :],
                                                           psR[g % 2][:, GE + t * E8:GE + (t + 1) * E8], ALU.add))
                    part = PB[:, group(g), :]
                    chain.link(nc.vector.tensor_tensor(part, TP[:, group(g), :],
                                                       psR[g % 2][:, 0:GE].rearrange("p (t e) -> p t e", e=E8), ALU.add))
                    chain.link(nc.vector.tensor_tensor(part, part, broadcast_mid(BASE[:], GT), ALU.add))
                    for k in range(top):
                        chain.link(nc.vector.tensor_tensor(SEL[:, group(g), :], part, OH[k][:, group(g), :], ALU.mult))
                        chain.link(nc.vector.tensor_reduce(PF[:, k, group(g)], SEL[:, group(g), :], AXX, ALU.add))
                    nc.vector.tensor_copy(POS[:, :, group(g)], PF[:, :, group(g)]).then_inc(placed, 1)

                if normed:
                    for g in range(GROUPS):
                        stats(g)
                for g in range(GROUPS + 2):
                    if normed and g < GROUPS:
                        normalise(g)
                    if 1 <= g <= GROUPS:
                        choose(g - 1)
                    if g >= 2:
                        place(g - 2)
                nc.vector.tensor_tensor(EX[:], LG[:], broadcast_last(V8[:, :, 0], E8), ALU.subtract).then_inc(lg, 1)
                nc.vector.tensor_tensor(V2[:], V8[:, :, 1], V8[:, :, 0], ALU.subtract).then_inc(lg, 1)
                chain.link(nc.vector.tensor_scalar(NF[:], TP[:, TT, :], float(P - 1), None, ALU.add))
                nc.vector.tensor_tensor(ZF[:], TP[:, TT, :], BASE[:], ALU.add)
                chain.link(nc.vector.tensor_copy(NI[:], NF[:]))
                shift = P.bit_length() - 1
                nc.vector.tensor_copy(ZI[:], ZF[:])
                chain.link(nc.vector.tensor_scalar(NI[:], NI[:], shift, shift, ALU.arith_shift_right,
                                                   ALU.logical_shift_left))
                chain.link(nc.vector.tensor_copy(NF[:], NI[:]))
                nc.vector.tensor_scalar(SKIP[:], NF[:], -1.0, float(ROOM), ALU.mult, ALU.add)
                for e in range(E8):
                    chain.link(nc.vector.tensor_tensor(OFF[:, e + 1:e + 2], OFF[:, e:e + 1], NF[:, e:e + 1], ALU.add))
                tile_rows = iota[:, E8:E8 + MT]
                chain.link(nc.vector.tensor_tensor(CMP[:], broadcast_mid(OFF[:, 1:E8], MT),
                                                   broadcast_last(tile_rows, E8 - 1), ALU.is_le))
                chain.link(nc.vector.tensor_reduce(EF[:], CMP[:], AXX, ALU.add))
                nc.vector.tensor_copy(EI[:], EF[:])
                chain.link(nc.vector.tensor_tensor(CMP[:], CMP[:], broadcast_mid(SKIP[:, 0:E8 - 1], MT), ALU.mult))
                chain.link(nc.vector.tensor_reduce(RF[:], CMP[:], AXX, ALU.add))
                chain.link(nc.vector.tensor_tensor(RF[:], RF[:], tile_rows, ALU.add))
                chain.link(nc.vector.tensor_scalar(LAST[:], NF[:, E8 - 1:E8], float(P), float((E8 - 1) * ROOM),
                                                   ALU.max, ALU.add))
                chain.link(nc.vector.tensor_scalar(LAST[:], LAST[:], float(-P), None, ALU.add))
                chain.link(nc.vector.tensor_scalar(RF[:], RF[:], LAST[:], None, ALU.min))
                nc.vector.tensor_copy(RI[:], RF[:])
                nc.vector.memset(NEF[:, 0:2], 1.0)
                chain.link(nc.vector.tensor_tensor(NEF[:, 2:MT], EF[:, 2:MT], EF[:, 0:MT - 2], ALU.not_equal))
                nc.vector.tensor_copy(NEW[:], NEF[:]).then_inc(routed, 1)
                chain.link(nc.vector.tensor_tensor(SHIFT[:], OFF[:, 0:E8], BASE[:], ALU.subtract))
                chain.link(nc.vector.tensor_tensor(PB[:], PB[:], broadcast_mid(SHIFT[:], TT), ALU.add))
                for k in range(top):
                    chain.link(nc.vector.tensor_tensor(SEL[:], PB[:], OH[k][:], ALU.mult))
                    chain.link(nc.vector.tensor_reduce(PF[:, k, :], SEL[:], AXX, ALU.add))
                nc.vector.tensor_copy(YPOS[:], PF[:]).then_inc(placed, 1)
                dve.wait_ge(ex, 2)
                chain.link(nc.vector.tensor_reduce(SE[:], EX[:], AXX, ALU.add))
                chain.link(nc.vector.reciprocal(G[:, 0, :], SE[:]))
                if top > 1:
                    chain.link(nc.vector.tensor_tensor(G[:, 1, :], G[:, 0, :], V2[:], ALU.mult))
                    chain.link(nc.vector.scalar_tensor_tensor(out=SE[:], in0=G[:, 0, :], scalar=1e-8, in1=G[:, 1, :],
                                                              op0=ALU.add, op1=ALU.add))
                    chain.link(nc.vector.reciprocal(V2[:], SE[:]))
                    chain.link(nc.vector.tensor_tensor(G[:], G[:], broadcast_mid(V2[:], top), ALU.mult))

                def down(n, i, j):
                    dve.wait_ge(y_ps, n + 1)
                    dve.wait_ge(w2_in[i], 16 * W2_PARTS * (j + 1))
                    at_least(dve, y_out[i], 16 * j)
                    nc.vector.tensor_tensor(YS[i][:], psY[i][:, 0:D], B2[i][:], ALU.add).then_inc(y_sb, 1)

                if normed:
                    chain.link(nc.vector.tensor_scalar(X[:], X[:], 2.0, None, ALU.mult))

                down(0, 0, 0)
                down(1, 1, 0)
                with dve.Fori(1, MT // 2) as m:
                    down(2 * m, 0, m)
                    down(2 * m + 1, 1, m)
                if MT % 2:
                    down(MT - 1, 0, MT // 2)
                def combine(g):
                    dve.wait_ge(gathered[g], 16 * top * GT)
                    for k in range(top):
                        for t in range(GT * g, GT * (g + 1)):
                            last = nc.vector.scalar_tensor_tensor(out=X[:, t, :], in0=YG[:, k, t, :],
                                                                  scalar=G[:, k, t:t + 1], in1=X[:, t, :],
                                                                  op0=ALU.mult, op1=ALU.add)
                        chain.link(last)
                    for t in range(GT * g, GT * (g + 1)):
                        last = nc.vector.bn_stats(st[:, t, :], X[:, t, :])
                    chain.link(last)
                    for t in range(GT * g, GT * (g + 1)):
                        last = nc.vector.bn_aggr(mv[:, t, :], st[:, t, :])
                    chain.link(last)
                    nc.vector.tensor_scalar(ve[:, group(g)], mv[:, group(g), 1], LN_EPS, None, ALU.add).then_inc(var, 1)

                def result(g):
                    dve.wait_ge(rstd_ok, STATS + g + 1)
                    for t in range(GT * g, GT * (g + 1)):
                        last = nc.vector.tensor_scalar(OUT[:, t, :], X[:, t, :], mv[:, t, 0:1], rstd[:, t:t + 1],
                                                       ALU.subtract, ALU.mult)
                    last.then_inc(out_ok, 1)

                for g in range(GROUPS):
                    combine(g)
                    if g >= 2:
                        result(g - 2)
                result(GROUPS - 2)
                result(GROUPS - 1)

            @block.gpsimd
            def _(pool):
                nc.gpsimd.memset(neghalf[:], -0.5).then_inc(eh, 1)
                pool.wait_ge(eh, 1)

                def deviation(g, n):
                    pool.wait_ge(var, n)
                    nc.gpsimd.tensor_tensor(rstd[:, group(g)], ve[:, group(g)], neghalf[:, group(g)],
                                            ALU.pow).then_inc(rstd_ok, 1)

                if normed:
                    for g in range(GROUPS):
                        deviation(g, g + 1)
                for g in range(GROUPS):
                    if normed:
                        pool.wait_ge(xn, g + 1)
                    pool.wait_ge(x_in[g], 16)
                    pool.wait_ge(placed, g + 1)
                    for t in range(GT * g, GT * (g + 1)):
                        for k in range(top):
                            nc.gpsimd.indirect_dma_start(xs, bass.IndirectOffsetOnAxis(POS[:, k, t:t + 1], 0),
                                                         XN[:, t, :], None).then_inc(scattered, 16)
                pool.wait_ge(routed, 1)

                def second(n, i):
                    e = pool.value_load(EI[0:1, bass.ds(n, 1)], min_val=0, max_val=E8 - 1)
                    fresh = pool.value_load(NEW[0:1, bass.ds(n, 1)], min_val=0, max_val=1)
                    at_least(pool, y_ps, n - 1)
                    at_least(pool, y_sb, n - 1)
                    own_wait(pool, pool_waited)
                    pool.dma_start(W2[i][:], d["W2"][e].rearrange("(k p) n -> p k n", p=P), cond=fresh,
                                   cond_hint=True).then_inc(w2_in[i], 16)
                    pool.dma_start(B2[i][:], d["b2"][e].partition_broadcast(P)).then_inc(w2_in[i], 16)

                def store(n, i):
                    pool.wait_ge(y_sb, n + 1)
                    own_wait(pool, pool_waited)
                    pool.dma_start(ys.rearrange("(m p) n -> m p n", p=P)[n], YS[i][:]).then_inc(y_out[i], 16)

                second(0, 0)
                second(1, 1)
                store(0, 0)
                with pool.Fori(1, MT // 2) as m:
                    second(2 * m, 0)
                    store(2 * m - 1, 1)
                    second(2 * m + 1, 1)
                    store(2 * m, 0)
                if MT % 2:
                    second(MT - 1, 0)
                    store(MT - 2, 1)
                    store(MT - 1, 0)
                else:
                    store(MT - 1, 1)
                pool.wait_ge(y_out[0], 16 * ((MT + 1) // 2))
                pool.wait_ge(y_out[1], 16 * (MT // 2))
                pool.wait_ge(placed, GROUPS + 1)
                for g in range(GROUPS):
                    for t in range(GT * g, GT * (g + 1)):
                        for k in range(top):
                            nc.gpsimd.indirect_dma_start(YG[:, k, t, :], None, ys,
                                                         bass.IndirectOffsetOnAxis(YPOS[:, k, t:t + 1], 0)).then_inc(gathered[g], 16)
                    if g:
                        deviation(g - 1, STATS + g)
                deviation(GROUPS - 1, STATS + GROUPS)
        al.end()

DH = 64
PM = 16
CH = H * DH // P
INNER = H * DH
RMS_EPS = 1e-6


def segment_attention_phase(nc, d):
    with ExitStack() as phase:
        al = Alloc(nc, phase, "c_")
        sb, sem = al.sb, al.sem
        scale = float(DH) ** -0.5
        NK = PM + P
        RING = 8

        FR0, FR1, QK, RT, SC0, SC1, PTB, PO = [al.bank(n) for n in
                                               ("FR0", "FR1", "QK", "RT", "SC0", "SC1", "PTB", "PO")]
        SC = [SC0, SC1]
        ident = sb("ident", [P, P])
        headmask = sb("headmask", [P, HC])
        col = sb("col", [P, 6])
        row = sb("row", [P, 3, D])
        cs = sb("cs", [P, 2, 2, S])
        rot = sb("rot", [P, P])
        mask = sb("mask", [P, NK])
        neghalf = sb("neghalf", [P, NT])
        wqkv = sb("wqkv", [P, KC, 3 * INNER])
        wout = sb("wout", [P, CH, D])
        XIN = sb("XIN", [P, NT, D])
        XB = sb("XB", [P, NT, D])
        XR = sb("XR", [P, NT, D])
        xT = sb("xT", [P, KC, S])
        raw, t1, t2 = [[sb(f"{n}{i}", [P, 2, S]) for i in range(2)] for n in ("raw", "t1", "t2")]
        qT = sb("qT", [P, CH, S])
        kP = sb("kP", [P, CH, 2, NT, NK])
        v = sb("v", [P, NT, INNER])
        vpm = sb("vpm", [P, 2, 8 * DH])
        SM = sb("SM", [P, RING, NK])
        PP = sb("PP", [P, 2, 8 * PM])
        nb = sb("nb", [P, RING])
        sm = sb("sm", [P, RING])
        rs = sb("rs", [P, RING])
        PTr = sb("PTr", [P, 16, P])
        PPT = sb("PPT", [P, 2, P])
        OT = sb("OT", [P, CH, S])
        R = sb("R", [P, NT, D])
        sq = sb("sq", [P, NT, D])
        ss = sb("ss", [P, NT])
        ms = sb("ms", [P, NT])
        rr = sb("rr", [P, NT])
        st = sb("st", [P, NT, 6])
        mv = sb("mv", [P, NT, 2])
        ve = sb("ve", [P, NT])
        rstd = sb("rstd", [P, NT])
        X1 = sb("X1", [P, NT, D])
        a = {"ident": ident, "headmask": headmask, "neghalf": neghalf, "X1": X1,
             "ctxT": d["ctxT"], "x2_out": d["x5"],
             "xbq": col[:, 2:4], "xbk": col[:, 4:6], "xbv": row[:, 1, :], "xbo": row[:, 2, :]}
        consts, zeroed, hv = sem("consts"), sem("zeroed"), sem("neghalf")
        x_in = sem("x_in")
        ms_ok, rr_ok, xr, xr_ps, xT_sb = sem("ms"), sem("rr"), sem("xr"), sem("xr_ps"), sem("xT_sb")
        qk_ps, raw_sb, t1_sb, rot_ps, t2_sb, q_sb, k_sb = (sem("qk_ps"), sem("raw_sb"), sem("t1_sb"), sem("rot_ps"),
                                                            sem("t2_sb"), sem("q_sb"), sem("k_sb"))
        v_ps, v_sb, xb = sem("v_ps"), sem("v_sb"), sem("xb")
        sc_ps, maxed, exped, normed = sem("sc_ps"), sem("maxed"), sem("exped"), sem("normed")
        pT_ps, pT_sb, pp_ps, pp_sb, o_ps, o_sb = (sem("pT_ps"), sem("pT_sb"), sem("pp_ps"), sem("pp_sb"),
                                                  sem("o_ps"), sem("o_sb"))
        y_ps, r_sb, var, rstd_ok, x1_ok = sem("y_ps"), sem("r_sb"), sem("var"), sem("rstd"), sem("x1")
        dv, waited, sp_waited = sem("dve_chain"), sem("dve_waited"), sem("sp_waited")
        U = NT * H
        order = [(w, 8 * o + h) for o in range(2) for w in range(NT) for h in range(8)]
        x = Cross(al, a, d["L1_xattn"], False, x1_ok, [FR0, FR1])
        LINKS = 1 + U + 2 + x.VECTOR_LINKS

        def chunk_at(n):
            return (n % 16) // 4 + (CH // 2 if n < 16 else 0) if n % 4 == 0 else None

        def values_at(n):
            return (n % 16 - 9) // 4 + (2 if n < 16 else 0) if n % 16 in (9, 13) else None

        NORM, TRANSPOSE, OUTPUT, COPY_O, PROJECT, RESIDUAL, RESULT = 2, 5, 6, 7, 8, 9, 10
        CROSS = {}
        for k in range(x.STEPS):
            CROSS.setdefault(RESULT + 1 + (7 * k // 6 if k < x.PAIRS[0] else 12 + (k - x.PAIRS[0]) * 4 // 3), []).append(k)

        with nc.Block() as block:

            @block.sync
            def _(sp):
                for dst, src in ((ident[:], d["ident"]), (headmask[:], d["headmask"]), (col[:], d["L1_col"]),
                                 (row[:], d["L1_row"].partition_broadcast(P)), (cs[:], d["cossin"]),
                                 (rot[:], d["rot"]), (mask[:], d["mask"]),
                                 (wqkv[:], d["w_qkv"].rearrange("(k p) n -> p k n", p=P)),
                                 (wout[:], d["w_out"].rearrange("(k p) n -> p k n", p=P))):
                    sp.dma_start(dst, src).then_inc(consts, 16)
                sp.wait_ge(zeroed, 2)
                pmk = d["pm_kT"].rearrange("(c u n) k -> u n c k", u=2, n=DH)
                for u in range(2):
                    for w in range(NT):
                        sp.dma_start(kP[u * DH:(u + 1) * DH, :, u, w, 0:PM], pmk[u]).then_inc(consts, 16)
                for h in range(H):
                    sp.dma_start(vpm[(h % 8) * PM:(h % 8 + 1) * PM, h // 8, (h % 8) * DH:(h % 8 + 1) * DH],
                                 d["pm_v"][h]).then_inc(consts, 16)
                x.load_weights(sp)

                def load_x(b):
                    at_least(sp, xb, b)
                    at_least(sp, xr, b)
                    own_wait(sp, sp_waited)
                    sp.dma_start(XIN[:], d["x"][b].rearrange("(t p) n -> p t n", p=P)).then_inc(x_in, 16)

                load_x(0)
                def step(b, first=False):
                    load_x(b + 1)
                    x.load_ctx(sp, b)
                    if not first:
                        x.store(sp, b - 1)

                step(0, first=True)
                step(1)
                with sp.Fori(2, B - 1) as b:
                    step(b)
                x.load_ctx(sp, B - 1)
                for b in range(B - 2, B):
                    x.store(sp, b)
                sp.wait_ge(x.stored, 16 * B)

            ALL_CONSTS = 16 * (9 + 4 + H)

            @block.tensor
            def _(pe):
                pe.wait_ge(consts, ALL_CONSTS)
                pe.wait_ge(x.weights, x.WEIGHTS)

                def front_input(b):
                    pe.wait_ge(xr, b + 1)
                    at_least(pe, v_sb, 4 * b)
                    for t in range(NT):
                        for k in range(KC):
                            last = nc.tensor.transpose(QK[:, k * S + t * P:k * S + (t + 1) * P],
                                                       XR[:, t, k * P:(k + 1) * P], ident[:])
                    last.then_inc(xr_ps, 1)

                def project(b, c):
                    if c == 0:
                        pe.wait_ge(xT_sb, b + 1)
                    else:
                        pe.wait_ge(raw_sb, CH * b + c)
                    if c % 4 == 3 or c == 4:
                        pe.wait_ge(v_sb, 4 * b + (2 if c == 4 else 2 * (c // 4) + 1))
                    for n in range(2):
                        for k in range(KC):
                            last = nc.tensor.matmul(QK[:, n * S:(n + 1) * S],
                                                    wqkv[:, k, n * INNER + c * P:n * INNER + (c + 1) * P],
                                                    xT[:, k, :], start=k == 0, stop=k == KC - 1)
                    last.then_inc(qk_ps, 1)

                def rotate(b, c):
                    pe.wait_ge(raw_sb, CH * b + c + 1)
                    at_least(pe, t2_sb, CH * b + c)
                    nc.tensor.matmul(RT[:], rot[:], raw[c % 2][:].rearrange("p a s -> p (a s)"),
                                     start=True, stop=True).then_inc(rot_ps, 1)

                def values(b, n):
                    pe.wait_ge(raw_sb, CH * b + 4 * (n // 2) + 3 + n % 2)
                    for k in range(KC):
                        last = nc.tensor.matmul(QK[:], xT[:, k, (n % 2) * P:(n % 2 + 1) * P],
                                                wqkv[:, k, 2 * INNER + (n // 2) * 512:2 * INNER + (n // 2 + 1) * 512],
                                                start=k == 0, stop=k == KC - 1)
                    last.then_inc(v_ps, 1)

                def front(b, n):
                    if chunk_at(n) is not None:
                        project(b, chunk_at(n))
                    if n >= 1 and chunk_at(n - 1) is not None:
                        rotate(b, chunk_at(n - 1))
                    if values_at(n) is not None:
                        values(b, values_at(n))

                def scores(b, n):
                    w, h = order[n]
                    if w == 0 and h % 2 == 0:
                        pe.wait_ge(q_sb, CH * b + h // 2 + 1)
                        pe.wait_ge(k_sb, CH * b + h // 2 + 1)
                    at_least(pe, maxed, U * b + n - 1)
                    nc.tensor.matmul(SC[n % 2][:, 0:NK], qT[:, h // 2, w * P:(w + 1) * P], kP[:, h // 2, h % 2, w, :],
                                     start=True, stop=True).then_inc(sc_ps, 1)

                def transposes(b, n):
                    pe.wait_ge(normed, U * b + n + 1)
                    at_least(pe, pT_sb, U * b + n)
                    if n % 8 == 7:
                        at_least(pe, pp_sb, U // 8 * b + n // 8)
                        nc.tensor.transpose(PTB[:, P:2 * P], PP[:, (n // 8) % 2, :], ident[:]).then_inc(pp_ps, 1)
                    nc.tensor.transpose(PTB[:, 0:P], SM[:, n % RING, PM:NK], ident[:]).then_inc(pT_ps, 1)

                def outputs(b, n):
                    if n % 8 != 7:
                        return
                    m = n // 8
                    pe.wait_ge(pT_sb, U * b + n + 1)
                    pe.wait_ge(pp_sb, U // 8 * b + m + 1)
                    pe.wait_ge(v_sb, 4 * b + m + 1)
                    if m == 0:
                        at_least(pe, r_sb, b)
                    at_least(pe, o_sb, U // 8 * b + m)
                    for j in range(8):
                        w, h = order[8 * m + j]
                        dst = PO[(h % 2) * DH:(h % 2 + 1) * DH, (j // 2) * P:(j // 2 + 1) * P]
                        nc.tensor.matmul(dst, v[:, w, h * DH:(h + 1) * DH], PTr[:, 8 * (m % 2) + j, :],
                                         start=True, stop=False)
                        last = nc.tensor.matmul(dst, vpm[:, h // 8, (h % 8) * DH:(h % 8 + 1) * DH], PPT[:, m % 2, :],
                                                start=False, stop=True)
                    last.then_inc(o_ps, 1)

                def output_projection(b, n):
                    if n != U - 1:
                        return
                    pe.wait_ge(o_sb, U // 8 * (b + 1))
                    for t in range(NT):
                        for c in range(CH):
                            last = nc.tensor.matmul(PO[:, t * D:(t + 1) * D], OT[:, c, t * P:(t + 1) * P],
                                                    wout[:, c, :], start=c == 0, stop=c == CH - 1)
                    last.then_inc(y_ps, 1)

                def behind(b, n):
                    lagged(b, n, U, TRANSPOSE, transposes)
                    lagged(b, n, U, OUTPUT, outputs)
                    lagged(b, n, U, PROJECT, output_projection)

                def step(b, first=False, last=False):
                    for n in range(U):
                        scores(b, n)
                        behind(b, n)
                        if n < 16:
                            front(b, n)
                        if n == 14 and not last:
                            front_input(b + 1)
                        if n >= 16 and not last:
                            front(b + 1, n)
                        if not first:
                            for k in CROSS.get(n, ()):
                                x.tensor(pe, b - 1, k)

                front_input(0)
                for n in range(16, U):
                    front(0, n)
                step(0, first=True)
                step(1)
                with pe.Fori(2, B - 1) as b:
                    step(b)
                step(B - 1, last=True)
                for n in range(PROJECT + 1):
                    behind(B, n)
                for k in range(x.STEPS):
                    x.tensor(pe, B - 1, k)

            @block.scalar
            def _(act):
                act.wait_ge(consts, ALL_CONSTS)

                def front_input(b):
                    act.wait_ge(xr_ps, b + 1)
                    for k in range(KC):
                        last = nc.scalar.activation(xT[:, k, :], QK[:, k * S:(k + 1) * S], ACT.Copy,
                                                    scale=col[:, k:k + 1])
                    last.then_inc(xT_sb, 1)

                def front(b, n):
                    c, m = chunk_at(n), values_at(n)
                    if c is not None:
                        act.wait_ge(qk_ps, CH * b + c + 1)
                        at_least(act, rot_ps, CH * b + c - 1)
                        at_least(act, t1_sb, CH * b + c - 1)
                        nc.scalar.activation(raw[c % 2][:].rearrange("p a s -> p (a s)"), QK[:],
                                             ACT.Copy).then_inc(raw_sb, 1)
                    if m is not None:
                        act.wait_ge(v_ps, 4 * b + m + 1)
                        at_least(act, o_ps, 4 * (b - 1) + 2 * (m // 2) + 2)
                        nc.scalar.activation(v[:, m % 2, (m // 2) * 512:(m // 2 + 1) * 512], QK[:],
                                             ACT.Copy).then_inc(v_sb, 1)

                def exps(b, n):
                    r = n % RING
                    act.wait_ge(maxed, U * b + n + 1)
                    nc.scalar.activation(SM[:, r, :], SM[:, r, :], ACT.Exp, bias=nb[:, r:r + 1],
                                         scale=-1.0, accum_out=sm[:, r:r + 1]).then_inc(exped, 1)

                def copy_pT(b, n):
                    act.wait_ge(pT_ps, U * b + n + 1)
                    if n % 8 == 0:
                        at_least(act, o_ps, U // 8 * b + n // 8 - 1)
                    if n % 8 == 7:
                        nc.scalar.activation(PPT[:, (n // 8) % 2, :], PTB[:, P:2 * P], ACT.Copy).then_inc(pp_sb, 1)
                    nc.scalar.activation(PTr[:, n % 16, :], PTB[:, 0:P], ACT.Copy).then_inc(pT_sb, 1)

                def copy_o(b, n):
                    if n % 8 != 7:
                        return
                    m = n // 8
                    act.wait_ge(o_ps, U // 8 * b + m + 1)
                    if m == 0:
                        at_least(act, y_ps, b)
                    w, h = order[8 * m]
                    nc.scalar.activation(OT[:, h // 2:h // 2 + 4, w * P:(w + 1) * P],
                                         PO[:].rearrange("p (c s) -> p c s", c=4), ACT.Copy).then_inc(o_sb, 1)

                def behind(b, n):
                    lagged(b, n, U, TRANSPOSE, copy_pT)
                    lagged(b, n, U, COPY_O, copy_o)

                def step(b, first=False, last=False):
                    for n in range(U):
                        behind(b, n)
                        exps(b, n)
                        if n < 16:
                            front(b, n)
                        if n == 14 and not last:
                            front_input(b + 1)
                        if n >= 16 and not last:
                            front(b + 1, n)
                        if not first:
                            for k in CROSS.get(n, ()):
                                x.scalar(act, b - 1, k)

                front_input(0)
                for n in range(16, U):
                    front(0, n)
                step(0, first=True)
                step(1)
                with act.Fori(2, B - 1) as b:
                    step(b)
                step(B - 1, last=True)
                for n in range(COPY_O + 1):
                    behind(B, n)
                for k in range(x.STEPS):
                    x.scalar(act, B - 1, k)

            @block.vector
            def _(dve):
                chain = Chain(dve, dv, waited)
                nc.vector.memset(kP[:], 0.0).then_inc(zeroed, 1)
                nc.vector.memset(vpm[:], 0.0).then_inc(zeroed, 1)
                nc.vector.memset(x.wo[:], 0.0).then_inc(x.zeroed, 1)
                nc.vector.memset(x.v[:], 0.0).then_inc(x.zeroed, 1)
                dve.wait_ge(consts, ALL_CONSTS)

                def squares(b):
                    dve.wait_ge(x_in, 16 * b + 16)
                    own_wait(dve, waited)
                    for t in range(NT):
                        last = nc.vector.tensor_tensor_reduce(out=sq[:, t, :], in0=XIN[:, t, :], in1=XIN[:, t, :],
                                                              scale=1.0, scalar=0.0, op0=ALU.mult, op1=ALU.add,
                                                              accum_out=ss[:, t:t + 1])
                    chain.link(last)
                    nc.vector.tensor_scalar(ms[:], ss[:], 1.0 / D, RMS_EPS, ALU.mult, ALU.add).then_inc(ms_ok, 1)

                def rms_scaled(b):
                    dve.wait_ge(rr_ok, b + 1)
                    for t in range(NT):
                        last = nc.vector.tensor_scalar(XR[:, t, :], XIN[:, t, :], rr[:, t:t + 1], None, ALU.mult)
                    last.then_inc(xr, 1)

                def front(b, n):
                    if n >= 1 and chunk_at(n - 1) is not None:
                        c = chunk_at(n - 1)
                        at_least(dve, q_sb, CH * b + c - 1)
                        dve.wait_ge(rot_ps, CH * b + c + 1)
                        nc.vector.tensor_tensor(t2[c % 2][:].rearrange("p a s -> p (a s)"), RT[:],
                                                cs[:, 1, :, :].rearrange("p a s -> p (a s)"), ALU.mult).then_inc(t2_sb, 1)
                    if n >= 2 and chunk_at(n - 2) is not None:
                        c = chunk_at(n - 2)
                        dve.wait_ge(t2_sb, CH * b + c + 1)
                        dve.wait_ge(t1_sb, CH * b + c + 1)
                        if c % 4 == 0:
                            at_least(dve, sc_ps, U * (b - 1) + (c // 4 + 1) * 16)
                        for u in range(2):
                            r = slice(u * DH, (u + 1) * DH)
                            last = nc.vector.tensor_tensor(kP[r, c, u, :, PM:NK],
                                                           t1[c % 2][r, 1, :].rearrange("p (w s) -> p w s", w=NT),
                                                           t2[c % 2][r, 1, :].rearrange("p (w s) -> p w s", w=NT), ALU.add)
                        last.then_inc(k_sb, 1)

                def maxima(b, n):
                    r = n % RING
                    dve.wait_ge(sc_ps, U * b + n + 1)
                    at_least(dve, pT_ps, U * b + n + 1 - RING)
                    own_wait(dve, waited)
                    nc.vector.tensor_tensor_reduce(out=SM[:, r, :], in0=SC[n % 2][:, 0:NK], in1=mask[:],
                                                   scale=-scale, scalar=3.0e38, op0=ALU.add, op1=ALU.min,
                                                   accum_out=nb[:, r:r + 1]).then_inc(maxed, 1)

                def norm(b, n):
                    r = n % RING
                    dve.wait_ge(exped, U * b + n + 1)
                    chain.link(nc.vector.reciprocal(rs[:, r:r + 1], sm[:, r:r + 1]))
                    if n % 8 == 0:
                        at_least(dve, pp_ps, U // 8 * b + n // 8 - 1)
                    nc.vector.tensor_scalar(PP[:, (n // 8) % 2, (n % 8) * PM:(n % 8 + 1) * PM], SM[:, r, 0:PM],
                                            rs[:, r:r + 1], None, ALU.mult)
                    nc.vector.tensor_scalar(SM[:, r, PM:NK], SM[:, r, PM:NK], rs[:, r:r + 1],
                                            None, ALU.mult).then_inc(normed, 1)

                def residual(b, n):
                    if n != U - 1:
                        return
                    dve.wait_ge(y_ps, b + 1)
                    dve.wait_ge(xb, b + 1)
                    nc.vector.tensor_tensor(R[:].rearrange("p t n -> p (t n)"), PO[:],
                                            XB[:].rearrange("p t n -> p (t n)"), ALU.add).then_inc(r_sb, 1)
                    dve.wait_ge(r_sb, b + 1)
                    layernorm_stats(nc, chain, R, st, mv, ve, var, LN_EPS)

                def result(b, n):
                    if n != U - 1:
                        return
                    dve.wait_ge(rstd_ok, b + 1)
                    at_least(dve, x.x1T_ps, b)
                    at_least(dve, x.x1b, b)
                    layernorm_apply(nc, R, mv, rstd, X1).then_inc(x1_ok, 1)

                def behind(b, n):
                    lagged(b, n, U, NORM, norm)
                    lagged(b, n, U, RESIDUAL, residual)
                    lagged(b, n, U, RESULT, result)

                def step(b, first=False, last=False):
                    for n in range(U):
                        maxima(b, n)
                        behind(b, n)
                        if n < 16:
                            front(b, n)
                        if n == 11 and not last:
                            squares(b + 1)
                        if n == 12 and not last:
                            rms_scaled(b + 1)
                        if n >= 16 and not last:
                            front(b + 1, n)
                        if not first:
                            for k in CROSS.get(n, ()):
                                x.vector(dve, b - 1, k, chain)

                squares(0)
                rms_scaled(0)
                for n in range(16, U):
                    front(0, n)
                step(0, first=True)
                step(1)
                start = chain.n
                with dve.Fori(2, B - 1) as b:
                    chain.start(start + LINKS * (b - 2))
                    step(b)
                    assert chain.n == LINKS, (chain.n, LINKS)
                chain.start(start + LINKS * (B - 3))
                step(B - 1, last=True)
                for n in range(RESULT + 1):
                    behind(B, n)
                for k in range(x.STEPS):
                    x.vector(dve, B - 1, k, chain)

            @block.gpsimd
            def _(pool):
                nc.gpsimd.memset(neghalf[:], -0.5).then_inc(hv, 1)
                pool.wait_ge(hv, 1)
                pool.wait_ge(consts, ALL_CONSTS)

                def rms(b):
                    pool.wait_ge(ms_ok, b + 1)
                    nc.gpsimd.tensor_tensor(rr[:], ms[:], neghalf[:], ALU.pow).then_inc(rr_ok, 1)

                def add_bias(b):
                    at_least(pool, r_sb, b)
                    nc.gpsimd.tensor_tensor(XB[:], XIN[:], broadcast_mid(row[:, 0, :], NT), ALU.add).then_inc(xb, 1)

                def front(b, n):
                    if n >= 1 and chunk_at(n - 1) is not None:
                        c = chunk_at(n - 1)
                        pool.wait_ge(raw_sb, CH * b + c + 1)
                        at_least(pool, k_sb, CH * b + c - 1)
                        nc.gpsimd.tensor_tensor(t1[c % 2][:], raw[c % 2][:], cs[:, 0, :, :], ALU.mult).then_inc(t1_sb, 1)
                    if n >= 2 and chunk_at(n - 2) is not None:
                        c = chunk_at(n - 2)
                        pool.wait_ge(t1_sb, CH * b + c + 1)
                        pool.wait_ge(t2_sb, CH * b + c + 1)
                        if c % 4 == 0:
                            at_least(pool, sc_ps, U * (b - 1) + (c // 4 + 1) * 16)
                        nc.gpsimd.tensor_tensor(qT[:, c, :], t1[c % 2][:, 0, :], t2[c % 2][:, 0, :],
                                                ALU.add).then_inc(q_sb, 1)

                def deviation(b, n):
                    if n != U - 1:
                        return
                    pool.wait_ge(var, b + 1)
                    nc.gpsimd.tensor_tensor(rstd[:], ve[:], neghalf[:], ALU.pow).then_inc(rstd_ok, 1)

                def step(b, first=False, last=False):
                    for n in range(U):
                        lagged(b, n, U, RESIDUAL, deviation)
                        if n < 16:
                            front(b, n)
                        if n == RESULT:
                            add_bias(b)
                        if n == 11 and not last:
                            rms(b + 1)
                        if n >= 16 and not last:
                            front(b + 1, n)
                        if not first:
                            for k in CROSS.get(n, ()):
                                x.pool(pool, b - 1, k)

                rms(0)
                for n in range(16, U):
                    front(0, n)
                step(0, first=True)
                step(1)
                with pool.Fori(2, B - 1) as b:
                    step(b)
                step(B - 1, last=True)
                lagged(B, RESIDUAL - 1, U, RESIDUAL, deviation)
                for k in range(x.STEPS):
                    x.pool(pool, B - 1, k)
        al.end()


def decoder(nc, d):
    x2 = nc.dram_tensor("after_L0_xattn", (B, S, D), F32, kind="Internal").ap()
    x3 = nc.dram_tensor("after_L0_ffn", (B, S, D), F32, kind="Internal").ap()
    x5 = nc.dram_tensor("after_L1_xattn", (B, S, D), F32, kind="Internal").ap()
    flat = lambda ap: ap.rearrange("b s n -> (b s) n")
    cross = lambda layer: {n: d[f"{layer}_xattn_{n}"] for n in ("Wq", "Wk", "Wv", "Wo")}
    router = lambda layer: {"ident": d["ident"], "before": d["before"], "iota": d["iota"],
                            **{n: d[f"{layer}_ffn_{n}"] for n in ("Wr", "br", "W1", "b1", "W2", "b2")}}
    relative_attention_phase(nc, {**d, "x2": x2, "L0_xattn": cross("L0")})
    experts_phase(nc, {**router("L0"), "x": flat(x2), "out": flat(x3)}, "b_", 1, 512, ACT.Relu, False)
    segment_attention_phase(nc, {**d, "x": x3, "x5": x5, "L1_xattn": cross("L1")})
    experts_phase(nc, {**router("L1"), "gb": d["L1_gb"], "x": flat(x5), "out": flat(d["out"])},
                  "e_", 2, 1024, ACT.Gelu, True)


def constants():
    f = np.float32
    c = {"ident": np.eye(P, dtype=f),
         "before": (np.arange(P)[:, None] < np.arange(P)).astype(f),
         "headmask": (np.arange(P)[:, None] // HD == np.arange(HC)).astype(f),
         "iota": np.tile(np.concatenate([np.arange(E8), P * np.arange(most_tiles(2))]).astype(f), (P, 1))}
    buckets, furthest = 64, 128
    mid = buckets // 2
    r = np.arange(1 - S, S)
    far = np.maximum(np.abs(r), mid - 1).astype(f)
    log = np.ceil(np.log(far / f(mid)) / f(np.log((furthest - 1) / mid)) * f(mid - 1)) + mid
    bucket = np.clip(np.where(far <= mid, r, log * np.sign(r)).astype(int) + buckets, 0, 2 * buckets - 1)
    onehot = (np.arange(P)[:, None] == bucket).astype(f)
    c["onehot"] = np.concatenate([onehot[:, ::-1], onehot], 1)
    inv = (f(1) / f(10000.0) ** (np.arange(0, DH, 2, dtype=f) / f(DH))).astype(f)
    angle = np.arange(S, dtype=f)[:, None] * inv
    both = [np.tile(np.repeat(g(angle), 2, -1).T, (P // DH, 1)) for g in (np.cos, np.sin)]
    c["cossin"] = np.stack([np.stack([g, g], 1) for g in both], 1).astype(f)
    rot = np.zeros((P, P), f)
    even = np.arange(0, P, 2)
    rot[even + 1, even], rot[even, even + 1] = -1, 1
    c["rot"] = rot
    c["mask"] = np.zeros((P, PM + P), f)
    c["mask"][:, PM:] = np.where(np.arange(P) <= np.arange(P)[:, None], 0, -3e38)
    return c


def laid_out(v):
    col = lambda n: v[n].reshape(KC, P).T
    out = dict(constants())
    for n in ("L0_attn_Wq", "L0_attn_Wk", "L0_attn_Wv", "L0_attn_Wo", "L0_attn_Wpk", "L0_attn_Wpq", "L0_attn_rel_emb"):
        out[n.replace("attn_", "")] = v[n]
    for layer in ("L0", "L1"):
        for n in ("Wq", "Wk", "Wv", "Wo"):
            out[f"{layer}_xattn_{n}"] = v[f"{layer}_xattn_{n}"]
        out[f"{layer}_ffn_b1"] = v[f"{layer}_ffn_b1"].reshape(E8, -1, P).transpose(0, 2, 1)
        out[f"{layer}_ffn_b2"] = v[f"{layer}_ffn_b2"]
    out["L0_ffn_Wr"], out["L1_ffn_Wr"] = v["L0_ffn_Wr"], v["L1_ffn_Wg"].T
    out["L0_ffn_br"], out["L1_ffn_br"] = v["L0_ffn_br"], v["L1_ffn_bg"]
    for n in ("W1", "W2"):
        out[f"L0_ffn_{n}"] = v[f"L0_ffn_{n}"]
        out[f"L1_ffn_{n}"] = v[f"L1_ffn_{n}"].transpose(0, 2, 1)
    out["L0_col"] = np.concatenate([col("L0_attn_bq"), col("L0_attn_bk"), col("L0_xattn_bq"), col("L0_xattn_bk")], 1)
    out["L0_row"] = np.stack([v["L0_attn_bv"], v["L0_attn_bv"], v["L0_attn_bo"], v["L0_xattn_bv"], v["L0_xattn_bo"]])
    out["L0_prow"] = np.stack([v["L0_attn_ln_g"], v["L0_attn_ln_b"], v["L0_attn_bpk"], v["L0_attn_bpq"]])
    out["L1_col"] = np.concatenate([col("L1_attn_norm_w"), col("L1_xattn_bq"), col("L1_xattn_bk")], 1)
    out["L1_row"] = np.stack([v["L1_attn_b_out"], v["L1_xattn_bv"], v["L1_xattn_bo"]])
    out["L1_gb"] = np.stack([v["L1_ffn_gamma"], v["L1_ffn_beta"]])
    out["w_qkv"], out["w_out"] = v["L1_attn_w_qkv"], v["L1_attn_w_out"]
    out["pm_kT"] = v["L1_attn_pm_k"].transpose(0, 2, 1).reshape(INNER, PM)
    out["pm_v"] = v["L1_attn_pm_v"]
    out["ctxT"] = v["ctx_768"].transpose(0, 2, 1)
    out["x"] = v["x"]
    return out


def kernel(**inputs):
    from concourse import bacc
    from concourse.bass_utils import run_bass_kernel_spmd

    nc = bacc.Bacc("TRN2", target_bir_lowering=False, num_devices=1)
    arrays, d = {}, {}
    for name, a in laid_out({n: np.asarray(a) for n, a in inputs.items()}).items():
        a = np.ascontiguousarray(a)
        arrays[f"in_{name}"] = a
        d[name] = nc.dram_tensor(f"in_{name}", a.shape, mybir.dt.from_np(a.dtype), kind="ExternalInput").ap()
    d["out"] = nc.dram_tensor("out", (B, S, D), F32, kind="ExternalOutput").ap()
    decoder(nc, d)
    return run_bass_kernel_spmd(nc, [arrays], core_ids=[0]).results[0]["out"]
```

```python
from contextlib import ExitStack

import numpy as np

import concourse.bass as bass
from concourse import mybir

F32 = mybir.dt.float32
I32 = mybir.dt.int32
U32 = mybir.dt.uint32
ALU = mybir.AluOpType
ACT = mybir.ActivationFunctionType
AXX = mybir.AxisListType.X

P = 128
B, S, D = 8, 256, 256
T = B * S
KC = D // P
NT = S // P
H, HD = 16, 16
HG = 4
NG = H // HG
HC = P // HD
CK, CD = 77, 192
CC = CD // 2
REL = 2 * S - 1
WIN = S + P - 1
CLAMP = 10000.0
LN_EPS = 1e-5


def at_least(eng, sem, value):
    if not (isinstance(value, int) and value <= 0):
        eng.wait_ge(sem, value)


def own_wait(eng, sem):
    eng.sem_inc(sem, 1)


def wait_alone(eng, sem, awaited, value):
    if not (isinstance(value, int) and value <= 0):
        eng.wait_ge(awaited, value)
        own_wait(eng, sem)


def repeated(ap, n):
    return bass.AP(ap.tensor, ap.offset, [ap.ap[0], [0, n]])


class Chain:

    def __init__(self, eng, sem, waited=None):
        self.eng, self.sem, self.waited, self.n, self.base = eng, sem, waited, 0, 0

    def start(self, base):
        self.base, self.n = base, 0

    def link(self, ins):
        ins.then_inc(self.sem, 1)
        self.n += 1
        self.eng.wait_ge(self.sem, self.base + self.n)


def broadcast_mid(ap, n):
    return bass.AP(ap.tensor, ap.offset, [ap.ap[0], [0, n], ap.ap[1]])


def broadcast_last(ap, n):
    return bass.AP(ap.tensor, ap.offset, [ap.ap[0], ap.ap[1], [0, n]])


def exists(b):
    return not isinstance(b, int) or 0 <= b < B


def lagged(b, n, count, lag, do):
    batches, unit = divmod(n - lag, count)
    if exists(b + batches):
        do(b + batches, unit)


class Alloc:

    def __init__(self, nc, phase, prefix):
        self.nc, self.phase, self.prefix = nc, phase, prefix
        self.sems = []

    def sb(self, name, shape, dt=F32):
        return self.phase.enter_context(self.nc.sbuf_tensor(self.prefix + name, shape, dt))

    def bank(self, name):
        return self.phase.enter_context(self.nc.psum_tensor(self.prefix + name, [P, 512], F32))

    def sem(self, name):
        self.sems.append(self.nc.alloc_semaphore(name=self.prefix + name))
        return self.sems[-1]

    def end(self):
        self.nc.all_engine_barrier()
        self.nc.clear_and_free_semaphores(self.sems)
        self.nc.all_engine_barrier()


class Cross:

    STEPS = 16
    SCORES = range(2, 6)
    PAIRS = range(9, 13)
    OUTPUTS = range(10, 14)
    VECTOR_LINKS = NT + 2

    def __init__(self, al, a, w, clip, x1_ok, banks):
        self.nc, self.a, self.clip, self.x1_ok = al.nc, a, clip, x1_ok
        self.w = w
        self.FR = banks
        self.wq = al.sb("xwq", [P, KC, D])
        self.wk = al.sb("xwk", [CC, 2, D])
        self.wv = al.sb("xwv", [CC, 2, D])
        self.wo = al.sb("xwo", [P, NG, D])
        self.ctxT = al.sb("ctxT", [CC, 2, CK])
        self.x1T = al.sb("x1T", [P, KC, S])
        self.OT = al.sb("xOT", [P, NG, S])
        self.R = al.sb("xR", [P, NT, D])
        self.PT = al.sb("xPT", [CK, 2, HG, S])
        self.qT = al.sb("xqT", [P, KC, S])
        self.kM = al.sb("xkM", [P, KC, HC * CK])
        self.v = al.sb("xv", [CK, H, 32])
        self.SX = al.sb("SX", [P, NT, H * CK])
        self.mx = al.sb("xmx", [P, NT, H])
        self.sm = al.sb("xsm", [P, NT, H])
        self.rs = al.sb("xrs", [P, NT, H])
        self.X1B = al.sb("X1B", [P, NT, D])
        self.st = al.sb("xst", [P, NT, 6])
        self.mv = al.sb("xmv", [P, NT, 2])
        self.ve = al.sb("xve", [P, NT])
        self.rstd = al.sb("xrstd", [P, NT])
        self.X2 = al.sb("X2", [P, NT, D])
        s = al.sem
        self.sp_waited = s("x_sp_waited")
        self.weights = s("x_weights")
        self.zeroed = s("x_zeroed")
        self.ctx_in = s("x_ctx_in")
        self.x1T_ps = s("x_x1T_ps")
        self.x1T_sb = s("x_x1T_sb")
        self.q_ps = s("x_q_ps")
        self.q_sb = s("x_q_sb")
        self.kv_ps = s("x_kv_ps")
        self.kv_sb = s("x_kv_sb")
        self.sc_ps = s("x_sc_ps")
        self.sc_sb = s("x_sc_sb")
        self.maxed = s("x_maxed")
        self.shifted = s("x_shifted")
        self.exped = s("x_exped")
        self.recip = s("x_recip")
        self.normed = s("x_normed")
        self.pT_ps = s("x_pT_ps")
        self.pT_sbA = s("x_pT_sbA")
        self.pT_sbV = s("x_pT_sbV")
        self.o_ps = s("x_o_ps")
        self.o_sb = s("x_o_sb")
        self.y_ps = s("x_y_ps")
        self.x1b = s("x_x1b")
        self.r_sb = s("x_r_sb")
        self.var = s("x_var")
        self.rstd_ok = s("x_rstd")
        self.x2 = s("x_x2")
        self.stored = s("x_stored")

    def load_weights(self, sp):
        w = self.w
        sp.dma_start(self.wq[:], w["Wq"].rearrange("(k p) n -> p k n", p=P)).then_inc(self.weights, 16)
        sp.dma_start(self.wk[:], w["Wk"].rearrange("(k p) n -> p k n", p=CC)).then_inc(self.weights, 16)
        sp.dma_start(self.wv[:], w["Wv"].rearrange("(k p) n -> p k n", p=CC)).then_inc(self.weights, 16)
        sp.wait_ge(self.zeroed, 2)
        wo = w["Wo"].rearrange("(g j i) n -> j i g n", j=HG, i=HD)
        for j in range(HG):
            sp.dma_start(self.wo[32 * j:32 * j + HD, :, :], wo[j]).then_inc(self.weights, 16)

    WEIGHTS = (3 + HG) * 16

    def load_ctx(self, sp, b):
        at_least(sp, self.kv_ps, b)
        own_wait(sp, self.sp_waited)
        sp.dma_start(self.ctxT[:], self.a["ctxT"][b].rearrange("(k p) n -> p k n", p=CC)).then_inc(self.ctx_in, 16)

    def store(self, sp, b):
        sp.wait_ge(self.x2, b + 1)
        own_wait(sp, self.sp_waited)
        sp.dma_start(self.a["x2_out"][b].rearrange("(t p) n -> p t n", p=P), self.X2[:]).then_inc(self.stored, 16)

    def tensor(self, pe, b, step):
        nc, (FR0, FR1) = self.nc, self.FR
        if step == 0:
            pe.wait_ge(self.x1_ok, b + 1)
            for t in range(NT):
                for k in range(KC):
                    last = nc.tensor.transpose(FR0[:, k * S + t * P:k * S + (t + 1) * P],
                                               self.a["X1"][:, t, k * P:(k + 1) * P], self.a["ident"][:])
            last.then_inc(self.x1T_ps, 1)
        if step == 1:
            pe.wait_ge(self.ctx_in, b * 16 + 16)
            pe.wait_ge(self.x1T_sb, b + 1)
            at_least(pe, self.r_sb, b)
            for c in range(KC):
                for k in range(KC):
                    last = nc.tensor.matmul(FR1[:, c * S:(c + 1) * S], self.wq[:, k, c * P:(c + 1) * P],
                                            self.x1T[:, k, :], start=k == 0, stop=k == KC - 1)
            last.then_inc(self.q_ps, 1)
            for c in range(KC):
                for k in range(2):
                    nc.tensor.matmul(FR0[:, c * CK:(c + 1) * CK], self.wk[:, k, c * P:(c + 1) * P],
                                     self.ctxT[:, k, :], start=k == 0, stop=k == 1)
            for k in range(2):
                last = nc.tensor.matmul(FR0[0:CK, S:S + D], self.ctxT[:, k, :], self.wv[:, k, :],
                                        start=k == 0, stop=k == 1)
            last.then_inc(self.kv_ps, 1)
        if step in self.SCORES:
            for i in range(2 * (step - 2), 2 * (step - 2) + 2):
                t, q = i // 4, i % 4
                if i == 0:
                    pe.wait_ge(self.kv_sb, b + 1)
                    pe.wait_ge(self.q_sb, b + 1)
                if i >= 2:
                    pe.wait_ge(self.sc_sb, 8 * b + i - 1)
                nc.tensor.matmul(self.FR[i % 2][:, 0:4 * CK], self.qT[:, q // 2, t * P:(t + 1) * P],
                                 self.kM[:, q // 2, (q % 2) * 4 * CK:(q % 2 + 1) * 4 * CK],
                                 start=True, stop=True).then_inc(self.sc_ps, 1)
        if step in self.OUTPUTS:
            g = step - 10
            pe.wait_ge(self.pT_sbA, 4 * b + g + 1)
            pe.wait_ge(self.pT_sbV, 4 * b + g + 1)
            for j in range(HG):
                last = nc.tensor.matmul(FR0[32 * j:32 * j + 32, 0:S], self.v[:, HG * g + j, :],
                                        self.PT[:, g % 2, j, :], start=True, stop=True)
            last.then_inc(self.o_ps, 1)
        if step in self.PAIRS:
            for hp in range(2 * (step - 9), 2 * (step - 9) + 2):
                if hp == 0:
                    pe.wait_ge(self.normed, 2 * b + 2)
                    at_least(pe, self.router.lg_sb, b)
                elif hp == 1:
                    at_least(pe, self.router.placed, b)
                elif hp % 2 == 1:
                    pe.wait_ge(self.o_sb, 4 * b + hp // 2)
                for u in range(2):
                    for t in range(NT):
                        h = 2 * hp + u
                        last = nc.tensor.transpose(
                            self.FR[1 - hp % 2][0:CK, u * S + t * P:u * S + (t + 1) * P],
                            self.SX[:, t, h * CK:(h + 1) * CK], self.a["ident"][:])
                last.then_inc(self.pT_ps, 1)
        if step == 14:
            pe.wait_ge(self.o_sb, 4 * b + 4)
            for t in range(NT):
                for g in range(NG):
                    last = nc.tensor.matmul(FR1[:, t * D:(t + 1) * D], self.OT[:, g, t * P:(t + 1) * P],
                                            self.wo[:, g, :], start=g == 0, stop=g == NG - 1)
            last.then_inc(self.y_ps, 1)

    def scalar(self, act, b, step):
        nc, (FR0, FR1) = self.nc, self.FR
        if step == 0:
            act.wait_ge(self.x1T_ps, b + 1)
            nc.scalar.activation(self.x1T[:].rearrange("p k n -> p (k n)"), FR0[:], ACT.Copy).then_inc(self.x1T_sb, 1)
        if step == 1:
            act.wait_ge(self.q_ps, b + 1)
            for c in range(KC):
                last = nc.scalar.activation(self.qT[:, c, :], FR1[:, c * S:(c + 1) * S], ACT.Identity,
                                            bias=self.a["xbq"][:, c:c + 1])
            last.then_inc(self.q_sb, 1)
        if step in self.SCORES and not self.clip:
            for i in range(2 * (step - 2), 2 * (step - 2) + 2):
                t, q = i // 4, i % 4
                act.wait_ge(self.sc_ps, 8 * b + i + 1)
                nc.scalar.activation(self.SX[:, t, q * 4 * CK:(q + 1) * 4 * CK], self.FR[i % 2][:, 0:4 * CK],
                                     ACT.Copy).then_inc(self.sc_sb, 1)
        if step in (5, 7):
            t = (step - 5) // 2
            act.wait_ge(self.shifted, 2 * b + t + 1)
            nc.scalar.activation(self.SX[:, t, :], self.SX[:, t, :], ACT.Exp,
                                 scale=float(HD) ** -0.5).then_inc(self.exped, 1)
        if step in self.OUTPUTS:
            g = step - 10
            act.wait_ge(self.o_ps, 4 * b + g + 1)
            nc.scalar.activation(self.OT[:, g, :], FR0[:, 0:S], ACT.Copy).then_inc(self.o_sb, 1)
        if step in self.PAIRS:
            g = step - 9
            act.wait_ge(self.pT_ps, 8 * b + 2 * g + 1)
            nc.scalar.activation(self.PT[:, g % 2, 0:2, :].rearrange("p h n -> p (h n)"),
                                 FR1[0:CK, :], ACT.Copy).then_inc(self.pT_sbA, 1)

    def vector(self, dve, b, step, chain):
        nc, a, (FR0, FR1) = self.nc, self.a, self.FR
        lim = CLAMP / float(HD) ** -0.5
        heads = lambda t: self.SX[:, t, :].rearrange("p (h n) -> p h n", h=H)
        if step == 1:
            dve.wait_ge(self.kv_ps, b + 1)
            for c in range(KC):
                nc.vector.scalar_tensor_tensor(
                    out=self.kM[:, c, :].rearrange("p (h n) -> p h n", h=HC),
                    in0=broadcast_mid(FR0[:, c * CK:(c + 1) * CK], HC), scalar=a["xbk"][:, c:c + 1],
                    in1=broadcast_last(a["headmask"][:, 0:HC], CK), op0=ALU.add, op1=ALU.mult)
            nc.vector.tensor_tensor(self.v[:, :, 0:HD], FR0[0:CK, S:S + D].rearrange("p (h n) -> p h n", h=H),
                                    a["xbv"][0:CK, :].rearrange("p (h n) -> p h n", h=H),
                                    ALU.add).then_inc(self.kv_sb, 1)
        if step in self.SCORES and self.clip:
            for i in range(2 * (step - 2), 2 * (step - 2) + 2):
                t, q = i // 4, i % 4
                dve.wait_ge(self.sc_ps, 8 * b + i + 1)
                nc.vector.tensor_scalar(self.SX[:, t, q * 4 * CK:(q + 1) * 4 * CK], self.FR[i % 2][:, 0:4 * CK],
                                        lim, -lim, ALU.min, ALU.max).then_inc(self.sc_sb, 1)
        if step in (3, 5):
            t = (step - 3) // 2
            dve.wait_ge(self.sc_sb, 8 * b + 4 * t + 4)
            nc.vector.tensor_reduce(self.mx[:, t, :], heads(t), AXX, ALU.max).then_inc(self.maxed, 1)
        if step in (4, 6):
            t = (step - 4) // 2
            dve.wait_ge(self.maxed, 2 * b + t + 1)
            nc.vector.tensor_tensor(heads(t), heads(t), broadcast_last(self.mx[:, t, :], CK),
                                    ALU.subtract).then_inc(self.shifted, 1)
        if step in (7, 8):
            t = step - 7
            dve.wait_ge(self.exped, 2 * b + t + 1)
            chain.link(nc.vector.tensor_reduce(self.sm[:, t, :], heads(t), AXX, ALU.add))
            nc.vector.reciprocal(self.rs[:, t, :], self.sm[:, t, :]).then_inc(self.recip, 1)
        if step in self.PAIRS:
            g = step - 9
            dve.wait_ge(self.pT_ps, 8 * b + 2 * g + 2)
            nc.vector.tensor_copy(self.PT[:, g % 2, 2:4, :].rearrange("p h n -> p (h n)"),
                                  FR0[0:CK, :]).then_inc(self.pT_sbV, 1)
        if step == 14:
            dve.wait_ge(self.y_ps, b + 1)
            dve.wait_ge(self.x1b, b + 1)
            nc.vector.tensor_tensor(self.R[:].rearrange("p t n -> p (t n)"), FR1[:],
                                    self.X1B[:].rearrange("p t n -> p (t n)"), ALU.add).then_inc(self.r_sb, 1)
            dve.wait_ge(self.r_sb, b + 1)
            layernorm_stats(nc, chain, self.R, self.st, self.mv, self.ve, self.var, LN_EPS)
        if step == 15:
            dve.wait_ge(self.rstd_ok, b + 1)
            at_least(dve, self.stored, 16 * b)
            if not self.router.normed:
                at_least(dve, self.router.scattered, 16 * NT * self.router.top * b)
            layernorm_apply(nc, self.R, self.mv, self.rstd, self.X2).then_inc(self.x2, 1)

    def pool(self, pool, b, step):
        nc, a = self.nc, self.a
        if step == 0:
            pool.wait_ge(self.x1_ok, b + 1)
            at_least(pool, self.r_sb, b)
            nc.gpsimd.tensor_tensor(self.X1B[:], a["X1"][:], broadcast_mid(a["xbo"], NT),
                                    ALU.add).then_inc(self.x1b, 1)
        if step in (7, 8):
            t = step - 7
            pool.wait_ge(self.recip, 2 * b + t + 1)
            v = self.SX[:, t, :].rearrange("p (h n) -> p h n", h=H)
            nc.gpsimd.tensor_tensor(v, v, broadcast_last(self.rs[:, t, :], CK), ALU.mult).then_inc(self.normed, 1)
        if step == 14:
            pool.wait_ge(self.var, b + 1)
            nc.gpsimd.tensor_tensor(self.rstd[:], self.ve[:], a["neghalf"][:, 0:NT], ALU.pow).then_inc(self.rstd_ok, 1)


def layernorm_stats(nc, chain, R, st, mv, ve, var, eps):
    for t in range(NT):
        last = nc.vector.bn_stats(st[:, t, :], R[:, t, :])
    chain.link(last)
    own_wait(chain.eng, chain.waited)
    for t in range(NT):
        last = nc.vector.bn_aggr(mv[:, t, :], st[:, t, :])
    chain.link(last)
    nc.vector.tensor_scalar(ve[:], mv[:, :, 1], eps, None, ALU.add).then_inc(var, 1)


def layernorm_apply(nc, R, mv, rstd, out):
    for t in range(NT):
        last = nc.vector.tensor_scalar(out[:, t, :], R[:, t, :], mv[:, t, 0:1], rstd[:, t:t + 1],
                                       ALU.subtract, ALU.mult)
    return last


E8 = 8
ROOM = T + P
LOGITS, BEST, NUMBER, AHEAD, SO_FAR = [slice(E8 * i, E8 * (i + 1)) for i in range(5)]
FIELDS = 5 * E8


class Router:

    STATS, APPLY, INPUT, LOGIT, COUNT = 0, 2, 6, 7, 8

    def __init__(self, al, a, r, x, top, normed):
        self.nc, self.a, self.r, self.x, self.top, self.normed = al.nc, a, r, x, top, normed
        self.VECTOR_LINKS = (3 if normed else 0) + 3 + (top > 1) + 5 + 2 * top
        self.SCATTER = range(self.COUNT, self.COUNT + NT * top)
        self.STEPS = self.SCATTER.stop
        self.before = al.sb("before", [P, P])
        self.ones = al.sb("ones", [P, P])
        self.iota = al.sb("riota", [P, E8])
        self.base = al.sb("base", [P, E8])
        self.wr = al.sb("wr", [P, KC, E8])
        self.br = al.sb("br", [P, E8])
        self.gb = al.sb("gb", [P, 2, D]) if normed else None
        self.XN = al.sb("XN", [P, NT, D]) if normed else x.X2
        self.rT = al.sb("rT", [P, NT, KC, P])
        self.rec = al.sb("rec", [P, NT, FIELDS])
        self.I8 = al.sb("I8", [P, NT, E8], U32)
        self.OH = [al.sb(f"OH{k}", [P, NT, E8]) for k in range(top)]
        self.OHS = al.sb("OHS", [P, NT, E8]) if top > 1 else self.OH[0]
        self.TP = al.sb("TP", [P, NT + 1, E8])
        self.SEL = al.sb("SEL", [P, NT, E8])
        self.PF = al.sb("PF", [P, top, NT])
        self.POS = al.sb("POS", [P, top, NT], U32)
        self.st = al.sb("rst", [P, NT, 6])
        self.mv = al.sb("rmv", [P, NT, 2])
        self.ve = al.sb("rve", [P, NT])
        self.rstd = al.sb("rrstd", [P, NT])
        s = al.sem
        self.consts = s("r_consts")
        self.ready = s("r_ready")
        self.var = s("r_var")
        self.rstd_ok = s("r_rstd")
        self.scaled = s("r_scaled")
        self.xn = s("r_xn")
        self.xT_ps = s("r_xT_ps")
        self.xT_sb = s("r_xT_sb")
        self.lg_ps = s("r_lg_ps")
        self.lg_sb = s("r_lg_sb")
        self.oh = s("r_oh")
        self.ranks = s("r_ranks")
        self.placed = s("r_placed")
        self.scattered = s("r_scattered")
        self.saved = s("r_saved")
        self.waits = [s("r_dve_waited"), s("r_pool_waited"), s("r_sp_waited")]
        self.CONSTS = 16 * (4 + normed)

    def load_constants(self, sp):
        r = self.r
        loads = [(self.before[:], r["before"]), (self.iota[:], r["iota"][:, 0:E8]),
                 (self.wr[:], r["Wr"].rearrange("(k p) n -> p k n", p=P)),
                 (self.br[:], r["br"].partition_broadcast(P))]
        if self.normed:
            loads.append((self.gb[:], r["gb"].partition_broadcast(P)))
        for dst, src in loads:
            sp.dma_start(dst, src).then_inc(self.consts, 16)

    def store_record(self, sp, b):
        sp.wait_ge(self.placed, b + 1)
        own_wait(sp, self.waits[2])
        sp.dma_start(self.r["record"].rearrange("(b t) p f -> b p t f", t=NT)[b], self.rec[:]).then_inc(self.saved, 16)

    def tensor(self, pe, b, step):
        nc, (FR0, FR1) = self.nc, self.x.FR
        if step == self.INPUT:
            if self.normed:
                pe.wait_ge(self.xn, b + 1)
            else:
                pe.wait_ge(self.x.x2, b + 1)
            at_least(pe, self.x.sc_sb, min(8 * b + 15, 8 * B) if isinstance(b, int) else 8 * b + 15)
            for t in range(NT):
                for k in range(KC):
                    last = nc.tensor.transpose(FR0[:, (t * KC + k) * P:(t * KC + k + 1) * P],
                                               self.XN[:, t, k * P:(k + 1) * P], self.a["ident"][:])
            last.then_inc(self.xT_ps, 1)
        if step == self.LOGIT:
            pe.wait_ge(self.xT_sb, b + 1)
            at_least(pe, self.x.sc_sb, min(8 * b + 16, 8 * B) if isinstance(b, int) else 8 * b + 16)
            at_least(pe, self.x.r_sb, b + 1)
            for t in range(NT):
                for k in range(KC):
                    last = nc.tensor.matmul(FR1[:, t * E8:(t + 1) * E8], self.rT[:, t, k, :], self.wr[:, k, :],
                                            start=k == 0, stop=k == KC - 1)
            last.then_inc(self.lg_ps, 1)
        if step == self.COUNT:
            pe.wait_ge(self.oh, b + 1)
            flat = self.OHS[:].rearrange("p t e -> p (t e)")
            nc.tensor.matmul(FR0[:, 0:NT * E8], self.before[:], flat, start=True, stop=True)
            nc.tensor.matmul(FR0[:, NT * E8:2 * NT * E8], self.ones[:], flat,
                             start=True, stop=True).then_inc(self.ranks, 1)

    def scalar(self, act, b, step):
        if step == self.INPUT:
            act.wait_ge(self.xT_ps, b + 1)
            self.nc.scalar.activation(self.rT[:].rearrange("p t k n -> p (t k n)"), self.x.FR[0][:],
                                      ACT.Copy).then_inc(self.xT_sb, 1)

    def prepare(self, dve):
        nc = self.nc
        nc.vector.memset(self.ones[:], 1.0)
        nc.vector.memset(self.TP[:], 0.0)
        dve.wait_ge(self.consts, self.CONSTS)
        nc.vector.tensor_scalar(self.base[:], self.iota[:], float(ROOM), None, ALU.mult).then_inc(self.ready, 1)
        dve.wait_ge(self.ready, 1)

    def vector(self, dve, b, step, chain):
        nc, (FR0, FR1), rec = self.nc, self.x.FR, self.rec
        v = lambda ins: chain.link(ins)
        if step == self.STATS and self.normed:
            dve.wait_ge(self.x.x2, b + 1)
            own_wait(dve, self.waits[0])
            layernorm_stats(nc, chain, self.x.X2, self.st, self.mv, self.ve, self.var, LN_EPS)
        if step == self.APPLY and self.normed:
            dve.wait_ge(self.rstd_ok, b + 1)
            at_least(dve, self.scattered, 16 * NT * self.top * b)
            layernorm_apply(nc, self.x.X2, self.mv, self.rstd, self.XN).then_inc(self.scaled, 1)
            dve.wait_ge(self.scaled, b + 1)
            v(nc.vector.tensor_tensor(self.XN[:], self.XN[:], broadcast_mid(self.gb[:, 0, :], NT), ALU.mult))
            nc.vector.tensor_tensor(self.XN[:], self.XN[:], broadcast_mid(self.gb[:, 1, :], NT),
                                    ALU.add).then_inc(self.xn, 1)
        if step == self.LOGIT:
            dve.wait_ge(self.lg_ps, b + 1)
            at_least(dve, self.saved, 16 * b)
            nc.vector.tensor_tensor(rec[:, :, LOGITS], FR1[:, 0:NT * E8].rearrange("p (t e) -> p t e", e=E8),
                                    broadcast_mid(self.br[:], NT), ALU.add).then_inc(self.lg_sb, 1)
            dve.wait_ge(self.lg_sb, b + 1)
            own_wait(dve, self.waits[0])
            for t in range(NT):
                last = nc.vector.max(rec[:, t, BEST], rec[:, t, LOGITS])
            v(last)
            own_wait(dve, self.waits[0])
            for t in range(NT):
                last = nc.vector.max_index(self.I8[:, t, :], rec[:, t, BEST], rec[:, t, LOGITS])
            v(last)
            v(nc.vector.tensor_copy(rec[:, :, NUMBER], self.I8[:]))
            for k in range(self.top):
                last = nc.vector.tensor_tensor(self.OH[k][:], broadcast_mid(self.iota[:], NT),
                                               broadcast_last(rec[:, :, NUMBER.start + k], E8), ALU.is_equal)
            if self.top > 1:
                v(last)
                last = nc.vector.tensor_tensor(self.OHS[:], self.OH[0][:], self.OH[1][:], ALU.add)
            last.then_inc(self.oh, 1)
        if step == self.COUNT:
            dve.wait_ge(self.ranks, b + 1)
            at_least(dve, self.scattered, 16 * NT * self.top * b)
            v(nc.vector.tensor_copy(self.TP[:, 0, :], self.TP[:, NT, :]))
            for t in range(NT):
                v(nc.vector.tensor_tensor(self.TP[:, t + 1, :], self.TP[:, t, :],
                                          FR0[:, (NT + t) * E8:(NT + t + 1) * E8], ALU.add))
            v(nc.vector.tensor_tensor(rec[:, :, AHEAD], self.TP[:, 0:NT, :],
                                      FR0[:, 0:NT * E8].rearrange("p (t e) -> p t e", e=E8), ALU.add))
            nc.vector.tensor_copy(rec[:, :, SO_FAR], self.TP[:, 1:NT + 1, :])
            v(nc.vector.tensor_tensor(rec[:, :, AHEAD], rec[:, :, AHEAD], broadcast_mid(self.base[:], NT), ALU.add))
            for k in range(self.top):
                v(nc.vector.tensor_tensor(self.SEL[:], rec[:, :, AHEAD], self.OH[k][:], ALU.mult))
                v(nc.vector.tensor_reduce(self.PF[:, k, :], self.SEL[:], AXX, ALU.add))
            nc.vector.tensor_copy(self.POS[:], self.PF[:]).then_inc(self.placed, 1)

    def pool(self, pool, b, step):
        nc = self.nc
        if step == self.STATS and self.normed:
            pool.wait_ge(self.var, b + 1)
            nc.gpsimd.tensor_tensor(self.rstd[:], self.ve[:], self.a["neghalf"][:, 0:NT], ALU.pow).then_inc(self.rstd_ok, 1)
        if step in self.SCATTER:
            t, k = divmod(step - self.COUNT, self.top)
            pool.wait_ge(self.x.x2, b + 1)
            if self.normed:
                pool.wait_ge(self.xn, b + 1)
            pool.wait_ge(self.placed, b + 1)
            own_wait(pool, self.waits[1])
            nc.gpsimd.indirect_dma_start(self.r["sorted"], bass.IndirectOffsetOnAxis(self.POS[:, k, t:t + 1], 0),
                                         self.XN[:, t, :], None).then_inc(self.scattered, 16)


def relative_attention_phase(nc, d):
    with ExitStack() as phase:
        al = Alloc(nc, phase, "a_")
        sb, sem = al.sb, al.sem
        scale = float(3 * HD) ** -0.5
        table_scale = float(3 * HD / (2 * HD)) ** 0.5

        FR0, FR1, BD0, BD1, SC0, SC1, PTB, PO = [al.bank(n) for n in
                                                 ("FR0", "FR1", "BD0", "BD1", "SC0", "SC1", "PTB", "PO")]
        BD, SC = [BD0, BD1], [SC0, SC1]
        RING = 4

        ident = sb("ident", [P, P])
        headmask = sb("headmask", [P, HC])
        col = sb("col", [P, 8])
        row = sb("row", [P, 5, D])
        neghalf = sb("neghalf", [P, NT])
        wq = sb("wq", [P, KC, D])
        wk = sb("wk", [P, KC, D])
        wv = sb("wv", [P, KC, D])
        wo = sb("wo", [P, KC, D])
        E = [sb("E1", [P, KC, REL]), sb("E2", [P, KC, REL])]
        XIN = sb("XIN", [P, NT, D])
        XB = sb("XB", [P, NT, D])
        xT = sb("xT", [P, KC, S])
        qM = sb("qM", [P, H, S])
        kT = sb("kT", [P, KC, S])
        kM = sb("kM", [P, H, S])
        v = sb("v", [P, NT, H, 32])
        ST = [sb(f"stage{k}", [P, RING, NT, WIN]) for k in range(2)]
        SK = [sb(f"skewed{k}", [P, RING, NT, S]) for k in range(2)]
        SM = sb("SM", [P, RING, NT, S])
        nb = sb("nb", [P, RING, NT])
        sm = sb("sm", [P, RING, NT])
        rs = sb("rs", [P, RING, NT])
        OT = sb("OT", [P, KC, S])
        R = sb("R", [P, NT, D])
        st = sb("st", [P, NT, 6])
        mv = sb("mv", [P, NT, 2])
        ve = sb("ve", [P, NT])
        rstd = sb("rstd", [P, NT])
        X1 = sb("X1", [P, NT, D])
        remb = SM[:, 0, 0, :]
        rows = [SM[:, 1, 0, :], SM[:, 1, 1, :]]
        prow = ST[0][:].rearrange("p h i w -> p (h i w)")[:, 0:4 * D].rearrange("p (r n) -> p r n", r=4)

        scratch = [nc.dram_tensor(f"a_band{k}", (RING, NT, P, WIN), F32, kind="Internal").ap() for k in range(2)]

        a = {"ident": ident, "headmask": headmask, "neghalf": neghalf, "X1": X1,
             "ctxT": d["ctxT"], "x2_out": d["x2"],
             "xbq": col[:, 4:6], "xbk": col[:, 6:8], "xbv": row[:, 3, :], "xbo": row[:, 4, :]}
        PTr = sb("PTr", [P, 2, NT, S])

        consts = sem("consts")
        table_weights = sem("table_weights")
        weights = sem("weights")
        zeroed = sem("zeroed")
        tv = sem("table_vector")
        tp = sem("table_pool")
        tt = sem("table_tensor")
        x_in, sp_waited = sem("x_in"), sem("sp_waited")
        xT_ps, xT_sb = sem("xT_ps"), sem("xT_sb")
        q_ps, k_ps, v_ps = sem("q_ps"), sem("k_ps"), sem("v_ps")
        q_sb, k_sb, v_sb, kM_sb = sem("q_sb"), sem("k_sb"), sem("v_sb"), sem("kM_sb")
        xb_in, xb = sem("xb_in"), sem("xb")
        band_ps = [sem("band_ps0"), sem("band_ps1")]
        band_sb = [sem("band_sb0"), sem("band_sb1")]
        band_out = [sem("band_out_even"), sem("band_out_odd")]
        band_in = [[sem("keys_in_even"), sem("keys_in_odd")], [sem("queries_in_even"), sem("queries_in_odd")]]
        sc_ps = sem("sc_ps")
        maxed = sem("maxed")
        exped = sem("exped")
        normed = sem("normed")
        pT_ps, pT_sb = sem("pT_ps"), sem("pT_sb")
        o_ps, o_sb = sem("o_ps"), sem("o_sb")
        y_ps, r_sb, var, rstd_ok, x1_ok = sem("y_ps"), sem("r_sb"), sem("var"), sem("rstd"), sem("x1")
        dv, waited = sem("dve_chain"), sem("dve_waited")
        x = Cross(al, a, d["L0_xattn"], True, x1_ok, [FR0, FR1])
        x.router = router = Router(al, a, d["L0_router"], x, 1, False)

        LINKS = H + 2 + x.VECTOR_LINKS + router.VECTOR_LINKS

        LEAD, NORM, TRANSPOSE, OUTPUT = 5, 1, 2, 3
        CHUNK1, PROJECT, RESULT, VALUES1 = 0, 3, 4, 5
        INPUT, CHUNK0, VALUES0 = 7, 8, 12
        CROSS_LAG = H + 5

        NEAR = [slice(0, S), slice(WIN - S, WIN)]
        FAR = [slice(S, WIN), slice(0, WIN - S)]

        def cross(b, n, do):
            lagged(b, n, H, CROSS_LAG, do)

        with nc.Block() as block:

            @block.sync
            def _(sp):
                for dst, src in ((ident[:], d["ident"]), (headmask[:], d["headmask"]), (col[:], d["L0_col"]),
                                 (remb, d["L0_rel_emb"]),
                                 (row[:], d["L0_row"].partition_broadcast(P)),
                                 (prow, d["L0_prow"].partition_broadcast(P)),
                                 (qM[:, 0:4, :].rearrange("p h n -> p (h n)")[:, 0:2 * REL], d["onehot"])):
                    sp.dma_start(dst, src).then_inc(consts, 16)
                for dst, src in ((kM[:, 0:2, :], d["L0_Wpk"]), (kM[:, 2:4, :], d["L0_Wpq"])):
                    sp.dma_start(dst, src.rearrange("(k p) n -> p k n", p=P)).then_inc(table_weights, 16)
                for dst, src in ((wq[:], d["L0_Wq"]), (wk[:], d["L0_Wk"]), (wv[:], d["L0_Wv"])):
                    sp.dma_start(dst, src.rearrange("(k p) n -> p k n", p=P)).then_inc(weights, 16)
                w4 = d["L0_Wo"].rearrange("(c u j i) n -> j u i c n", u=2, j=HG, i=HD)
                for j in range(HG):
                    for u in range(2):
                        sp.dma_start(wo[32 * j + HD * u:32 * j + HD * (u + 1), :, :], w4[j][u]).then_inc(weights, 16)
                x.load_weights(sp)
                router.load_constants(sp)

                def load_x(b):
                    wait_alone(sp, sp_waited, xT_ps, b)
                    sp.dma_start(XIN[:], d["x"][b].rearrange("(t p) n -> p t n", p=P)).then_inc(x_in, 16)

                def load_residual(b):
                    wait_alone(sp, sp_waited, r_sb, b)
                    sp.dma_start(XB[:], d["x"][b].rearrange("(t p) n -> p t n", p=P)).then_inc(xb_in, 16)

                def bands_out(b, h):
                    for i in range(2):
                        wait_alone(sp, sp_waited, band_sb[i], 32 * b + 2 * h + 2)
                    for k in range(2):
                        wait_alone(sp, sp_waited, band_in[k][h % 2], 16 * (8 * b + h // 2 - 1))
                    for k in range(2):
                        sp.dma_start(scratch[k][h % RING].rearrange("n p w -> p n w"),
                                     ST[k][:, h % RING]).then_inc(band_out[h % 2], 16)

                def bands_back(b, h):
                    wait_alone(sp, sp_waited, band_out[h % 2], 32 * (8 * b + h // 2 + 1))
                    wait_alone(sp, sp_waited, maxed, 16 * b + h + 1 - RING)
                    wait_alone(sp, sp_waited, sc_ps, 16 * b + h + 1 - RING)
                    for k in range(2):
                        wait_alone(sp, sp_waited, band_in[k][h % 2], 16 * (8 * b + h // 2))
                    for k in range(2):
                        base = scratch[k][h % RING]
                        src = bass.AP(base.tensor, base.offset + P - 1, [[WIN - 1, P], [P * WIN, NT], [1, S]])
                        sp.dma_start(SK[k][:, h % RING], src).then_inc(band_in[k][h % 2], 16)

                def step(b, slots=range(H)):
                    for n in slots:
                        lagged(b, n, H, -LEAD, bands_out)
                        lagged(b, n, H, 1 - LEAD, bands_back)
                        if n == 2 and exists(b + 1):
                            load_x(b + 1)
                        if n == PROJECT + 2 and exists(b):
                            load_residual(b)
                        if n == 8 and exists(b):
                            x.load_ctx(sp, b)
                        if n == 8 and exists(b - 2):
                            x.store(sp, b - 2)
                        if n == H - 2 and exists(b - 2) and not (isinstance(b, int) and b - 2 == B - 1):
                            router.store_record(sp, b - 2)

                load_x(0)
                step(-1, range(INPUT, H))
                step(0)
                step(1)
                step(2)
                with sp.Fori(3, B - 1) as b:
                    step(b)
                for b in range(B - 1, B + 2):
                    step(b)
                router.store_record(sp, B - 1)
                sp.wait_ge(x.stored, 16 * B)
                sp.wait_ge(router.saved, 16 * B)

            @block.tensor
            def _(pe):
                pe.wait_ge(consts, 112)
                pe.wait_ge(table_weights, 32)
                pe.wait_ge(tv, 5)
                for k in range(KC):
                    last = nc.tensor.transpose(FR0[:, k * P:(k + 1) * P], remb[:, k * P:(k + 1) * P], ident[:])
                last.then_inc(tt, 1)
                pe.wait_ge(tv, 6)
                for n in range(2):
                    for k in range(KC):
                        last = nc.tensor.matmul(FR1[:, n * D:(n + 1) * D], xT[:, k, 0:P], kM[:, 2 * n + k, :],
                                                start=k == 0, stop=k == KC - 1)
                last.then_inc(tt, 1)
                pe.wait_ge(tv, 8)
                onehot = qM[:, 0:4, :].rearrange("p h n -> p (h n)")
                for n in range(2):
                    for c in range(KC):
                        last = nc.tensor.matmul([BD0, BD1, SC0, SC1][2 * n + c][:, 0:REL],
                                                rows[n][:, c * P:(c + 1) * P], onehot[:, n * REL:(n + 1) * REL],
                                                start=True, stop=True)
                last.then_inc(tt, 1)
                pe.wait_ge(tv, 9)

                def banks_copied(b, n):
                    if n == CHUNK1 + 1 and exists(b):
                        pe.wait_ge(q_sb, 2 * b + 2)
                        pe.wait_ge(k_sb, 2 * b + 2)
                    if n == PROJECT + 1 and exists(b - 1):
                        pe.wait_ge(r_sb, b)
                    if n == VALUES1 + 1 and exists(b):
                        pe.wait_ge(v_sb, 2 * b + 2)
                    if n == INPUT + 1 and exists(b + 1):
                        pe.wait_ge(xT_sb, b + 2)
                    if n == CHUNK0 + 1 and exists(b + 1):
                        pe.wait_ge(q_sb, 2 * b + 3)
                        pe.wait_ge(k_sb, 2 * b + 3)
                    if n == VALUES0 + 1 and exists(b + 1):
                        pe.wait_ge(v_sb, 2 * b + 3)

                def bands_copied(b, n, banks):
                    for i in banks:
                        count = 32 * b + 2 * (n + LEAD + 1)
                        at_least(pe, band_sb[i], min(count, 32 * B) if isinstance(b, int) else count)

                def band(k):
                    def do(b, h):
                        if h % HC == 0:
                            pe.wait_ge(kM_sb if k else q_sb, 2 * b + h // HC + 1)
                        for i in range(NT):
                            at_least(pe, band_sb[i], 32 * b + 2 * h + k)
                            near = NEAR[i]
                            nc.tensor.matmul(BD[i][:, 0:S], (kM if k else qM)[:, h, i * P:(i + 1) * P],
                                             E[k][:, h // HC, P - P * i + near.start:P - P * i + near.stop],
                                             start=True, stop=True).then_inc(band_ps[i], 1)
                    return do

                def scores(b, h):
                    if h % HC == 0:
                        pe.wait_ge(k_sb, 2 * b + h // HC + 1)
                    pe.wait_ge(band_in[1][h % 2], 16 * (8 * b + h // 2 + 1))
                    at_least(pe, maxed, 16 * b + h - 1)
                    for i in range(NT):
                        for j in range(NT):
                            nc.tensor.matmul(SC[h % 2][:, i * S + j * P:i * S + (j + 1) * P],
                                             SK[1][:, h % RING, j, i * P:(i + 1) * P], ident[:],
                                             start=j == 0, stop=False, skip_group_check=True)
                        last = nc.tensor.matmul(SC[h % 2][:, i * S:(i + 1) * S], qM[:, h, i * P:(i + 1) * P],
                                                kT[:, h // HC, :], start=False, stop=True, skip_group_check=True)
                    last.then_inc(sc_ps, 1)

                def transposes(b, h):
                    pe.wait_ge(normed, 16 * b + h + 1)
                    at_least(pe, pT_sb, 16 * b + h)
                    for j in range(NT):
                        for i in range(NT):
                            last = nc.tensor.transpose(PTB[:, j * S + i * P:j * S + (i + 1) * P],
                                                       SM[:, h % RING, i, j * P:(j + 1) * P], ident[:])
                    last.then_inc(pT_ps, 1)

                def outputs(b, h):
                    pe.wait_ge(pT_sb, 16 * b + h + 1)
                    c, u, j = h // HC, h // HG % 2, h % HG
                    if h % HC == 0:
                        pe.wait_ge(v_sb, 2 * b + c + 1)
                        at_least(pe, o_sb, 2 * b + c)
                    for t in range(NT):
                        last = nc.tensor.matmul(PO[32 * j:32 * j + 32, 0:S], v[:, t, h, :], PTr[:, h % 2, t, :],
                                                start=u == 0 and t == 0, stop=u == 1 and t == NT - 1,
                                                skip_group_check=True)
                    last.then_inc(o_ps, 1)

                def project(b):
                    bands_copied(b + 1, PROJECT, [1])
                    pe.wait_ge(o_sb, 2 * b + 2)
                    for t in range(NT):
                        for c in range(KC):
                            last = nc.tensor.matmul(BD1[:, t * D:(t + 1) * D], OT[:, c, t * P:(t + 1) * P],
                                                    wo[:, c, :], start=c == 0, stop=c == KC - 1)
                    last.then_inc(y_ps, 1)

                def front_input(b):
                    bands_copied(b - 1, INPUT, [0])
                    pe.wait_ge(x_in, 16 * b + 16)
                    for t in range(NT):
                        for k in range(KC):
                            last = nc.tensor.transpose(BD0[:, k * S + t * P:k * S + (t + 1) * P],
                                                       XIN[:, t, k * P:(k + 1) * P], ident[:])
                    last.then_inc(xT_ps, 1)

                def chunk(b, c):
                    bands_copied(b if c else b - 1, CHUNK1 if c else CHUNK0, [0, 1])
                    pe.wait_ge(xT_sb, b + 1)
                    for k in range(KC):
                        last = nc.tensor.matmul(BD1[:, 0:S], wq[:, k, c * P:(c + 1) * P], xT[:, k, :],
                                                start=k == 0, stop=k == KC - 1)
                    last.then_inc(q_ps, 1)
                    for k in range(KC):
                        last = nc.tensor.matmul(BD0[:, 0:S], wk[:, k, c * P:(c + 1) * P], xT[:, k, :],
                                                start=k == 0, stop=k == KC - 1)
                    last.then_inc(k_ps, 1)

                def values(b, c):
                    bands_copied(b if c else b - 1, VALUES1 if c else VALUES0, [1])
                    for t in range(NT):
                        for k in range(KC):
                            last = nc.tensor.matmul(BD1[:, t * P:(t + 1) * P], xT[:, k, t * P:(t + 1) * P],
                                                    wv[:, k, c * P:(c + 1) * P], start=k == 0, stop=k == KC - 1)
                    last.then_inc(v_ps, 1)

                def cross_step(b, k):
                    x.tensor(pe, b, k)
                    if exists(b - 1):
                        router.tensor(pe, b - 1, k)

                def step(b, slots=range(H)):
                    for n in slots:
                        banks_copied(b, n)
                        lagged(b, n, H, -LEAD, band(0))
                        lagged(b, n, H, 0, scores)
                        lagged(b, n, H, -LEAD, band(1))
                        lagged(b, n, H, TRANSPOSE, transposes)
                        lagged(b, n, H, OUTPUT, outputs)
                        if n == PROJECT and exists(b - 1):
                            project(b - 1)
                        if n == CHUNK1 and exists(b):
                            chunk(b, 1)
                        if n == VALUES1 and exists(b):
                            values(b, 1)
                        if n == INPUT and exists(b + 1):
                            front_input(b + 1)
                        if n == CHUNK0 and exists(b + 1):
                            chunk(b + 1, 0)
                        if n == VALUES0 and exists(b + 1):
                            values(b + 1, 0)
                        cross(b, n, cross_step)

                pe.wait_ge(weights, (3 + 2 * HG) * 16)
                pe.wait_ge(x.weights, x.WEIGHTS)
                pe.wait_ge(router.consts, router.CONSTS)
                pe.wait_ge(router.ready, 1)
                step(-1, range(INPUT, H))
                step(0)
                step(1)
                step(2)
                with pe.Fori(3, B - 1) as b:
                    step(b)
                for b in range(B - 1, B + 2):
                    step(b)
                for k in range(router.STEPS):
                    router.tensor(pe, B - 1, k)

            @block.scalar
            def _(act):
                act.wait_ge(consts, 112)

                def front_input(b):
                    act.wait_ge(xT_ps, b + 1)
                    at_least(act, v_ps, 2 * b)
                    nc.scalar.activation(xT[:].rearrange("p k n -> p (k n)"), BD0[:], ACT.Copy).then_inc(xT_sb, 1)

                def chunk(b, c):
                    act.wait_ge(k_ps, 2 * b + c + 1)
                    at_least(act, sc_ps, 16 * (b - 1) + HC * (c + 1))
                    at_least(act, kM_sb, 2 * b + c - 1)
                    nc.scalar.activation(kT[:, c, :], BD0[:, 0:S], ACT.Identity,
                                         bias=col[:, 2 + c:3 + c]).then_inc(k_sb, 1)

                def stage(k):
                    def do(b, h):
                        at_least(act, band_out[h % 2], 32 * (8 * b + h // 2 - 1))
                        act.wait_ge(band_ps[0], 32 * b + 2 * h + k + 1)
                        nc.scalar.activation(ST[k][:, h % RING, 0, NEAR[0]], BD0[:, 0:S], ACT.Copy)
                        nc.scalar.activation(ST[k][:, h % RING, 0, FAR[0]], repeated(BD0[:, S - 1:S], WIN - S),
                                             ACT.Copy).then_inc(band_sb[0], 1)
                        if k:
                            act.wait_ge(band_ps[1], 32 * b + 2 * h + 2)
                            nc.scalar.activation(ST[k][:, h % RING, 1, NEAR[1]], BD1[:, 0:S], ACT.Copy)
                            nc.scalar.activation(ST[k][:, h % RING, 1, FAR[1]], repeated(BD1[:, 0:1], WIN - S),
                                                 ACT.Copy).then_inc(band_sb[1], 1)
                    return do

                def exps(b, h):
                    act.wait_ge(maxed, 16 * b + h + 1)
                    r = h % RING
                    for i in range(NT):
                        last = nc.scalar.activation(SM[:, r, i, :], SM[:, r, i, :], ACT.Exp, bias=nb[:, r, i:i + 1],
                                                    scale=-1.0, accum_out=sm[:, r, i:i + 1])
                    last.then_inc(exped, 1)

                def copy_pT(b, h):
                    act.wait_ge(pT_ps, 16 * b + h + 1)
                    at_least(act, o_ps, 16 * b + h - 1)
                    nc.scalar.activation(PTr[:, h % 2, :, :].rearrange("p t s -> p (t s)"), PTB[:],
                                         ACT.Copy).then_inc(pT_sb, 1)

                def copy_o(b, h):
                    if h % HC != HC - 1:
                        return
                    act.wait_ge(o_ps, 16 * b + h + 1)
                    at_least(act, y_ps, b)
                    nc.scalar.activation(OT[:, h // HC, :], PO[:, 0:S], ACT.Copy).then_inc(o_sb, 1)

                def cross_step(b, k):
                    x.scalar(act, b, k)
                    if exists(b - 1):
                        router.scalar(act, b - 1, k)

                def step(b, slots=range(H)):
                    for n in slots:
                        lagged(b, n, H, -LEAD, stage(0))
                        lagged(b, n, H, -LEAD, stage(1))
                        lagged(b, n, H, 0, exps)
                        lagged(b, n, H, TRANSPOSE, copy_pT)
                        lagged(b, n, H, OUTPUT, copy_o)
                        if n == CHUNK1 and exists(b):
                            chunk(b, 1)
                        if n == INPUT and exists(b + 1):
                            front_input(b + 1)
                        if n == CHUNK0 and exists(b + 1):
                            chunk(b + 1, 0)
                        cross(b, n, cross_step)

                step(-1, range(INPUT, H))
                step(0)
                step(1)
                step(2)
                with act.Fori(3, B - 1) as b:
                    step(b)
                for b in range(B - 1, B + 2):
                    step(b)
                for k in range(router.STEPS):
                    router.scalar(act, B - 1, k)

            @block.vector
            def _(dve):
                chain = Chain(dve, dv, waited)
                nc.vector.memset(v[:], 0.0).then_inc(zeroed, 1)
                dve.wait_ge(zeroed, 1)
                nc.vector.memset(x.wo[:], 0.0).then_inc(x.zeroed, 1)
                nc.vector.memset(x.v[:], 0.0).then_inc(x.zeroed, 1)
                dve.wait_ge(consts, 112)
                nc.vector.bn_stats(st[:, 0, :], remb).then_inc(tv, 1)
                dve.wait_ge(tv, 1)
                nc.vector.bn_aggr(mv[:, 0, :], st[:, 0, :]).then_inc(tv, 1)
                dve.wait_ge(tv, 2)
                nc.vector.tensor_scalar(ve[:, 0:1], mv[:, 0, 1:2], LN_EPS, None, ALU.add).then_inc(tv, 1)
                dve.wait_ge(tp, 2)
                nc.vector.tensor_scalar(remb, remb, mv[:, 0, 0:1], rstd[:, 0:1], ALU.subtract,
                                        ALU.mult).then_inc(tv, 1)
                dve.wait_ge(tv, 4)
                nc.vector.tensor_tensor(remb, remb, prow[:, 0, :], ALU.mult).then_inc(zeroed, 1)
                dve.wait_ge(zeroed, 2)
                nc.vector.tensor_tensor(remb, remb, prow[:, 1, :], ALU.add).then_inc(tv, 1)
                dve.wait_ge(tt, 1)
                nc.vector.tensor_copy(xT[:, :, 0:P], FR0[:, 0:D].rearrange("p (k n) -> p k n", k=KC)).then_inc(tv, 1)
                dve.wait_ge(tt, 2)
                for n in range(2):
                    nc.vector.tensor_tensor(rows[n], FR1[:, n * D:(n + 1) * D], prow[:, 2 + n, :],
                                            ALU.add).then_inc(tv, 1)
                dve.wait_ge(tt, 3)
                for n in range(2):
                    for c in range(KC):
                        last = nc.vector.tensor_scalar(E[n][:, c, :], [BD0, BD1, SC0, SC1][2 * n + c][:, 0:REL],
                                                       table_scale, None, ALU.mult)
                last.then_inc(tv, 1)

                def chunk(b, c):
                    dve.wait_ge(q_ps, 2 * b + c + 1)
                    at_least(dve, sc_ps, 16 * (b - 1) + HC * (c + 1))
                    nc.vector.scalar_tensor_tensor(
                        out=qM[:, c * HC:(c + 1) * HC, :], in0=broadcast_mid(BD1[:, 0:S], HC),
                        scalar=col[:, c:c + 1], in1=broadcast_last(headmask[:], S), op0=ALU.add,
                        op1=ALU.mult).then_inc(q_sb, 1)

                def values(b, c):
                    dve.wait_ge(v_ps, 2 * b + c + 1)
                    at_least(dve, o_ps, 16 * (b - 1) + HC * (c + 1))
                    for u in range(2):
                        heads = slice(c * HC + u * HG, c * HC + (u + 1) * HG)
                        cols = slice(u * HG * HD, (u + 1) * HG * HD)
                        last = nc.vector.tensor_tensor(
                            v[:, :, heads, u * HD:(u + 1) * HD],
                            BD1[:, 0:S].rearrange("p (t h) -> p t h", t=NT)[:, :, cols].rearrange(
                                "p t (h n) -> p t h n", n=HD),
                            row[:, 0:2, c * P:(c + 1) * P][:, :, cols].rearrange("p t (h n) -> p t h n", n=HD), ALU.add)
                    last.then_inc(v_sb, 1)

                def stage(b, h):
                    at_least(dve, band_out[h % 2], 32 * (8 * b + h // 2 - 1))
                    dve.wait_ge(band_ps[1], 32 * b + 2 * h + 1)
                    nc.vector.tensor_copy(ST[0][:, h % RING, 1, NEAR[1]], BD1[:, 0:S])
                    nc.vector.tensor_copy(ST[0][:, h % RING, 1, FAR[1]],
                                          repeated(BD1[:, 0:1], WIN - S)).then_inc(band_sb[1], 1)

                def maxima(b, h):
                    r = h % RING
                    dve.wait_ge(band_in[0][h % 2], 16 * (8 * b + h // 2 + 1))
                    dve.wait_ge(sc_ps, 16 * b + h + 1)
                    at_least(dve, pT_ps, 16 * b + h + 1 - RING)
                    own_wait(dve, waited)
                    for i in range(NT):
                        last = nc.vector.tensor_tensor_reduce(
                            out=SM[:, r, i, :], in0=SC[h % 2][:, i * S:(i + 1) * S],
                            in1=SK[0][:, r, i, :], scale=-scale, scalar=3.0e38, op0=ALU.add, op1=ALU.min,
                            accum_out=nb[:, r, i:i + 1])
                    last.then_inc(maxed, 1)

                def norm(b, h):
                    r = h % RING
                    dve.wait_ge(exped, 16 * b + h + 1)
                    chain.link(nc.vector.reciprocal(rs[:, r, :], sm[:, r, :]))
                    for i in range(NT):
                        last = nc.vector.tensor_scalar(SM[:, r, i, :], SM[:, r, i, :], rs[:, r, i:i + 1],
                                                       None, ALU.mult)
                    last.then_inc(normed, 1)

                def residual(b):
                    dve.wait_ge(y_ps, b + 1)
                    dve.wait_ge(xb, b + 1)
                    nc.vector.tensor_tensor(R[:].rearrange("p t n -> p (t n)"), BD1[:],
                                            XB[:].rearrange("p t n -> p (t n)"), ALU.add).then_inc(r_sb, 1)
                    dve.wait_ge(r_sb, b + 1)
                    layernorm_stats(nc, chain, R, st, mv, ve, var, LN_EPS)

                def result(b):
                    dve.wait_ge(rstd_ok, b + 1)
                    at_least(dve, x.x1T_ps, b)
                    at_least(dve, x.x1b, b)
                    layernorm_apply(nc, R, mv, rstd, X1).then_inc(x1_ok, 1)

                def cross_step(b, k):
                    x.vector(dve, b, k, chain)
                    if exists(b - 1):
                        router.vector(dve, b - 1, k, chain)

                def step(b, slots=range(H)):
                    for n in slots:
                        lagged(b, n, H, -LEAD, stage)
                        lagged(b, n, H, 0, maxima)
                        lagged(b, n, H, NORM, norm)
                        if n == PROJECT and exists(b - 1):
                            residual(b - 1)
                        if n == RESULT and exists(b - 1):
                            result(b - 1)
                        if n == CHUNK1 and exists(b):
                            chunk(b, 1)
                        if n == VALUES1 and exists(b):
                            values(b, 1)
                        if n == CHUNK0 and exists(b + 1):
                            chunk(b + 1, 0)
                        if n == VALUES0 and exists(b + 1):
                            values(b + 1, 0)
                        cross(b, n, cross_step)

                router.prepare(dve)
                step(-1, range(INPUT, H))
                step(0)
                step(1)
                step(2)
                start = chain.n
                with dve.Fori(3, B - 1) as b:
                    chain.start(start + LINKS * (b - 3))
                    step(b)
                    assert chain.n == LINKS, (chain.n, LINKS)
                chain.start(start + LINKS * (B - 4))
                for b in range(B - 1, B + 2):
                    step(b)
                for k in range(router.STEPS):
                    router.vector(dve, B - 1, k, chain)

            @block.gpsimd
            def _(pool):
                nc.gpsimd.memset(neghalf[:], -0.5).then_inc(tp, 1)
                pool.wait_ge(tp, 1)
                pool.wait_ge(tv, 3)
                nc.gpsimd.tensor_tensor(rstd[:, 0:1], ve[:, 0:1], neghalf[:, 0:1], ALU.pow).then_inc(tp, 1)
                pool.wait_ge(tt, 3)

                def add_bias(b):
                    pool.wait_ge(xb_in, 16 * b + 16)
                    nc.gpsimd.tensor_tensor(XB[:], XB[:], broadcast_mid(row[:, 2, :], NT), ALU.add).then_inc(xb, 1)

                def chunk(b, c):
                    pool.wait_ge(k_sb, 2 * b + c + 1)
                    at_least(pool, sc_ps, 16 * (b - 1) + HC * (c + 1))
                    nc.gpsimd.tensor_tensor(kM[:, c * HC:(c + 1) * HC, :], broadcast_mid(kT[:, c, :], HC),
                                            broadcast_last(headmask[:], S), ALU.mult).then_inc(kM_sb, 1)

                def deviation(b):
                    pool.wait_ge(var, b + 1)
                    nc.gpsimd.tensor_tensor(rstd[:], ve[:], neghalf[:], ALU.pow).then_inc(rstd_ok, 1)

                def cross_step(b, k):
                    x.pool(pool, b, k)
                    if exists(b - 1):
                        router.pool(pool, b - 1, k)

                def step(b, slots=range(H)):
                    for n in slots:
                        if n == PROJECT and exists(b - 1):
                            deviation(b - 1)
                        if n == CHUNK1 and exists(b):
                            chunk(b, 1)
                        if n == PROJECT + 4 and exists(b):
                            add_bias(b)
                        if n == CHUNK0 and exists(b + 1):
                            chunk(b + 1, 0)
                        cross(b, n, cross_step)

                step(-1, range(INPUT, H))
                step(0)
                step(1)
                step(2)
                with pool.Fori(3, B - 1) as b:
                    step(b)
                for b in range(B - 1, B + 2):
                    step(b)
                for k in range(router.STEPS):
                    router.pool(pool, B - 1, k)
                pool.wait_ge(router.scattered, 16 * NT * B)
        al.end()

def most_tiles(top):
    return (T * top + E8 * (P - 1)) // P


def experts_phase(nc, d, name, top, DF, func, normed):
    TT = T // P
    GT = 4
    GROUPS = TT // GT
    group = lambda g: slice(GT * g, GT * (g + 1))
    FC = DF // P
    MT = most_tiles(top)
    with ExitStack() as phase:
        al = Alloc(nc, phase, name)
        sb, sem = al.sb, al.sem
        ident = sb("ident", [P, P])
        iota = sb("iota", [P, E8 + MT])
        neghalf = sb("neghalf", [P, TT])
        X = sb("X", [P, TT, D])
        REC = sb("REC", [P, TT, FIELDS])
        EX = sb("EX", [P, TT, E8])
        V2 = sb("V2", [P, TT])
        SE = sb("SE", [P, TT])
        G = sb("G", [P, top, TT])
        OH = [sb(f"OH{k}", [P, TT, E8]) for k in range(top)]
        NI = sb("NI", [P, E8], I32)
        NF = sb("NF", [P, E8])
        OFF = sb("OFF", [P, E8 + 1])
        BASE = sb("BASE", [P, E8])
        SEL = sb("SEL", [P, TT, E8])
        PF = sb("PF", [P, top, TT])
        YPOS = sb("YPOS", [P, top, TT], U32)
        SHIFT = sb("SHIFT", [P, E8])
        CMP = sb("CMP", [P, MT, E8 - 1])
        EF = sb("EF", [P, MT])
        EI = sb("EI", [P, MT], I32)
        RF = sb("RF", [P, MT])
        RI = sb("RI", [P, MT], I32)
        LAST = sb("LAST", [P, 1])
        SKIP = sb("SKIP", [P, E8])
        ZF = sb("ZF", [P, E8])
        ZI = sb("ZI", [P, E8], I32)
        NEW = sb("NEW", [P, MT], I32)
        NEF = sb("NEF", [P, MT])
        Z = sb("Z", [P, D])
        W1 = [sb(f"W1_{i}", [P, KC, DF]) for i in range(2)]
        W2 = [sb(f"W2_{i}", [P, FC, D]) for i in range(2)]
        B1 = [sb(f"B1_{i}", [P, FC]) for i in range(2)]
        B2 = [sb(f"B2_{i}", [P, D]) for i in range(2)]
        XS = [sb(f"XS{i}", [P, D]) for i in range(2)]
        XST = [sb(f"XST{i}", [P, KC, P]) for i in range(2)]
        HT = [sb(f"HT{i}", [P, FC, P]) for i in range(2)]
        YS = [sb(f"YS{i}", [P, D]) for i in range(2)]
        YG = sb("YG", [P, top, TT, D])
        st = sb("st", [P, TT, 6])
        mv = sb("mv", [P, TT, 2])
        ve = sb("ve", [P, TT])
        rstd = sb("rstd", [P, TT])
        OUT = sb("OUT", [P, TT, D])

        banks = [al.bank(f"ps{i}") for i in range(8)]
        psT = banks[0:2]
        psH = banks[2:6]
        psY = banks[6:8]

        xs = d["sorted"]
        ys = nc.dram_tensor(name + "results", (MT * P, D), F32, kind="Internal").ap()

        consts, zeros_out = sem("consts"), sem("zeros_out")
        x_in, rec_in = sem("x_in"), sem("rec_in")
        ez, eh = sem("zero_row"), sem("neghalf")
        lg, ex, routed, placed, var, rstd_ok = (sem("lg"), sem("ex"), sem("routed"), sem("placed"), sem("var"),
                                                sem("rstd"))
        xs_in = [sem(f"xs_in{i}") for i in range(2)]
        w1_in = [sem(f"w1_in{i}") for i in range(2)]
        w2_in = [sem(f"w2_in{i}") for i in range(2)]
        xsT_ps, xsT_sb = sem("xsT_ps"), sem("xsT_sb")
        h_ps, h_sb, y_ps, y_sb = sem("h_ps"), sem("h_sb"), sem("y_ps"), sem("y_sb")
        y_out = [sem(f"y_out{i}") for i in range(2)]
        gathered = [sem(f"gathered{g}") for g in range(GROUPS)]
        out_ok, stored = sem("out"), sem("stored")
        dv, sp_waited, pool_waited = sem("dve_chain"), sem("sp_waited"), sem("pool_waited")
        NB = FC // 4
        W1_PARTS, W2_PARTS = 2, 2
        assert MT % 2

        with nc.Block() as block:

            @block.sync
            def _(sp):
                sp.dma_start(REC[:], d["record"].rearrange("t p f -> p t f")).then_inc(rec_in, 16)
                for dst, src in ((iota[:], d["iota"][:, 0:E8 + MT]), (ident[:], d["ident"])):
                    sp.dma_start(dst, src).then_inc(consts, 16)
                sp.wait_ge(ez, 1)
                sp.wait_ge(routed, 1)
                for e in range(E8):
                    row = sp.value_load(ZI[0:1, e:e + 1], min_val=0, max_val=E8 * ROOM - P)
                    sp.dma_start(xs[bass.ds(row, P), :], Z[:]).then_inc(zeros_out, 16)
                def first(n, i):
                    e = sp.value_load(EI[0:1, bass.ds(n, 1)], min_val=0, max_val=E8 - 1)
                    fresh = sp.value_load(NEW[0:1, bass.ds(n, 1)], min_val=0, max_val=1)
                    sp.dma_start(W1[i][:], d["W1"][e].rearrange("(k p) n -> p k n", p=P), cond=fresh,
                                 cond_hint=True).then_inc(w1_in[i], 16)
                    sp.dma_start(B1[i][:], d["b1"][e]).then_inc(w1_in[i], 16)

                def rows(n, i):
                    row = sp.value_load(RI[0:1, bass.ds(n, 1)], min_val=0, max_val=E8 * ROOM - P)
                    sp.dma_start(XS[i][:], xs[bass.ds(row, P), :]).then_inc(xs_in[i], 16)

                first(0, 0)
                sp.wait_ge(zeros_out, 16 * E8)
                for n in range(2):
                    rows(n, n)
                first(1, 1)
                sp.dma_start(X[:], d["x"].rearrange("(t p) n -> p t n", p=P)).then_inc(x_in, 16)

                def tile(n, i):
                    sp.wait_ge(xsT_ps, n - 1)
                    own_wait(sp, sp_waited)
                    rows(n, i)
                    sp.wait_ge(h_ps, NB * (n - 1))
                    sp.wait_ge(h_sb, NB * (n - 1))
                    own_wait(sp, sp_waited)
                    first(n, i)

                with sp.Fori(1, MT // 2) as m:
                    for i in range(2):
                        tile(2 * m + i, i)
                tile(MT - 1, 0)
                for g in range(GROUPS):
                    sp.wait_ge(out_ok, g + 1)
                    sp.dma_start(d["out"].rearrange("(t p) n -> p t n", p=P)[:, group(g), :],
                                 OUT[:, group(g), :]).then_inc(stored, 16)
                sp.wait_ge(stored, 16 * GROUPS)

            @block.tensor
            def _(pe):
                pe.wait_ge(consts, 32)

                def transposes(n, i, j):
                    pe.wait_ge(xs_in[i], 16 * (j + 1))
                    at_least(pe, xsT_sb, n - 1)
                    for k in range(KC):
                        last = nc.tensor.transpose(psT[i][:, k * P:(k + 1) * P], XS[i][:, k * P:(k + 1) * P], ident[:])
                    last.then_inc(xsT_ps, 1)

                def up(n, i, j):
                    pe.wait_ge(w1_in[i], 16 * W1_PARTS * (j + 1))
                    pe.wait_ge(xsT_sb, n + 1)
                    for f in range(FC):
                        bank = psH[(i * NB + f // 4) % 4]
                        if f % 4 == 0:
                            at_least(pe, h_sb, (n - 4 // NB + 1) * NB if NB * 2 > 4 else NB * (n - 1))
                        for k in range(KC):
                            last = nc.tensor.matmul(bank[:, (f % 4) * P:(f % 4 + 1) * P], W1[i][:, k, f * P:(f + 1) * P],
                                                    XST[i][:, k, :], start=k == 0, stop=k == KC - 1)
                        if f % 4 == 3:
                            last.then_inc(h_ps, 1)

                def down(n, i, j):
                    pe.wait_ge(h_sb, NB * (n + 1))
                    pe.wait_ge(w2_in[i], 16 * W2_PARTS * (j + 1))
                    at_least(pe, y_sb, n - 1)
                    for f in range(FC):
                        last = nc.tensor.matmul(psY[i][:, 0:D], HT[i][:, f, :], W2[i][:, f, :],
                                                start=f == 0, stop=f == FC - 1)
                    last.then_inc(y_ps, 1)

                transposes(0, 0, 0)
                up(0, 0, 0)
                transposes(1, 1, 0)
                up(1, 1, 0)
                transposes(2, 0, 1)
                down(0, 0, 0)

                def pair(m):
                    up(2 * m, 0, m)
                    transposes(2 * m + 1, 1, m)
                    down(2 * m - 1, 1, m - 1)
                    up(2 * m + 1, 1, m)
                    transposes(2 * m + 2, 0, m + 1)
                    down(2 * m, 0, m)

                pair(1)
                with pe.Fori(2, MT // 2) as m:
                    pair(m)
                up(MT - 1, 0, MT // 2)
                down(MT - 2, 1, MT // 2 - 1)
                down(MT - 1, 0, MT // 2)

            @block.scalar
            def _(act):
                def copy_rows(n, i):
                    act.wait_ge(xsT_ps, n + 1)
                    nc.scalar.activation(XST[i][:].rearrange("p k n -> p (k n)"), psT[i][:, 0:D],
                                         ACT.Copy).then_inc(xsT_sb, 1)

                def up(n, i, j):
                    act.wait_ge(w1_in[i], 16 * W1_PARTS * (j + 1))
                    at_least(act, y_ps, n - 1)
                    for f in range(FC):
                        bank = psH[(i * NB + f // 4) % 4]
                        if f % 4 == 0:
                            act.wait_ge(h_ps, NB * n + f // 4 + 1)
                        last = nc.scalar.activation(HT[i][:, f, :], bank[:, (f % 4) * P:(f % 4 + 1) * P], func,
                                                    bias=B1[i][:, f:f + 1])
                        if f % 4 == 3:
                            last.then_inc(h_sb, 1)

                act.wait_ge(lg, 2)
                nc.scalar.activation(EX[:].rearrange("p t e -> p (t e)"), EX[:].rearrange("p t e -> p (t e)"),
                                     ACT.Exp).then_inc(ex, 1)
                nc.scalar.activation(V2[:], V2[:], ACT.Exp).then_inc(ex, 1)

                copy_rows(0, 0)
                for n in range(2):
                    up(n, n, 0)
                    copy_rows(n + 1, (n + 1) % 2)
                with act.Fori(1, MT // 2) as m:
                    for i in range(2):
                        up(2 * m + i, i, m)
                        copy_rows(2 * m + i + 1, 1 - i)
                up(MT - 1, 0, MT // 2)

            @block.vector
            def _(dve):
                chain = Chain(dve, dv)
                nc.vector.memset(Z[:], 0.0).then_inc(ez, 1)
                nc.vector.memset(OFF[:, 0:1], 0.0)
                dve.wait_ge(consts, 32)
                dve.wait_ge(rec_in, 16)
                chain.link(nc.vector.tensor_scalar(BASE[:], iota[:, 0:E8], float(ROOM), None, ALU.mult))
                total = REC[:, TT - 1, SO_FAR]
                chain.link(nc.vector.tensor_scalar(NF[:], total, float(P - 1), None, ALU.add))
                nc.vector.tensor_tensor(ZF[:], total, BASE[:], ALU.add)
                chain.link(nc.vector.tensor_copy(NI[:], NF[:]))
                shift = P.bit_length() - 1
                nc.vector.tensor_copy(ZI[:], ZF[:])
                chain.link(nc.vector.tensor_scalar(NI[:], NI[:], shift, shift, ALU.arith_shift_right,
                                                   ALU.logical_shift_left))
                chain.link(nc.vector.tensor_copy(NF[:], NI[:]))
                nc.vector.tensor_scalar(SKIP[:], NF[:], -1.0, float(ROOM), ALU.mult, ALU.add)
                for e in range(E8):
                    chain.link(nc.vector.tensor_tensor(OFF[:, e + 1:e + 2], OFF[:, e:e + 1], NF[:, e:e + 1], ALU.add))
                tile_rows = iota[:, E8:E8 + MT]
                chain.link(nc.vector.tensor_tensor(CMP[:], broadcast_mid(OFF[:, 1:E8], MT),
                                                   broadcast_last(tile_rows, E8 - 1), ALU.is_le))
                chain.link(nc.vector.tensor_reduce(EF[:], CMP[:], AXX, ALU.add))
                nc.vector.tensor_copy(EI[:], EF[:])
                chain.link(nc.vector.tensor_tensor(CMP[:], CMP[:], broadcast_mid(SKIP[:, 0:E8 - 1], MT), ALU.mult))
                chain.link(nc.vector.tensor_reduce(RF[:], CMP[:], AXX, ALU.add))
                chain.link(nc.vector.tensor_tensor(RF[:], RF[:], tile_rows, ALU.add))
                chain.link(nc.vector.tensor_scalar(LAST[:], NF[:, E8 - 1:E8], float(P), float((E8 - 1) * ROOM),
                                                   ALU.max, ALU.add))
                chain.link(nc.vector.tensor_scalar(LAST[:], LAST[:], float(-P), None, ALU.add))
                chain.link(nc.vector.tensor_scalar(RF[:], RF[:], LAST[:], None, ALU.min))
                nc.vector.tensor_copy(RI[:], RF[:])
                nc.vector.memset(NEF[:, 0:2], 1.0)
                chain.link(nc.vector.tensor_tensor(NEF[:, 2:MT], EF[:, 2:MT], EF[:, 0:MT - 2], ALU.not_equal))
                nc.vector.tensor_copy(NEW[:], NEF[:]).then_inc(routed, 1)
                nc.vector.tensor_tensor(EX[:], REC[:, :, LOGITS], broadcast_last(REC[:, :, BEST.start], E8),
                                        ALU.subtract).then_inc(lg, 1)
                nc.vector.tensor_tensor(V2[:], REC[:, :, BEST.start + 1], REC[:, :, BEST.start],
                                        ALU.subtract).then_inc(lg, 1)
                chain.link(nc.vector.tensor_tensor(SHIFT[:], OFF[:, 0:E8], BASE[:], ALU.subtract))
                ahead = REC[:, :, AHEAD]
                chain.link(nc.vector.tensor_tensor(ahead, ahead, broadcast_mid(SHIFT[:], TT), ALU.add))
                for k in range(top):
                    chain.link(nc.vector.tensor_tensor(OH[k][:], broadcast_mid(iota[:, 0:E8], TT),
                                                       broadcast_last(REC[:, :, NUMBER.start + k], E8), ALU.is_equal))
                    chain.link(nc.vector.tensor_tensor(SEL[:], ahead, OH[k][:], ALU.mult))
                    chain.link(nc.vector.tensor_reduce(PF[:, k, :], SEL[:], AXX, ALU.add))
                nc.vector.tensor_copy(YPOS[:], PF[:]).then_inc(placed, 1)
                dve.wait_ge(ex, 2)
                chain.link(nc.vector.tensor_reduce(SE[:], EX[:], AXX, ALU.add))
                chain.link(nc.vector.reciprocal(G[:, 0, :], SE[:]))
                if top > 1:
                    chain.link(nc.vector.tensor_tensor(G[:, 1, :], G[:, 0, :], V2[:], ALU.mult))
                    chain.link(nc.vector.scalar_tensor_tensor(out=SE[:], in0=G[:, 0, :], scalar=1e-8, in1=G[:, 1, :],
                                                              op0=ALU.add, op1=ALU.add))
                    chain.link(nc.vector.reciprocal(V2[:], SE[:]))
                    chain.link(nc.vector.tensor_tensor(G[:], G[:], broadcast_mid(V2[:], top), ALU.mult))

                def down(n, i, j):
                    dve.wait_ge(y_ps, n + 1)
                    dve.wait_ge(w2_in[i], 16 * W2_PARTS * (j + 1))
                    at_least(dve, y_out[i], 16 * j)
                    nc.vector.tensor_tensor(YS[i][:], psY[i][:, 0:D], B2[i][:], ALU.add).then_inc(y_sb, 1)

                dve.wait_ge(x_in, 16)
                if normed:
                    chain.link(nc.vector.tensor_scalar(X[:], X[:], 2.0, None, ALU.mult))

                down(0, 0, 0)
                down(1, 1, 0)
                with dve.Fori(1, MT // 2) as m:
                    down(2 * m, 0, m)
                    down(2 * m + 1, 1, m)
                if MT % 2:
                    down(MT - 1, 0, MT // 2)
                def combine(g):
                    dve.wait_ge(gathered[g], 16 * top * GT)
                    for k in range(top):
                        for t in range(GT * g, GT * (g + 1)):
                            last = nc.vector.scalar_tensor_tensor(out=X[:, t, :], in0=YG[:, k, t, :],
                                                                  scalar=G[:, k, t:t + 1], in1=X[:, t, :],
                                                                  op0=ALU.mult, op1=ALU.add)
                        chain.link(last)
                    for t in range(GT * g, GT * (g + 1)):
                        last = nc.vector.bn_stats(st[:, t, :], X[:, t, :])
                    chain.link(last)
                    for t in range(GT * g, GT * (g + 1)):
                        last = nc.vector.bn_aggr(mv[:, t, :], st[:, t, :])
                    chain.link(last)
                    nc.vector.tensor_scalar(ve[:, group(g)], mv[:, group(g), 1], LN_EPS, None, ALU.add).then_inc(var, 1)

                def result(g):
                    dve.wait_ge(rstd_ok, g + 1)
                    for t in range(GT * g, GT * (g + 1)):
                        last = nc.vector.tensor_scalar(OUT[:, t, :], X[:, t, :], mv[:, t, 0:1], rstd[:, t:t + 1],
                                                       ALU.subtract, ALU.mult)
                    last.then_inc(out_ok, 1)

                for g in range(GROUPS):
                    combine(g)
                    if g >= 2:
                        result(g - 2)
                result(GROUPS - 2)
                result(GROUPS - 1)

            @block.gpsimd
            def _(pool):
                nc.gpsimd.memset(neghalf[:], -0.5).then_inc(eh, 1)
                pool.wait_ge(eh, 1)

                def deviation(g, n):
                    pool.wait_ge(var, n)
                    nc.gpsimd.tensor_tensor(rstd[:, group(g)], ve[:, group(g)], neghalf[:, group(g)],
                                            ALU.pow).then_inc(rstd_ok, 1)

                pool.wait_ge(routed, 1)

                def second(n, i):
                    e = pool.value_load(EI[0:1, bass.ds(n, 1)], min_val=0, max_val=E8 - 1)
                    fresh = pool.value_load(NEW[0:1, bass.ds(n, 1)], min_val=0, max_val=1)
                    at_least(pool, y_ps, n - 1)
                    at_least(pool, y_sb, n - 1)
                    own_wait(pool, pool_waited)
                    pool.dma_start(W2[i][:], d["W2"][e].rearrange("(k p) n -> p k n", p=P), cond=fresh,
                                   cond_hint=True).then_inc(w2_in[i], 16)
                    pool.dma_start(B2[i][:], d["b2"][e].partition_broadcast(P)).then_inc(w2_in[i], 16)

                def store(n, i):
                    pool.wait_ge(y_sb, n + 1)
                    own_wait(pool, pool_waited)
                    pool.dma_start(ys.rearrange("(m p) n -> m p n", p=P)[n], YS[i][:]).then_inc(y_out[i], 16)

                second(0, 0)
                second(1, 1)
                store(0, 0)
                with pool.Fori(1, MT // 2) as m:
                    second(2 * m, 0)
                    store(2 * m - 1, 1)
                    second(2 * m + 1, 1)
                    store(2 * m, 0)
                if MT % 2:
                    second(MT - 1, 0)
                    store(MT - 2, 1)
                    store(MT - 1, 0)
                else:
                    store(MT - 1, 1)
                pool.wait_ge(y_out[0], 16 * ((MT + 1) // 2))
                pool.wait_ge(y_out[1], 16 * (MT // 2))
                pool.wait_ge(placed, 1)
                for g in range(GROUPS):
                    for t in range(GT * g, GT * (g + 1)):
                        for k in range(top):
                            nc.gpsimd.indirect_dma_start(YG[:, k, t, :], None, ys,
                                                         bass.IndirectOffsetOnAxis(YPOS[:, k, t:t + 1], 0)).then_inc(gathered[g], 16)
                    if g:
                        deviation(g - 1, g)
                deviation(GROUPS - 1, GROUPS)
        al.end()

DH = 64
PM = 16
CH = H * DH // P
INNER = H * DH
RMS_EPS = 1e-6


def segment_attention_phase(nc, d):
    with ExitStack() as phase:
        al = Alloc(nc, phase, "c_")
        sb, sem = al.sb, al.sem
        scale = float(DH) ** -0.5
        NK = PM + P
        RING = 4

        FR0, FR1, QK, RT, SC0, SC1, PTB, PO = [al.bank(n) for n in
                                               ("FR0", "FR1", "QK", "RT", "SC0", "SC1", "PTB", "PO")]
        SC = [SC0, SC1]
        ident = sb("ident", [P, P])
        headmask = sb("headmask", [P, HC])
        col = sb("col", [P, 6])
        row = sb("row", [P, 3, D])
        cs = sb("cs", [P, 2, 2, S])
        rot = sb("rot", [P, P])
        mask = sb("mask", [P, NK])
        neghalf = sb("neghalf", [P, NT])
        wqkv = sb("wqkv", [P, KC, 3 * INNER])
        wout = sb("wout", [P, CH, D])
        XIN = sb("XIN", [P, NT, D])
        XB = sb("XB", [P, NT, D])
        XR = sb("XR", [P, NT, D])
        xT = sb("xT", [P, KC, S])
        raw, t1, t2 = [[sb(f"{n}{i}", [P, 2, S]) for i in range(2)] for n in ("raw", "t1", "t2")]
        qT = sb("qT", [P, CH, S])
        kP = sb("kP", [P, CH, 2, NT, NK])
        v = sb("v", [P, NT, INNER])
        vpm = sb("vpm", [P, 2, 8 * DH])
        SM = sb("SM", [P, RING, 2, NK])
        PP = sb("PP", [P, 2, 8 * PM])
        nb = sb("nb", [P, RING, 2])
        sm = sb("sm", [P, RING, 2])
        rs = sb("rs", [P, RING, 2])
        PTr = sb("PTr", [P, 16, P])
        PPT = sb("PPT", [P, 2, P])
        OT = sb("OT", [P, CH, S])
        R = sb("R", [P, NT, D])
        sq = sb("sq", [P, NT, D])
        ss = sb("ss", [P, NT])
        ms = sb("ms", [P, NT])
        rr = sb("rr", [P, NT])
        st = sb("st", [P, NT, 6])
        mv = sb("mv", [P, NT, 2])
        ve = sb("ve", [P, NT])
        rstd = sb("rstd", [P, NT])
        X1 = sb("X1", [P, NT, D])
        a = {"ident": ident, "headmask": headmask, "neghalf": neghalf, "X1": X1,
             "ctxT": d["ctxT"], "x2_out": d["x5"],
             "xbq": col[:, 2:4], "xbk": col[:, 4:6], "xbv": row[:, 1, :], "xbo": row[:, 2, :]}
        consts, late, zeroed, hv = sem("consts"), sem("late_consts"), sem("zeroed"), sem("neghalf")
        x_in = sem("x_in")
        ms_ok, rr_ok, xr, xr_ps, xT_sb = sem("ms"), sem("rr"), sem("xr"), sem("xr_ps"), sem("xT_sb")
        qk_ps, raw_sb, t1_sb, rot_ps, t2_sb, q_sb, k_sb = (sem("qk_ps"), sem("raw_sb"), sem("t1_sb"), sem("rot_ps"),
                                                            sem("t2_sb"), sem("q_sb"), sem("k_sb"))
        v_ps, v_sb, xb = sem("v_ps"), sem("v_sb"), sem("xb")
        sc_ps, maxed, exped, normed = sem("sc_ps"), sem("maxed"), sem("exped"), sem("normed")
        pT_ps, pT_sb, pp_ps, pp_sb, o_ps, o_sb = (sem("pT_ps"), sem("pT_sb"), sem("pp_ps"), sem("pp_sb"),
                                                  sem("o_ps"), sem("o_sb"))
        y_ps, r_sb, var, rstd_ok, x1_ok = sem("y_ps"), sem("r_sb"), sem("var"), sem("rstd"), sem("x1")
        dv, waited, sp_waited = sem("dve_chain"), sem("dve_waited"), sem("sp_waited")
        U = NT * H
        order = [(w, 8 * o + h) for o in range(2) for w in range(NT) for h in range(8)]
        x = Cross(al, a, d["L1_xattn"], False, x1_ok, [FR0, FR1])
        x.router = router = Router(al, a, d["L1_router"], x, 2, True)
        LINKS = 1 + U // 2 + 2 + x.VECTOR_LINKS + router.VECTOR_LINKS

        def chunk_at(n):
            return (n % 16) // 4 + (CH // 2 if n < 16 else 0) if n % 4 == 0 else None

        def values_at(n):
            return (n % 16 - 10) // 4 + (2 if n < 16 else 0) if n % 16 in (10, 14) else None

        NORM, TRANSPOSE, OUTPUT, COPY_O, PROJECT, RESIDUAL, RESULT = 2, 5, 6, 7, 8, 9, 10
        CROSS = {}
        for k in range(x.STEPS):
            CROSS.setdefault(RESULT + (7 * k // 6 if k < x.PAIRS[0] else 11 + (k - x.PAIRS[0]) * 4 // 3), []).append(k)

        with nc.Block() as block:

            @block.sync
            def _(sp):
                def load_x(b):
                    at_least(sp, xb, b)
                    at_least(sp, xr, b)
                    own_wait(sp, sp_waited)
                    sp.dma_start(XIN[:], d["x"][b].rearrange("(t p) n -> p t n", p=P)).then_inc(x_in, 16)

                load_x(0)
                for dst, src in ((ident[:], d["ident"]), (headmask[:], d["headmask"]), (col[:], d["L1_col"]),
                                 (row[:], d["L1_row"].partition_broadcast(P)), (cs[:], d["cossin"]),
                                 (rot[:], d["rot"]), (mask[:], d["mask"]),
                                 (wqkv[:], d["w_qkv"].rearrange("(k p) n -> p k n", p=P))):
                    sp.dma_start(dst, src).then_inc(consts, 16)
                sp.dma_start(wout[:], d["w_out"].rearrange("(k p) n -> p k n", p=P)).then_inc(late, 16)
                sp.wait_ge(zeroed, 2)
                pmk = d["pm_kT"].rearrange("(c u n) k -> u n c k", u=2, n=DH)
                for u in range(2):
                    for w in range(NT):
                        sp.dma_start(kP[u * DH:(u + 1) * DH, :, u, w, 0:PM], pmk[u]).then_inc(late, 16)
                for h in range(H):
                    sp.dma_start(vpm[(h % 8) * PM:(h % 8 + 1) * PM, h // 8, (h % 8) * DH:(h % 8 + 1) * DH],
                                 d["pm_v"][h]).then_inc(late, 16)
                x.load_weights(sp)
                router.load_constants(sp)

                def step(b, first=False):
                    load_x(b + 1)
                    x.load_ctx(sp, b)
                    if exists(b - 2):
                        router.store_record(sp, b - 2)
                    if not first:
                        x.store(sp, b - 1)

                step(0, first=True)
                step(1)
                step(2)
                with sp.Fori(3, B - 1) as b:
                    step(b)
                x.load_ctx(sp, B - 1)
                router.store_record(sp, B - 3)
                x.store(sp, B - 2)
                router.store_record(sp, B - 2)
                x.store(sp, B - 1)
                router.store_record(sp, B - 1)
                sp.wait_ge(x.stored, 16 * B)
                sp.wait_ge(router.saved, 16 * B)

            ALL_CONSTS, LATE = 16 * 8, 16 * (1 + 4 + H)

            @block.tensor
            def _(pe):
                pe.wait_ge(consts, ALL_CONSTS)

                def front_input(b):
                    pe.wait_ge(xr, b + 1)
                    at_least(pe, v_sb, 4 * b)
                    for t in range(NT):
                        for k in range(KC):
                            last = nc.tensor.transpose(QK[:, k * S + t * P:k * S + (t + 1) * P],
                                                       XR[:, t, k * P:(k + 1) * P], ident[:])
                    last.then_inc(xr_ps, 1)

                def project(b, c):
                    if c == 0:
                        pe.wait_ge(xT_sb, b + 1)
                    else:
                        pe.wait_ge(raw_sb, CH * b + c)
                    if c % 4 == 3 or c == 4:
                        pe.wait_ge(v_sb, 4 * b + (2 if c == 4 else 2 * (c // 4) + 1))
                    for n in range(2):
                        for k in range(KC):
                            last = nc.tensor.matmul(QK[:, n * S:(n + 1) * S],
                                                    wqkv[:, k, n * INNER + c * P:n * INNER + (c + 1) * P],
                                                    xT[:, k, :], start=k == 0, stop=k == KC - 1)
                    last.then_inc(qk_ps, 1)

                def rotate(b, c):
                    pe.wait_ge(raw_sb, CH * b + c + 1)
                    at_least(pe, t2_sb, CH * b + c)
                    nc.tensor.matmul(RT[:], rot[:], raw[c % 2][:].rearrange("p a s -> p (a s)"),
                                     start=True, stop=True).then_inc(rot_ps, 1)

                def values(b, n):
                    pe.wait_ge(raw_sb, CH * b + 4 * (n // 2) + 3 + n % 2)
                    for k in range(KC):
                        last = nc.tensor.matmul(QK[:], xT[:, k, (n % 2) * P:(n % 2 + 1) * P],
                                                wqkv[:, k, 2 * INNER + (n // 2) * 512:2 * INNER + (n // 2 + 1) * 512],
                                                start=k == 0, stop=k == KC - 1)
                    last.then_inc(v_ps, 1)

                def front(b, n):
                    if chunk_at(n) is not None:
                        project(b, chunk_at(n))
                    if n >= 2 and chunk_at(n - 2) is not None:
                        rotate(b, chunk_at(n - 2))
                    if values_at(n) is not None:
                        values(b, values_at(n))

                def scores(b, n):
                    if n % 2:
                        return
                    w, h = order[n]
                    if w == 0:
                        pe.wait_ge(q_sb, CH * b + h // 2 + 1)
                        pe.wait_ge(k_sb, CH * b + h // 2 + 1)
                    at_least(pe, maxed, U // 2 * b + n // 2 - 1)
                    for u in range(2):
                        last = nc.tensor.matmul(SC[n // 2 % 2][:, u * NK:(u + 1) * NK], qT[:, h // 2, w * P:(w + 1) * P],
                                                kP[:, h // 2, u, w, :], start=True, stop=True)
                    last.then_inc(sc_ps, 1)

                def transposes(b, n):
                    if n % 2:
                        return
                    pe.wait_ge(normed, U // 2 * b + n // 2 + 1)
                    at_least(pe, pT_sb, U // 2 * b + n // 2)
                    if n % 8 == 6:
                        at_least(pe, pp_sb, U // 8 * b + n // 8)
                        nc.tensor.transpose(PTB[:, 2 * P:3 * P], PP[:, (n // 8) % 2, :], ident[:]).then_inc(pp_ps, 1)
                    for u in range(2):
                        last = nc.tensor.transpose(PTB[:, u * P:(u + 1) * P], SM[:, n // 2 % RING, u, PM:NK], ident[:])
                    last.then_inc(pT_ps, 1)

                def outputs(b, n):
                    if n % 8 != 6:
                        return
                    m = n // 8
                    pe.wait_ge(pT_sb, U // 2 * b + n // 2 + 1)
                    pe.wait_ge(pp_sb, U // 8 * b + m + 1)
                    pe.wait_ge(v_sb, 4 * b + m + 1)
                    if m == 0:
                        at_least(pe, r_sb, b)
                    at_least(pe, o_sb, U // 8 * b + m)
                    for j in range(8):
                        w, h = order[8 * m + j]
                        cols = slice((j // 2) * P, (j // 2 + 1) * P)
                        nc.tensor.matmul(PO[(h % 2) * DH:(h % 2 + 1) * DH, cols], v[:, w, h * DH:(h + 1) * DH],
                                         PTr[:, 8 * (m % 2) + j, :], start=True, stop=False, skip_group_check=True)
                        if h % 2 == 1:
                            last = nc.tensor.matmul(PO[:, cols], vpm[:, h // 8, (h % 8 - 1) * DH:(h % 8 + 1) * DH],
                                                    PPT[:, m % 2, :], start=False, stop=True, skip_group_check=True)
                    last.then_inc(o_ps, 1)

                def output_projection(b, n):
                    if n != U - 2:
                        return
                    pe.wait_ge(o_sb, U // 8 * (b + 1))
                    for t in range(NT):
                        for c in range(CH):
                            last = nc.tensor.matmul(PO[:, t * D:(t + 1) * D], OT[:, c, t * P:(t + 1) * P],
                                                    wout[:, c, :], start=c == 0, stop=c == CH - 1)
                    last.then_inc(y_ps, 1)

                def behind(b, n):
                    lagged(b, n, U, TRANSPOSE, transposes)
                    lagged(b, n, U, OUTPUT, outputs)
                    lagged(b, n, U, PROJECT, output_projection)

                def step(b, first=False, last=False):
                    for n in range(U):
                        scores(b, n)
                        behind(b, n)
                        if n < 16:
                            front(b, n)
                        if n == 15 and not last:
                            front_input(b + 1)
                        if n >= 16 and not last:
                            front(b + 1, n)
                        if not first:
                            for k in CROSS.get(n, ()):
                                x.tensor(pe, b - 1, k)
                                if exists(b - 2):
                                    router.tensor(pe, b - 2, k)

                front_input(0)
                for n in range(16, U):
                    front(0, n)
                pe.wait_ge(late, LATE)
                pe.wait_ge(x.weights, x.WEIGHTS)
                pe.wait_ge(router.consts, router.CONSTS)
                pe.wait_ge(router.ready, 1)
                step(0, first=True)
                step(1)
                step(2)
                with pe.Fori(3, B - 1) as b:
                    step(b)
                step(B - 1, last=True)
                for n in range(PROJECT + 1):
                    behind(B, n)
                for k in range(x.STEPS):
                    x.tensor(pe, B - 1, k)
                    router.tensor(pe, B - 2, k)
                for k in range(router.STEPS):
                    router.tensor(pe, B - 1, k)

            @block.scalar
            def _(act):
                act.wait_ge(consts, ALL_CONSTS)

                def front_input(b):
                    act.wait_ge(xr_ps, b + 1)
                    for k in range(KC):
                        last = nc.scalar.activation(xT[:, k, :], QK[:, k * S:(k + 1) * S], ACT.Copy,
                                                    scale=col[:, k:k + 1])
                    last.then_inc(xT_sb, 1)

                def front(b, n):
                    c, m = chunk_at(n), values_at(n)
                    if c is not None:
                        act.wait_ge(qk_ps, CH * b + c + 1)
                        at_least(act, rot_ps, CH * b + c - 1)
                        at_least(act, t1_sb, CH * b + c - 1)
                        nc.scalar.activation(raw[c % 2][:].rearrange("p a s -> p (a s)"), QK[:],
                                             ACT.Copy).then_inc(raw_sb, 1)
                    if m is not None:
                        act.wait_ge(v_ps, 4 * b + m + 1)
                        at_least(act, o_ps, 4 * (b - 1) + 2 * (m // 2) + 2)
                        nc.scalar.activation(v[:, m % 2, (m // 2) * 512:(m // 2 + 1) * 512], QK[:],
                                             ACT.Copy).then_inc(v_sb, 1)

                def exps(b, n):
                    if n % 2:
                        return
                    r = n // 2 % RING
                    act.wait_ge(maxed, U // 2 * b + n // 2 + 1)
                    for u in range(2):
                        last = nc.scalar.activation(SM[:, r, u, :], SM[:, r, u, :], ACT.Exp, bias=nb[:, r, u:u + 1],
                                                    scale=-1.0, accum_out=sm[:, r, u:u + 1])
                    last.then_inc(exped, 1)

                def copy_pT(b, n):
                    if n % 2:
                        return
                    act.wait_ge(pT_ps, U // 2 * b + n // 2 + 1)
                    if n % 8 == 0:
                        at_least(act, o_ps, U // 8 * b + n // 8 - 1)
                    if n % 8 == 6:
                        nc.scalar.activation(PPT[:, (n // 8) % 2, :], PTB[:, 2 * P:3 * P], ACT.Copy).then_inc(pp_sb, 1)
                    nc.scalar.activation(PTr[:, n % 16:n % 16 + 2, :].rearrange("p h s -> p (h s)"), PTB[:, 0:2 * P],
                                         ACT.Copy).then_inc(pT_sb, 1)

                def copy_o(b, n):
                    if n % 8 != 6:
                        return
                    m = n // 8
                    act.wait_ge(o_ps, U // 8 * b + m + 1)
                    if m == 0:
                        at_least(act, y_ps, b)
                    w, h = order[8 * m]
                    nc.scalar.activation(OT[:, h // 2:h // 2 + 4, w * P:(w + 1) * P],
                                         PO[:].rearrange("p (c s) -> p c s", c=4), ACT.Copy).then_inc(o_sb, 1)

                def behind(b, n):
                    lagged(b, n, U, TRANSPOSE, copy_pT)
                    lagged(b, n, U, COPY_O, copy_o)

                def step(b, first=False, last=False):
                    for n in range(U):
                        behind(b, n)
                        exps(b, n)
                        if n < 16:
                            front(b, n)
                        if n == 15 and not last:
                            front_input(b + 1)
                        if n >= 16 and not last:
                            front(b + 1, n)
                        if not first:
                            for k in CROSS.get(n, ()):
                                x.scalar(act, b - 1, k)
                                if exists(b - 2):
                                    router.scalar(act, b - 2, k)

                front_input(0)
                for n in range(16, U):
                    front(0, n)
                step(0, first=True)
                step(1)
                step(2)
                with act.Fori(3, B - 1) as b:
                    step(b)
                step(B - 1, last=True)
                for n in range(COPY_O + 1):
                    behind(B, n)
                for k in range(x.STEPS):
                    x.scalar(act, B - 1, k)
                    router.scalar(act, B - 2, k)
                for k in range(router.STEPS):
                    router.scalar(act, B - 1, k)

            @block.vector
            def _(dve):
                chain = Chain(dve, dv, waited)
                nc.vector.memset(kP[:], 0.0).then_inc(zeroed, 1)
                nc.vector.memset(vpm[:], 0.0).then_inc(zeroed, 1)
                nc.vector.memset(x.wo[:], 0.0).then_inc(x.zeroed, 1)
                nc.vector.memset(x.v[:], 0.0).then_inc(x.zeroed, 1)
                dve.wait_ge(consts, ALL_CONSTS)

                def squares(b):
                    dve.wait_ge(x_in, 16 * b + 16)
                    own_wait(dve, waited)
                    for t in range(NT):
                        last = nc.vector.tensor_tensor_reduce(out=sq[:, t, :], in0=XIN[:, t, :], in1=XIN[:, t, :],
                                                              scale=1.0, scalar=0.0, op0=ALU.mult, op1=ALU.add,
                                                              accum_out=ss[:, t:t + 1])
                    chain.link(last)
                    nc.vector.tensor_scalar(ms[:], ss[:], 1.0 / D, RMS_EPS, ALU.mult, ALU.add).then_inc(ms_ok, 1)

                def rms_scaled(b):
                    dve.wait_ge(rr_ok, b + 1)
                    for t in range(NT):
                        last = nc.vector.tensor_scalar(XR[:, t, :], XIN[:, t, :], rr[:, t:t + 1], None, ALU.mult)
                    last.then_inc(xr, 1)

                def front(b, n):
                    if n >= 3 and chunk_at(n - 3) is not None:
                        c = chunk_at(n - 3)
                        at_least(dve, q_sb, CH * b + c - 1)
                        dve.wait_ge(rot_ps, CH * b + c + 1)
                        nc.vector.tensor_tensor(t2[c % 2][:].rearrange("p a s -> p (a s)"), RT[:],
                                                cs[:, 1, :, :].rearrange("p a s -> p (a s)"), ALU.mult).then_inc(t2_sb, 1)
                    if n >= 3 and chunk_at(n - 3) is not None:
                        c = chunk_at(n - 3)
                        dve.wait_ge(t2_sb, CH * b + c + 1)
                        dve.wait_ge(t1_sb, CH * b + c + 1)
                        if c % 4 == 0:
                            at_least(dve, sc_ps, U // 2 * (b - 1) + (c // 4 + 1) * 8)
                        for u in range(2):
                            r = slice(u * DH, (u + 1) * DH)
                            last = nc.vector.tensor_tensor(kP[r, c, u, :, PM:NK],
                                                           t1[c % 2][r, 1, :].rearrange("p (w s) -> p w s", w=NT),
                                                           t2[c % 2][r, 1, :].rearrange("p (w s) -> p w s", w=NT), ALU.add)
                        last.then_inc(k_sb, 1)

                def maxima(b, n):
                    if n % 2:
                        return
                    r = n // 2 % RING
                    dve.wait_ge(sc_ps, U // 2 * b + n // 2 + 1)
                    at_least(dve, pT_ps, U // 2 * b + n // 2 + 1 - RING)
                    own_wait(dve, waited)
                    for u in range(2):
                        last = nc.vector.tensor_tensor_reduce(
                            out=SM[:, r, u, :], in0=SC[n // 2 % 2][:, u * NK:(u + 1) * NK], in1=mask[:], scale=-scale,
                            scalar=3.0e38, op0=ALU.add, op1=ALU.min, accum_out=nb[:, r, u:u + 1])
                    last.then_inc(maxed, 1)

                def norm(b, n):
                    if n % 2:
                        return
                    r = n // 2 % RING
                    dve.wait_ge(exped, U // 2 * b + n // 2 + 1)
                    chain.link(nc.vector.reciprocal(rs[:, r, :], sm[:, r, :]))
                    if n % 8 == 0:
                        at_least(dve, pp_ps, U // 8 * b + n // 8 - 1)
                    nc.vector.tensor_tensor(
                        PP[:, (n // 8) % 2, (n % 8) * PM:(n % 8 + 2) * PM].rearrange("p (h k) -> p h k", h=2),
                        SM[:, r, :, 0:PM], broadcast_last(rs[:, r, :], PM), ALU.mult)
                    nc.vector.tensor_tensor(SM[:, r, :, PM:NK], SM[:, r, :, PM:NK], broadcast_last(rs[:, r, :], P),
                                            ALU.mult).then_inc(normed, 1)

                def residual(b, n):
                    if n != U - 2:
                        return
                    dve.wait_ge(y_ps, b + 1)
                    dve.wait_ge(xb, b + 1)
                    nc.vector.tensor_tensor(R[:].rearrange("p t n -> p (t n)"), PO[:],
                                            XB[:].rearrange("p t n -> p (t n)"), ALU.add).then_inc(r_sb, 1)
                    dve.wait_ge(r_sb, b + 1)
                    layernorm_stats(nc, chain, R, st, mv, ve, var, LN_EPS)

                def result(b, n):
                    if n != U - 2:
                        return
                    dve.wait_ge(rstd_ok, b + 1)
                    at_least(dve, x.x1T_ps, b)
                    at_least(dve, x.x1b, b)
                    layernorm_apply(nc, R, mv, rstd, X1).then_inc(x1_ok, 1)

                def behind(b, n):
                    lagged(b, n, U, NORM, norm)
                    lagged(b, n, U, RESIDUAL, residual)
                    lagged(b, n, U, RESULT, result)

                def step(b, first=False, last=False):
                    for n in range(U):
                        maxima(b, n)
                        behind(b, n)
                        if n < 16:
                            front(b, n)
                        if n == 11 and not last:
                            squares(b + 1)
                        if n == 12 and not last:
                            rms_scaled(b + 1)
                        if n >= 16 and not last:
                            front(b + 1, n)
                        if not first:
                            for k in CROSS.get(n, ()):
                                x.vector(dve, b - 1, k, chain)
                                if exists(b - 2):
                                    router.vector(dve, b - 2, k, chain)

                squares(0)
                rms_scaled(0)
                for n in range(16, U):
                    front(0, n)
                router.prepare(dve)
                step(0, first=True)
                step(1)
                step(2)
                start = chain.n
                with dve.Fori(3, B - 1) as b:
                    chain.start(start + LINKS * (b - 3))
                    step(b)
                    assert chain.n == LINKS, (chain.n, LINKS)
                chain.start(start + LINKS * (B - 4))
                step(B - 1, last=True)
                for n in range(RESULT + 1):
                    behind(B, n)
                for k in range(x.STEPS):
                    x.vector(dve, B - 1, k, chain)
                    router.vector(dve, B - 2, k, chain)
                for k in range(router.STEPS):
                    router.vector(dve, B - 1, k, chain)

            @block.gpsimd
            def _(pool):
                nc.gpsimd.memset(neghalf[:], -0.5).then_inc(hv, 1)
                pool.wait_ge(hv, 1)
                pool.wait_ge(consts, ALL_CONSTS)

                def rms(b):
                    pool.wait_ge(ms_ok, b + 1)
                    nc.gpsimd.tensor_tensor(rr[:], ms[:], neghalf[:], ALU.pow).then_inc(rr_ok, 1)

                def add_bias(b):
                    at_least(pool, r_sb, b)
                    nc.gpsimd.tensor_tensor(XB[:], XIN[:], broadcast_mid(row[:, 0, :], NT), ALU.add).then_inc(xb, 1)

                def front(b, n):
                    if n >= 1 and chunk_at(n - 1) is not None:
                        c = chunk_at(n - 1)
                        pool.wait_ge(raw_sb, CH * b + c + 1)
                        at_least(pool, k_sb, CH * b + c - 1)
                        nc.gpsimd.tensor_tensor(t1[c % 2][:], raw[c % 2][:], cs[:, 0, :, :], ALU.mult).then_inc(t1_sb, 1)
                    if n >= 3 and chunk_at(n - 3) is not None:
                        c = chunk_at(n - 3)
                        pool.wait_ge(t1_sb, CH * b + c + 1)
                        pool.wait_ge(t2_sb, CH * b + c + 1)
                        if c % 4 == 0:
                            at_least(pool, sc_ps, U // 2 * (b - 1) + (c // 4 + 1) * 8)
                        nc.gpsimd.tensor_tensor(qT[:, c, :], t1[c % 2][:, 0, :], t2[c % 2][:, 0, :],
                                                ALU.add).then_inc(q_sb, 1)

                def deviation(b, n):
                    if n != U - 2:
                        return
                    pool.wait_ge(var, b + 1)
                    nc.gpsimd.tensor_tensor(rstd[:], ve[:], neghalf[:], ALU.pow).then_inc(rstd_ok, 1)

                def step(b, first=False, last=False):
                    for n in range(U):
                        lagged(b, n, U, RESIDUAL, deviation)
                        if n < 16:
                            front(b, n)
                        if n == RESULT:
                            add_bias(b)
                        if n == 11 and not last:
                            rms(b + 1)
                        if n >= 16 and not last:
                            front(b + 1, n)
                        if not first:
                            for k in CROSS.get(n, ()):
                                x.pool(pool, b - 1, k)
                                if exists(b - 2):
                                    router.pool(pool, b - 2, k)

                rms(0)
                for n in range(16, U):
                    front(0, n)
                step(0, first=True)
                step(1)
                step(2)
                with pool.Fori(3, B - 1) as b:
                    step(b)
                step(B - 1, last=True)
                lagged(B, RESIDUAL - 2, U, RESIDUAL, deviation)
                for k in range(x.STEPS):
                    x.pool(pool, B - 1, k)
                    router.pool(pool, B - 2, k)
                for k in range(router.STEPS):
                    router.pool(pool, B - 1, k)
                pool.wait_ge(router.scattered, 16 * NT * 2 * B)
        al.end()


def decoder(nc, d):
    x2 = nc.dram_tensor("after_L0_xattn", (B, S, D), F32, kind="Internal").ap()
    x3 = nc.dram_tensor("after_L0_ffn", (B, S, D), F32, kind="Internal").ap()
    x5 = nc.dram_tensor("after_L1_xattn", (B, S, D), F32, kind="Internal").ap()
    flat = lambda ap: ap.rearrange("b s n -> (b s) n")
    cross = lambda layer: {n: d[f"{layer}_xattn_{n}"] for n in ("Wq", "Wk", "Wv", "Wo")}
    routing = {layer: {"sorted": nc.dram_tensor(f"{layer}_sorted", (E8 * ROOM, D), F32, kind="Internal").ap(),
                       "record": nc.dram_tensor(f"{layer}_record", (T // P, P, FIELDS), F32, kind="Internal").ap(),
                       **{n: d[f"{layer}_ffn_{n}"] for n in ("Wr", "br")}, "before": d["before"], "iota": d["iota"],
                       "gb": d["L1_gb"]} for layer in ("L0", "L1")}
    experts = lambda layer: {**routing[layer], "ident": d["ident"],
                             **{n: d[f"{layer}_ffn_{n}"] for n in ("W1", "b1", "W2", "b2")}}
    relative_attention_phase(nc, {**d, "x2": x2, "L0_xattn": cross("L0"), "L0_router": routing["L0"]})
    experts_phase(nc, {**experts("L0"), "x": flat(x2), "out": flat(x3)}, "b_", 1, 512, ACT.Relu, False)
    segment_attention_phase(nc, {**d, "x": x3, "x5": x5, "L1_xattn": cross("L1"), "L1_router": routing["L1"]})
    experts_phase(nc, {**experts("L1"), "x": flat(x5), "out": flat(d["out"])}, "e_", 2, 1024, ACT.Gelu, True)


def constants():
    f = np.float32
    c = {"ident": np.eye(P, dtype=f),
         "before": (np.arange(P)[:, None] < np.arange(P)).astype(f),
         "headmask": (np.arange(P)[:, None] // HD == np.arange(HC)).astype(f),
         "iota": np.tile(np.concatenate([np.arange(E8), P * np.arange(most_tiles(2))]).astype(f), (P, 1))}
    buckets, furthest = 64, 128
    mid = buckets // 2
    r = np.arange(1 - S, S)
    far = np.maximum(np.abs(r), mid - 1).astype(f)
    log = np.ceil(np.log(far / f(mid)) / f(np.log((furthest - 1) / mid)) * f(mid - 1)) + mid
    bucket = np.clip(np.where(far <= mid, r, log * np.sign(r)).astype(int) + buckets, 0, 2 * buckets - 1)
    onehot = (np.arange(P)[:, None] == bucket).astype(f)
    c["onehot"] = np.concatenate([onehot[:, ::-1], onehot], 1)
    inv = (f(1) / f(10000.0) ** (np.arange(0, DH, 2, dtype=f) / f(DH))).astype(f)
    angle = np.arange(S, dtype=f)[:, None] * inv
    both = [np.tile(np.repeat(g(angle), 2, -1).T, (P // DH, 1)) for g in (np.cos, np.sin)]
    c["cossin"] = np.stack([np.stack([g, g], 1) for g in both], 1).astype(f)
    rot = np.zeros((P, P), f)
    even = np.arange(0, P, 2)
    rot[even + 1, even], rot[even, even + 1] = -1, 1
    c["rot"] = rot
    c["mask"] = np.zeros((P, PM + P), f)
    c["mask"][:, PM:] = np.where(np.arange(P) <= np.arange(P)[:, None], 0, -3e38)
    return c


def laid_out(v):
    col = lambda n: v[n].reshape(KC, P).T
    out = dict(constants())
    for n in ("L0_attn_Wq", "L0_attn_Wk", "L0_attn_Wv", "L0_attn_Wo", "L0_attn_Wpk", "L0_attn_Wpq", "L0_attn_rel_emb"):
        out[n.replace("attn_", "")] = v[n]
    for layer in ("L0", "L1"):
        for n in ("Wq", "Wk", "Wv", "Wo"):
            out[f"{layer}_xattn_{n}"] = v[f"{layer}_xattn_{n}"]
        out[f"{layer}_ffn_b1"] = v[f"{layer}_ffn_b1"].reshape(E8, -1, P).transpose(0, 2, 1)
        out[f"{layer}_ffn_b2"] = v[f"{layer}_ffn_b2"]
    out["L0_ffn_Wr"], out["L1_ffn_Wr"] = v["L0_ffn_Wr"], v["L1_ffn_Wg"].T
    out["L0_ffn_br"], out["L1_ffn_br"] = v["L0_ffn_br"], v["L1_ffn_bg"]
    for n in ("W1", "W2"):
        out[f"L0_ffn_{n}"] = v[f"L0_ffn_{n}"]
        out[f"L1_ffn_{n}"] = v[f"L1_ffn_{n}"].transpose(0, 2, 1)
    out["L0_col"] = np.concatenate([col("L0_attn_bq"), col("L0_attn_bk"), col("L0_xattn_bq"), col("L0_xattn_bk")], 1)
    out["L0_row"] = np.stack([v["L0_attn_bv"], v["L0_attn_bv"], v["L0_attn_bo"], v["L0_xattn_bv"], v["L0_xattn_bo"]])
    out["L0_prow"] = np.stack([v["L0_attn_ln_g"], v["L0_attn_ln_b"], v["L0_attn_bpk"], v["L0_attn_bpq"]])
    out["L1_col"] = np.concatenate([col("L1_attn_norm_w"), col("L1_xattn_bq"), col("L1_xattn_bk")], 1)
    out["L1_row"] = np.stack([v["L1_attn_b_out"], v["L1_xattn_bv"], v["L1_xattn_bo"]])
    out["L1_gb"] = np.stack([v["L1_ffn_gamma"], v["L1_ffn_beta"]])
    out["w_qkv"], out["w_out"] = v["L1_attn_w_qkv"], v["L1_attn_w_out"]
    out["pm_kT"] = v["L1_attn_pm_k"].transpose(0, 2, 1).reshape(INNER, PM)
    out["pm_v"] = v["L1_attn_pm_v"]
    out["ctxT"] = v["ctx_768"].transpose(0, 2, 1)
    out["x"] = v["x"]
    return out


def kernel(**inputs):
    from concourse import bacc
    from concourse.bass_utils import run_bass_kernel_spmd

    nc = bacc.Bacc("TRN2", target_bir_lowering=False, num_devices=1)
    arrays, d = {}, {}
    for name, a in laid_out({n: np.asarray(a) for n, a in inputs.items()}).items():
        a = np.ascontiguousarray(a)
        arrays[f"in_{name}"] = a
        d[name] = nc.dram_tensor(f"in_{name}", a.shape, mybir.dt.from_np(a.dtype), kind="ExternalInput").ap()
    d["out"] = nc.dram_tensor("out", (B, S, D), F32, kind="ExternalOutput").ap()
    decoder(nc, d)
    return run_bass_kernel_spmd(nc, [arrays], core_ids=[0]).results[0]["out"]
```
